# Optimizing a Trainium2 kernel written in Bass

```python
import numpy as np
import jax
import jax.numpy as jnp

def _softmax(x, axis=-1):
    return jax.nn.softmax(x, axis=axis)

def _gelu(x):
    return jax.nn.gelu(x, approximate=True)

def _silu(x):
    return jax.nn.silu(x)

def _sigmoid(x):
    return jax.nn.sigmoid(x)

def _layernorm(x, axis=-1, eps=1e-05):
    m = jnp.mean(x, axis=axis, keepdims=True)
    v = jnp.var(x, axis=axis, keepdims=True)
    return (x - m) / jnp.sqrt(v + eps)

def _scatter_add(tgt, idx, src, axis=0):
    return tgt.at[idx].add(src)

def _segment_sum(src, seg, n):
    return jax.ops.segment_sum(src, seg, n)
kernel_name = 'mk_flamingo_gated_d1_seqx_r4_2fd0ee'

def setup_inputs(seed: int=0):
    np.random.seed(seed)
    _w = jnp.asarray

    def _rec_inputs():
        import jax
        import jax.numpy as jnp
        _rk = jax.random.key(seed)
        x = -0.0003929 + 0.9999 * jax.random.normal(jax.random.fold_in(_rk, 1), (4, 1024, 256), jnp.float32)
        _lenS = 1024 - jax.random.randint(jax.random.fold_in(_rk, 7), (4,), 0, max(1, 1024 // 4) + 1, jnp.int32)
        _lenS2 = 77 - jax.random.randint(jax.random.fold_in(_rk, 8), (4,), 0, max(1, 77 // 4) + 1, jnp.int32)
        _ctx_768P = jax.random.normal(jax.random.fold_in(_rk, 11), (4, 16, 192), jnp.float32)
        _ctx_768c = jax.random.dirichlet(jax.random.fold_in(_rk, 511), 0.3 * jnp.ones((16,), jnp.float32), (4, 77))
        _ctx_768t = jnp.einsum('bsk,bkd->bsd', _ctx_768c, _ctx_768P)
        _ctx_768t = _ctx_768t * jax.lax.rsqrt(jnp.mean(jnp.square(_ctx_768t)) + 1e-12) * 0.953939
        ctx_768 = -0.00055796 + 0.999787 * (_ctx_768t + 0.3 * jax.random.normal(jax.random.fold_in(_rk, 611), (4, 77, 192), jnp.float32))
        _g = jax.random.normal(jax.random.fold_in(_rk, 9001), (2, 1), jnp.float32)
        _g = jnp.sign(_g) * jnp.maximum(jnp.abs(_g), 1.0) + (_g == 0) * 1.0
        g_xattn = _g[0]
        g_ffn = _g[1]
        return (x, ctx_768, g_xattn, g_ffn)
    x, ctx_768, g_xattn, g_ffn = _rec_inputs()

    def _L0_xattn_setup():
        import jax, jax.numpy as jnp
        import numpy as np
        HEADS = 16
        DIM_HEAD = 64
        SCALE = DIM_HEAD ** (-0.5)
        key = jax.random.key(seed)
        ks = jax.random.split(key, 6)
        B, N, C = (4, 1024, 256)
        M, Cc = (128, 192)
        inner = HEADS * DIM_HEAD
        s = lambda d: d ** (-0.5)
        return {'x': jax.random.normal(ks[0], (B, N, C), jnp.float32), 'context': jax.random.normal(ks[1], (B, M, Cc), jnp.float32), 'Wq': jax.random.normal(ks[2], (C, inner), jnp.float32) * s(C), 'Wk': jax.random.normal(ks[3], (Cc, inner), jnp.float32) * s(Cc), 'Wv': jax.random.normal(ks[4], (Cc, inner), jnp.float32) * s(Cc), 'Wo': jax.random.normal(ks[5], (inner, C), jnp.float32) * s(inner), 'bo': jnp.zeros((C,), jnp.float32)}
    _L0_xattn_all = _L0_xattn_setup()
    _L0_xattn_in = {k: v for k, v in _L0_xattn_all.items() if k in ('Wq', 'Wk', 'Wv', 'Wo', 'bo')}
    del _L0_xattn_all

    def _L0_ffn_setup():
        import jax, jax.numpy as jnp
        import numpy as np
        DIM = 256
        H = 8
        DH = 64
        W = 64
        NQ = 128
        NKV = 256
        EPS = 1.0
        NITERS = 50
        FETCH = 9.0 / 8.0
        SCALE = DH ** (-0.5)

        def _ln(x, w, b):
            m = x.mean(-1, keepdims=True)
            v = ((x - m) ** 2).mean(-1, keepdims=True)
            return (x - m) * jax.lax.rsqrt(v + 1e-05) * w + b

        def _rms(x, g):
            n = jnp.maximum(jnp.linalg.norm(x, axis=-1, keepdims=True), 1e-12)
            return x / n * np.sqrt(DIM).astype(np.float32) * g

        def local_attn(x, Wqkv, Wout):
            b, n, _ = x.shape
            nw = n // W
            qkv = x @ Wqkv.T
            q, k, v = jnp.split(qkv, 3, axis=-1)

            def towin(t):
                return t.reshape(b, nw, W, H, DH).transpose(0, 3, 1, 2, 4)
            q, k, v = map(towin, (q, k, v))

            def expand(t):
                tp = jnp.pad(t, ((0, 0), (0, 0), (1, 1), (0, 0), (0, 0)))
                return jnp.concatenate([tp[:, :, :-2], tp[:, :, 1:-1], tp[:, :, 2:]], axis=3)
            ke, ve = (expand(k), expand(v))
            sim = jnp.einsum('bhnid,bhnjd->bhnij', q, ke) * SCALE
            win = jnp.arange(nw)
            valid = jnp.concatenate([jnp.repeat((win > 0)[:, None], W, 1), jnp.ones((nw, W), bool), jnp.repeat((win < nw - 1)[:, None], W, 1)], axis=1)
            sim = jnp.where(valid[None, None, :, None, :], sim, -1000000000.0)
            attn = jax.nn.softmax(sim, axis=-1)
            o = jnp.einsum('bhnij,bhnjd->bhnid', attn, ve)
            o = o.transpose(0, 2, 3, 1, 4).reshape(b, n, H * DH)
            return o @ Wout.T

        def route(x, routing_token, num_tokens):
            s = jnp.einsum('bnd,rd->brn', x, routing_token).reshape(x.shape[0], x.shape[1])
            n = s.shape[-1]
            logk = jnp.log(jnp.asarray(min(num_tokens * FETCH, float(n)), s.dtype))

            def body(ab, _):
                a, bb = ab
                a = EPS * (logk - jax.nn.logsumexp((s + bb) / EPS, axis=-1, keepdims=True))
                bb = -jax.nn.relu(s + a)
                return ((a, bb), None)
            (a, bb), _ = jax.lax.scan(body, (jnp.zeros((s.shape[0], 1), s.dtype), -s), None, length=NITERS)
            scores = jnp.exp((s + a + bb) / EPS)
            sel_scores, sel_idx = jax.lax.top_k(scores, num_tokens)
            sel_scores = sel_scores + jax.lax.stop_gradient(1.0 - sel_scores)
            return (sel_scores, sel_idx)

        def heavy_attn(xq, ctx, scores_kv, gamma, Wq, Wkv, Wout, null_kv):
            b = xq.shape[0]
            xq = _rms(xq, gamma)
            ctx = _rms(ctx, gamma)
            q = (xq @ Wq.T).reshape(b, -1, H, DH).transpose(0, 2, 1, 3)
            kv = (ctx @ Wkv.T).reshape(b, -1, H, 2 * DH).transpose(0, 2, 1, 3)
            k, v = (kv[..., :DH], kv[..., DH:])
            v = v * scores_kv[:, None, :, None]
            nk = jnp.broadcast_to(null_kv[0][None, :, None, :], (b, H, 1, DH))
            nv = jnp.broadcast_to(null_kv[1][None, :, None, :], (b, H, 1, DH))
            k = jnp.concatenate([nk, k], axis=2)
            v = jnp.concatenate([nv, v], axis=2)
            sim = jnp.einsum('bhid,bhjd->bhij', q, k) * SCALE
            attn = jax.nn.softmax(sim, axis=-1)
            o = jnp.einsum('bhij,bhjd->bhid', attn, v)
            o = o.transpose(0, 2, 1, 3).reshape(b, -1, H * DH)
            return o @ Wout.T
        key = jax.random.key(seed)
        ks = jax.random.split(key, 12)
        D, IN = (DIM, H * DH)
        w = lambda k, shape: jax.random.normal(k, shape, jnp.float32) * 0.02
        return {'x': jax.random.normal(ks[0], (4, 1024, D), jnp.float32), 'ln_w': jnp.ones((D,), jnp.float32), 'ln_b': jnp.zeros((D,), jnp.float32), 'Wqkv': w(ks[1], (3 * IN, D)), 'Wout_l': w(ks[2], (D, IN)), 'rt_q': jax.random.normal(ks[3], (1, D), jnp.float32), 'rt_kv': jax.random.normal(ks[4], (1, D), jnp.float32), 'gamma': jnp.ones((D,), jnp.float32), 'Wq': w(ks[5], (IN, D)), 'Wkv': w(ks[6], (2 * IN, D)), 'Wout_h': w(ks[7], (D, IN)), 'null_kv': jax.random.normal(ks[8], (2, H, DH), jnp.float32), 'null_q': jax.random.normal(ks[9], (D,), jnp.float32)}
    _L0_ffn_all = _L0_ffn_setup()
    _L0_ffn_in = {k: v for k, v in _L0_ffn_all.items() if k in ('ln_w', 'ln_b', 'Wqkv', 'Wout_l', 'rt_q', 'rt_kv', 'gamma', 'Wq', 'Wkv', 'Wout_h', 'null_kv', 'null_q')}
    del _L0_ffn_all
    return {'x': x, 'ctx_768': ctx_768, 'g_xattn': g_xattn, 'g_ffn': g_ffn, 'L0_xattn_Wq': _L0_xattn_in['Wq'], 'L0_xattn_Wk': _L0_xattn_in['Wk'], 'L0_xattn_Wv': _L0_xattn_in['Wv'], 'L0_xattn_Wo': _L0_xattn_in['Wo'], 'L0_xattn_bo': _L0_xattn_in['bo'], 'L0_ffn_ln_w': _L0_ffn_in['ln_w'], 'L0_ffn_ln_b': _L0_ffn_in['ln_b'], 'L0_ffn_Wqkv': _L0_ffn_in['Wqkv'], 'L0_ffn_Wout_l': _L0_ffn_in['Wout_l'], 'L0_ffn_rt_q': _L0_ffn_in['rt_q'], 'L0_ffn_rt_kv': _L0_ffn_in['rt_kv'], 'L0_ffn_gamma': _L0_ffn_in['gamma'], 'L0_ffn_Wq': _L0_ffn_in['Wq'], 'L0_ffn_Wkv': _L0_ffn_in['Wkv'], 'L0_ffn_Wout_h': _L0_ffn_in['Wout_h'], 'L0_ffn_null_kv': _L0_ffn_in['null_kv'], 'L0_ffn_null_q': _L0_ffn_in['null_q']}

def reference(x, ctx_768, g_xattn, g_ffn, L0_xattn_Wq, L0_xattn_Wk, L0_xattn_Wv, L0_xattn_Wo, L0_xattn_bo, L0_ffn_ln_w, L0_ffn_ln_b, L0_ffn_Wqkv, L0_ffn_Wout_l, L0_ffn_rt_q, L0_ffn_rt_kv, L0_ffn_gamma, L0_ffn_Wq, L0_ffn_Wkv, L0_ffn_Wout_h, L0_ffn_null_kv, L0_ffn_null_q):
    import jax
    import jax.numpy as jnp

    def _L0_xattn_ref(x, context, Wq, Wk, Wv, Wo, bo):
        import jax, jax.numpy as jnp
        import numpy as np
        HEADS = 16
        DIM_HEAD = 64
        SCALE = DIM_HEAD ** (-0.5)
        B, N, _ = x.shape
        M = context.shape[1]
        q = (x @ Wq).reshape(B, N, HEADS, DIM_HEAD).transpose(0, 2, 1, 3)
        k = (context @ Wk).reshape(B, M, HEADS, DIM_HEAD).transpose(0, 2, 1, 3)
        v = (context @ Wv).reshape(B, M, HEADS, DIM_HEAD).transpose(0, 2, 1, 3)
        dots = jnp.einsum('bhnd,bhmd->bhnm', q, k) * SCALE
        attn = jax.nn.softmax(dots, axis=-1)
        out = jnp.einsum('bhnm,bhmd->bhnd', attn, v)
        out = out.transpose(0, 2, 1, 3).reshape(B, N, HEADS * DIM_HEAD)
        return out @ Wo + bo

    def _L0_ffn_ref(x, ln_w, ln_b, Wqkv, Wout_l, rt_q, rt_kv, gamma, Wq, Wkv, Wout_h, null_kv, null_q):
        import jax, jax.numpy as jnp
        import numpy as np
        DIM = 256
        H = 8
        DH = 64
        W = 64
        NQ = 128
        NKV = 256
        EPS = 1.0
        NITERS = 50
        FETCH = 9.0 / 8.0
        SCALE = DH ** (-0.5)

        def _ln(x, w, b):
            m = x.mean(-1, keepdims=True)
            v = ((x - m) ** 2).mean(-1, keepdims=True)
            return (x - m) * jax.lax.rsqrt(v + 1e-05) * w + b

        def _rms(x, g):
            n = jnp.maximum(jnp.linalg.norm(x, axis=-1, keepdims=True), 1e-12)
            return x / n * np.sqrt(DIM).astype(np.float32) * g

        def local_attn(x, Wqkv, Wout):
            b, n, _ = x.shape
            nw = n // W
            qkv = x @ Wqkv.T
            q, k, v = jnp.split(qkv, 3, axis=-1)

            def towin(t):
                return t.reshape(b, nw, W, H, DH).transpose(0, 3, 1, 2, 4)
            q, k, v = map(towin, (q, k, v))

            def expand(t):
                tp = jnp.pad(t, ((0, 0), (0, 0), (1, 1), (0, 0), (0, 0)))
                return jnp.concatenate([tp[:, :, :-2], tp[:, :, 1:-1], tp[:, :, 2:]], axis=3)
            ke, ve = (expand(k), expand(v))
            sim = jnp.einsum('bhnid,bhnjd->bhnij', q, ke) * SCALE
            win = jnp.arange(nw)
            valid = jnp.concatenate([jnp.repeat((win > 0)[:, None], W, 1), jnp.ones((nw, W), bool), jnp.repeat((win < nw - 1)[:, None], W, 1)], axis=1)
            sim = jnp.where(valid[None, None, :, None, :], sim, -1000000000.0)
            attn = jax.nn.softmax(sim, axis=-1)
            o = jnp.einsum('bhnij,bhnjd->bhnid', attn, ve)
            o = o.transpose(0, 2, 3, 1, 4).reshape(b, n, H * DH)
            return o @ Wout.T

        def route(x, routing_token, num_tokens):
            s = jnp.einsum('bnd,rd->brn', x, routing_token).reshape(x.shape[0], x.shape[1])
            n = s.shape[-1]
            logk = jnp.log(jnp.asarray(min(num_tokens * FETCH, float(n)), s.dtype))

            def body(ab, _):
                a, bb = ab
                a = EPS * (logk - jax.nn.logsumexp((s + bb) / EPS, axis=-1, keepdims=True))
                bb = -jax.nn.relu(s + a)
                return ((a, bb), None)
            (a, bb), _ = jax.lax.scan(body, (jnp.zeros((s.shape[0], 1), s.dtype), -s), None, length=NITERS)
            scores = jnp.exp((s + a + bb) / EPS)
            sel_scores, sel_idx = jax.lax.top_k(scores, num_tokens)
            sel_scores = sel_scores + jax.lax.stop_gradient(1.0 - sel_scores)
            return (sel_scores, sel_idx)

        def heavy_attn(xq, ctx, scores_kv, gamma, Wq, Wkv, Wout, null_kv):
            b = xq.shape[0]
            xq = _rms(xq, gamma)
            ctx = _rms(ctx, gamma)
            q = (xq @ Wq.T).reshape(b, -1, H, DH).transpose(0, 2, 1, 3)
            kv = (ctx @ Wkv.T).reshape(b, -1, H, 2 * DH).transpose(0, 2, 1, 3)
            k, v = (kv[..., :DH], kv[..., DH:])
            v = v * scores_kv[:, None, :, None]
            nk = jnp.broadcast_to(null_kv[0][None, :, None, :], (b, H, 1, DH))
            nv = jnp.broadcast_to(null_kv[1][None, :, None, :], (b, H, 1, DH))
            k = jnp.concatenate([nk, k], axis=2)
            v = jnp.concatenate([nv, v], axis=2)
            sim = jnp.einsum('bhid,bhjd->bhij', q, k) * SCALE
            attn = jax.nn.softmax(sim, axis=-1)
            o = jnp.einsum('bhij,bhjd->bhid', attn, v)
            o = o.transpose(0, 2, 1, 3).reshape(b, -1, H * DH)
            return o @ Wout.T
        b, n, d = x.shape
        light = local_attn(_ln(x, ln_w, ln_b), Wqkv, Wout_l)
        sq, iq = route(x, rt_q, NQ)
        skv, ikv = route(x, rt_kv, NKV)
        br = jnp.arange(b)[:, None]
        xq = x[br, iq]
        xkv = x[br, ikv]
        heavy = heavy_attn(xq, xkv, skv, gamma, Wq, Wkv, Wout_h, null_kv)
        heavy = heavy * sq[..., None]
        out = jnp.broadcast_to(null_q[None, None, :], (b, n, d))
        out = out.at[br, iq].set(heavy)
        return out + light
    x = x + jnp.tanh(g_xattn[0]) * _L0_xattn_ref(_layernorm(x, axis=-1), ctx_768, L0_xattn_Wq, L0_xattn_Wk, L0_xattn_Wv, L0_xattn_Wo, L0_xattn_bo)
    x = x + jnp.tanh(g_ffn[0]) * _L0_ffn_ref(_layernorm(x, axis=-1), L0_ffn_ln_w, L0_ffn_ln_b, L0_ffn_Wqkv, L0_ffn_Wout_l, L0_ffn_rt_q, L0_ffn_rt_kv, L0_ffn_gamma, L0_ffn_Wq, L0_ffn_Wkv, L0_ffn_Wout_h, L0_ffn_null_kv, L0_ffn_null_q)
    return x

_drawn_inputs = setup_inputs


def setup_inputs(seed=0):
    import zlib

    import numpy as np

    out = dict(_drawn_inputs(seed))
    spreads = {'L0_xattn_bo': (0.0, 0.1),
     'L0_ffn_ln_w': (1.0, 0.6),
     'L0_ffn_ln_b': (0.0, 0.8),
     'L0_ffn_gamma': (1.0, 0.6)}
    factors = {'L0_ffn_rt_kv': 8.0,
     'L0_ffn_Wq': 8.0,
     'L0_ffn_Wkv': 4.207,
     'L0_ffn_Wout_h': 4.266,
     'L0_ffn_null_kv': 8.0}
    for name, (base, spread) in spreads.items():
        noise = np.random.default_rng([zlib.crc32(name.encode()), seed]).standard_normal(out[name].shape)
        drawn = base * np.exp(spread * noise) if base else spread * noise
        out[name] = jnp.asarray(drawn.astype(out[name].dtype))
    for name, factor in factors.items():
        out[name] = (out[name] * factor).astype(out[name].dtype)
    return out
```

```python
from contextlib import ExitStack
from math import log

import concourse.bass as bass
from concourse import mybir

F32 = mybir.dt.float32
F32R = mybir.dt.float32r
F16 = mybir.dt.float16
I32 = mybir.dt.int32
U32 = mybir.dt.uint32
ACT = mybir.ActivationFunctionType
ALU = mybir.AluOpType
AX_X = mybir.AxisListType.X

P = 128
B, N, C = 4, 1024, 256
CC = C // P
TB = N // P
NT = B * TB
EPS = 1e-5

XH, XD, M, XC = 16, 64, 77, 192
XI = XH * XD
XP = XH // 2
XKC = XC // 2
S1 = XH * M
KT = -(-S1 // P)
S1P = KT * P
PW = 2 * M
VW = P - 1 + PW + P - 1
SCOLS = [(0, 6 * M), (6 * M, 12 * M), (12 * M, 16 * M)]
GPAIRS = [(0, 3), (3, 6), (6, 8)]
GN = CC * len(GPAIRS)
UN = KT // 2
GU = GN + UN

H, DH, W = 8, 64, 64
HP = H // 2
IN = H * DH
SCALE = DH ** -0.5
NQ, NKV = 128, 256
FETCH = 9.0 / 8.0
UPD = 7
BLOCKS = 7
CAP = 80.0
NEG = -1e9
SMALLEST = 87.33655


def flat(ap):
    return ap.rearrange("p a b -> p (a b)")


def cols(ap, m):
    return ap.rearrange("p (h o) -> p h o", o=1).to_broadcast([ap.shape[0], ap.shape[1], m])


class Space:

    def __init__(self, nc, stack, phase):
        self.nc, self.stack, self.phase = nc, stack, phase

    def sb(self, name, shape, dt=F32):
        return self.stack.enter_context(self.nc.sbuf_tensor(f"{self.phase}_{name}", shape, dt))

    def sem(self, name):
        return self.stack.enter_context(self.nc.semaphore(f"{self.phase}_{name}"))


def cross_attention(nc, k, ps, d):
    XR, MV, RS, ident, tg, sraw = k["XR"], k["MV"], k["RS"], k["ident"], k["tg"], k["sraw"]
    with ExitStack() as stack:
        s = Space(nc, stack, "cross")
        KBD = s.sb("KBD", [P, B, XP, PW])
        vT = s.sb("vT", [P, XP, B, M])
        VBD = s.sb("VBD", [P, XP, VW])
        WqT = s.sb("WqT", [P, XP, C])
        Wo = s.sb("Wo", [P, XP, C])
        Ghi, Glo = s.sb("Ghi", [P, CC, S1], F32R), s.sb("Glo", [P, CC, S1], F32R)
        Uhi, Ulo = s.sb("Uhi", [P, KT, C], F32R), s.sb("Ulo", [P, KT, C], F32R)
        probs = s.sb("probs", [P, 4, S1P])
        pThi, pTlo = s.sb("pThi", [P, S1P], F32R), s.sb("pTlo", [P, S1P], F32R)
        h = s.sb("h", [P, 2, C])
        hThi, hTlo = s.sb("hThi", [P, 2, C], F32R), s.sb("hTlo", [P, 2, C], F32R)
        mx, sm, rc = s.sb("mx", [P, 2, XH]), s.sb("sm", [P, 2, XH]), s.sb("rc", [P, 2, XH])
        Wkv = s.sb("Wkv", [XKC, 2, 2, XI])
        ctx = s.sb("ctx", [XKC, 2, B * M])
        RT = s.sb("RT", [P, 2, C])
        junk = s.sb("junk", [P, 2, 2, C])
        bo = s.sb("bo", [P, C])
        bst = s.sb("bst", [P, 2, 6])
        x1b, mvb = s.sb("x1b", [P, 2, C]), s.sb("mvb", [P, TB, 2])
        sb8 = s.sb("sb8", [P, 2, TB])
        LA, LB, LC = s.sb("LA", [P, NT]), s.sb("LB", [P, NT]), s.sb("LC", [P, NT])
        banks_s, banks_p, bank_h, bank_o = ps[0:3], ps[3:6], ps[6], ps[7]

        w_loaded, x_loaded, c_loaded, x1_stored = (s.sem(n) for n in (
            "w_loaded", "x_loaded", "c_loaded", "x1_stored"))
        pool_once, vec_once, act_once = s.sem("pool_once"), s.sem("vec_once"), s.sem("act_once")
        kv_mult, kv_evac = s.sem("kv_mult"), s.sem("kv_evac")
        gu_mult, gu_hi, gu_lo, vbd_made = s.sem("gu_mult"), s.sem("gu_hi"), s.sem("gu_lo"), s.sem("vbd_made")
        h_made, h_turned, hhi_made, hlo_made = s.sem("h_made"), s.sem("h_turned"), s.sem("hhi_made"), s.sem("hlo_made")
        scored, max_made, shifted, exp_made = s.sem("scored"), s.sem("max_made"), s.sem("shifted"), s.sem("exp_made")
        sum_made, recip_made, probs_made = s.sem("sum_made"), s.sem("recip_made"), s.sem("probs_made")
        p_turned, phi_made, plo_made = s.sem("p_turned"), s.sem("phi_made"), s.sem("plo_made")
        pv_done, bias_added, x1_made = s.sem("pv_done"), s.sem("bias_added"), s.sem("x1_made")
        stats_made, mv_made, routed = s.sem("stats_made"), s.sem("mv_made"), s.sem("routed")
        x1_kept, mv_kept, spaced = s.sem("x1_kept"), s.sem("mv_kept"), s.sem("spaced")

        def gu_group(n):
            bank = ps[n % 4]
            if n < GN:
                c, (p0, p1) = n // len(GPAIRS), GPAIRS[n % len(GPAIRS)]
                at = slice(PW * p0, PW * p1)
                return bank[:, 0:PW * (p1 - p0)], Ghi[:, c, at], Glo[:, c, at]
            t = 2 * (n - GN)
            return bank[:, 0:2 * C], flat(Uhi[:, t:t + 2]), flat(Ulo[:, t:t + 2])

        block = stack.enter_context(nc.Block())

        @block.sync
        def _(sp):
            sp.dma_start(ctx[:], d["ctxT"].rearrange("(k p) n -> p k n", p=XKC)).then_inc(w_loaded, 16)
            sp.dma_start(Wkv[:, 0], d["xWk"].rearrange("(k p) n -> p k n", p=XKC)).then_inc(w_loaded, 16)
            sp.dma_start(Wkv[:, 1], d["xWv"].rearrange("(k p) n -> p k n", p=XKC)).then_inc(w_loaded, 16)
            xv = d["x"].rearrange("(t p) c -> p t c", p=P)
            for q in range(B):
                sp.dma_start(XR[:, q * TB:(q + 1) * TB], xv[:, q * TB:(q + 1) * TB]).then_inc(x_loaded, 16)
            sp.dma_start(WqT[:], d["xWqT"].rearrange("(k p) n -> p k n", p=P)).then_inc(w_loaded, 16)
            sp.dma_start(Wo[:], d["xWo"].rearrange("(k p) n -> p k n", p=P)).then_inc(w_loaded, 16)
            x1v = d["x1_rows"].rearrange("(t p) c -> p t c", p=P)
            with sp.Fori(0, NT) as i:
                sp.wait_ge(x1_kept, i + 1)
                sp.dma_start(x1v[:, bass.ds(i, 1)], XR[:, bass.ds(i, 1)]).then_inc(x1_stored, 16)
            sp.wait_ge(x1_stored, 16 * NT)

        @block.gpsimd
        def _(pool):
            pool.memset(ident[:], 0.0).then_inc(pool_once, 1)
            pool.wait_ge(pool_once, 1)
            pool.affine_select(out=ident[:], in_=ident[:], compare_op=ALU.not_equal, fill=1.0, base=0,
                               pattern=[[-1, P]], channel_multiplier=1).then_inc(pool_once, 1)
            pool.memset(KBD[:], 0.0).then_inc(pool_once, 1)
            pool.memset(VBD[:], 0.0).then_inc(pool_once, 1)
            pool.memset(probs[:, :, S1:S1P], 0.0).then_inc(pool_once, 1)
            pool.wait_ge(pool_once, 5)
            pool.wait_ge(act_once, 1)
            pool.tensor_tensor(bo[:], bo[:], tg[:, 0:1].to_broadcast([P, C]), ALU.mult).then_inc(pool_once, 1)
            pool.wait_ge(pool_once, 6)
            with pool.Fori(0, B) as b:
                for t in range(TB):
                    i = b * TB + t
                    if t < TB:
                        pool.wait_ge(h_made, i + 1)
                        xt = flat(XR[:, bass.ds(i, 1)])
                        pool.tensor_tensor(xt, xt, bo[:], ALU.add).then_inc(bias_added, 1)
                        pool.wait_ge(recip_made, i + 1)
                        pr = probs[:, t % 4, 0:S1].rearrange("p (h m) -> p h m", m=M)
                        pool.tensor_tensor(pr, pr, cols(rc[:, t % 2], M), ALU.mult).then_inc(probs_made, 1)

        @block.scalar
        def _(act):
            for src, dst in ((d["g_xattn"].rearrange("(o n) -> o n", o=1).to_broadcast([P, 1]), tg[:, 0:1]),
                             (d["g_ffn"].rearrange("(o n) -> o n", o=1).to_broadcast([P, 1]), tg[:, 1:2]),
                             (d["xbo"].rearrange("(o n) -> o n", o=1).to_broadcast([P, C]), bo[:]),
                             (d["rt_q"].to_broadcast([P, C]), RT[:, 0]),
                             (d["rt_kv"].to_broadcast([P, C]), RT[:, 1])):
                act.dma_start(dst, src).then_inc(c_loaded, 16)
            act.wait_ge(c_loaded, 16 * 5)
            act.activation(tg[:], tg[:], ACT.Tanh).then_inc(act_once, 1)
            act.wait_ge(vec_once, 1)
            act.activation(LB[:], LA[:], ACT.Ln).then_inc(act_once, 1)
            act.wait_ge(act_once, 2)
            act.activation(LC[:], LB[:], ACT.Exp, scale=-0.5).then_inc(act_once, 1)
            act.wait_ge(pool_once, 3)
            for p in range(XP):
                act.wait_ge(kv_mult, 2 * p + 1)
                for j in range(2):
                    rows = slice(XD * j, XD * (j + 1))
                    act.activation(KBD[rows, :, p, M * j:M * (j + 1)],
                                   ps[(2 * p) % 8][rows, 0:B * M].rearrange("p (b m) -> p b m", m=M),
                                   ACT.Copy, scale=XD ** -0.5).then_inc(kv_evac, 1)
                act.wait_ge(kv_mult, 2 * p + 2)
                act.activation(flat(vT[:, p]), ps[(2 * p + 1) % 8][:, 0:B * M], ACT.Copy).then_inc(kv_evac, 1)
            act.wait_ge(kv_evac, 3 * XP)
            act.wait_ge(pool_once, 4)
            with act.Fori(0, B) as b:
                for j in range(2):
                    rows = slice(XD * j, XD * (j + 1))
                    act.activation(VBD[rows, :, P - 1 + M * j:P - 1 + M * (j + 1)],
                                   vT[rows, :, bass.ds(b, 1), :].rearrange("p x o m -> p x (o m)"),
                                   ACT.Copy).then_inc(vbd_made, 1)
                for n in range(GU):
                    src, hi, _ = gu_group(n)
                    act.wait_ge(gu_mult, GU * b + n + 2)
                    act.activation(hi, src, ACT.Copy).then_inc(gu_hi, 1)
                for t in range(-1, TB + 2):
                    if t + 1 < TB:
                        act.wait_ge(h_turned, b * TB + t + 2)
                        act.activation(hThi[:, (t + 1) % 2], bank_h[:, 0:C], ACT.Copy).then_inc(hhi_made, 1)
                    if t >= 2:
                        for j in range(3):
                            w = min(512, S1P - 512 * j)
                            act.wait_ge(p_turned, 3 * (b * TB + t - 2) + j + 1)
                            act.activation(pThi[:, 512 * j:512 * j + w], banks_p[j][:, 0:w], ACT.Copy).then_inc(phi_made, 1)
                    if 0 <= t < TB:
                        act.wait_ge(shifted, b * TB + t + 1)
                        act.activation(probs[:, t % 4, 0:S1], probs[:, t % 4, 0:S1], ACT.Exp).then_inc(exp_made, 1)

        @block.vector
        def _(dve):
            for i in range(NT):
                if i % TB == 0:
                    dve.wait_ge(x_loaded, 16 * B)
                if i >= 2:
                    dve.wait_ge(mv_made, i - 1)
                dve.bn_stats(bst[:, i % 2], XR[:, i]).then_inc(stats_made, 1)
                dve.wait_ge(stats_made, i + 1)
                dve.bn_aggr(MV[:, i], bst[:, i % 2]).then_inc(mv_made, 1)
            dve.wait_ge(mv_made, NT)
            dve.tensor_scalar(LA[:], MV[:, :, 1], EPS, None, ALU.add).then_inc(vec_once, 1)
            dve.wait_ge(act_once, 3)
            dve.wait_ge(vec_once, 1)
            rsqrt_step(dve, RS, LC, LA, LB, vec_once, 1)

            def route_product(u, j):
                dve.scalar_tensor_tensor(junk[:, u % 2, j], x1b[:, u % 2], mvb[:, u, 0:1], RT[:, j],
                                         ALU.subtract, ALU.mult, accum_out=sb8[:, j, u:u + 1]).then_inc(routed, 1)

            with dve.Fori(0, B) as b:
                for n in range(GU):
                    src, hi, lo = gu_group(n)
                    dve.wait_ge(gu_hi, GU * b + n + 1)
                    dve.tensor_tensor(lo, src, hi.bitcast(F32), ALU.subtract).then_inc(gu_lo, 1)
                for t in range(-1, TB + 2):
                    if t + 1 < TB:
                        i = b * TB + t + 1
                        if t >= 1:
                            dve.wait_ge(h_turned, i - 1)
                        dve.tensor_scalar(h[:, (t + 1) % 2], flat(XR[:, bass.ds(i, 1)]),
                                          MV[:, bass.ds(i, 1), 0], RS[:, bass.ds(i, 1)],
                                          ALU.subtract, ALU.mult).then_inc(h_made, 1)
                    if 0 <= t < TB:
                        dve.wait_ge(scored, b * TB + t + 1)
                        for j, (c0, c1) in enumerate(SCOLS):
                            dve.tensor_reduce(mx[:, t % 2, c0 // M:c1 // M],
                                              banks_s[j][:, 0:c1 - c0].rearrange("p (h m) -> p h m", m=M),
                                              AX_X, ALU.max).then_inc(max_made, 1)
                    if t + 1 < TB:
                        dve.wait_ge(hhi_made, b * TB + t + 2)
                        dve.tensor_tensor(hTlo[:, (t + 1) % 2], bank_h[:, 0:C], hThi[:, (t + 1) % 2].bitcast(F32),
                                          ALU.subtract).then_inc(hlo_made, 1)
                    if t >= 2:
                        for j in range(3):
                            w = min(512, S1P - 512 * j)
                            at = slice(512 * j, 512 * j + w)
                            dve.wait_ge(phi_made, 3 * (b * TB + t - 2) + j + 1)
                            dve.tensor_tensor(pTlo[:, at], banks_p[j][:, 0:w], pThi[:, at].bitcast(F32),
                                              ALU.subtract).then_inc(plo_made, 1)
                    if 0 <= t < TB:
                        dve.wait_ge(max_made, 3 * (b * TB + t + 1))
                        for j, (c0, c1) in enumerate(SCOLS):
                            ins = dve.tensor_tensor(probs[:, t % 4, c0:c1].rearrange("p (h m) -> p h m", m=M),
                                                    banks_s[j][:, 0:c1 - c0].rearrange("p (h m) -> p h m", m=M),
                                                    cols(mx[:, t % 2, c0 // M:c1 // M], M), ALU.subtract)
                        ins.then_inc(shifted, 1)
                        dve.wait_ge(exp_made, b * TB + t + 1)
                        dve.tensor_reduce(sm[:, t % 2], probs[:, t % 4, 0:S1].rearrange("p (h m) -> p h m", m=M),
                                          AX_X, ALU.add).then_inc(sum_made, 1)
                        dve.wait_ge(sum_made, b * TB + t + 1)
                        dve.reciprocal(rc[:, t % 2], sm[:, t % 2]).then_inc(recip_made, 1)
                    if t >= 2:
                        i = b * TB + t - 2
                        u = t - 2
                        xt = flat(XR[:, bass.ds(i, 1)])
                        dve.wait_ge(pv_done, i + 1)
                        dve.wait_ge(bias_added, i + 1)
                        dve.scalar_tensor_tensor(x1b[:, u % 2], bank_o[:, 0:C], tg[:, 0:1], xt, ALU.mult, ALU.add).then_inc(x1_made, 1)
                        dve.scalar_tensor_tensor(xt, bank_o[:, 0:C], tg[:, 0:1], xt, ALU.mult, ALU.add).then_inc(x1_kept, 1)
                        dve.wait_ge(x1_made, i + 1)
                        dve.bn_stats(bst[:, u % 2], x1b[:, u % 2]).then_inc(stats_made, 1)
                        dve.wait_ge(stats_made, i + NT + 1)
                        if u >= 1:
                            dve.wait_ge(mv_made, i + NT)
                            route_product(u - 1, 0)
                        else:
                            dve.tensor_scalar(junk[:, 0, 0, 0:1], tg[:, 0:1], 0.0, None, ALU.mult).then_inc(spaced, 1)
                        dve.bn_aggr(mvb[:, u], bst[:, u % 2]).then_inc(mv_made, 1)
                        if u >= 1:
                            route_product(u - 1, 1)
                dve.wait_ge(mv_made, NT + TB * (b + 1))
                for j in range(2):
                    route_product(TB - 1, j)
                dve.tensor_scalar(MV[:, bass.ds(b * TB, TB)], mvb[:], 0.0, None, ALU.add).then_inc(mv_kept, 1)
                dve.wait_ge(routed, 2 * TB * (b + 1))
                for j in range(2):
                    dve.tensor_scalar(sraw[:, j, bass.ds(b * TB, TB)], sb8[:, j], 0.0, None, ALU.add).then_inc(mv_kept, 1)
                dve.wait_ge(mv_kept, 3 * (b + 1))

        @block.tensor
        def _(pe):
            pe.wait_ge(w_loaded, 16 * 5)
            for p in range(XP):
                for v in range(2):
                    n = 2 * p + v
                    if n >= 8:
                        pe.wait_ge(kv_evac, 3 * (n // 2 - 4) + (2 if v == 0 else 3))
                    for kc in range(2):
                        ins = pe.matmul(ps[n % 8][:, 0:B * M], Wkv[:, v, kc, P * p:P * (p + 1)], ctx[:, kc],
                                        start=(kc == 0), stop=(kc == 1))
                    ins.then_inc(kv_mult, 1)
            pe.wait_ge(kv_evac, 3 * XP)
            pe.wait_ge(pool_once, 5)
            pe.matmul(bank_o[0:1, 0:1], ident[:, 0:1], ident[:, 0:1], start=True, stop=True).then_inc(gu_mult, 1)
            with pe.Fori(0, B) as b:
                for n in range(GU):
                    bank, _, _ = gu_group(n)
                    if n >= 4:
                        pe.wait_ge(gu_lo, GU * b + n - 3)
                    if n < GN:
                        c, (p0, p1) = n // len(GPAIRS), GPAIRS[n % len(GPAIRS)]
                        for p in range(p0, p1):
                            ins = pe.matmul(bank[:, PW * (p - p0):PW * (p - p0 + 1)], WqT[:, p, P * c:P * (c + 1)],
                                            KBD[:, bass.ds(b, 1), p, :].rearrange("p o m -> p (o m)"),
                                            start=True, stop=True)
                    else:
                        if n == GN:
                            pe.wait_ge(vbd_made, 2 * (b + 1))
                        for j in range(2):
                            t = 2 * (n - GN) + j
                            over = [p for p in range(XP) if PW * p < P * (t + 1) and PW * (p + 1) > P * t]
                            for p in over:
                                at = P - 1 + P * t - PW * p
                                ins = pe.matmul(bank[:, C * j:C * (j + 1)], VBD[:, p, at:at + P], Wo[:, p],
                                                start=(p == over[0]), stop=(p == over[-1]))
                    ins.then_inc(gu_mult, 1)
                for t in range(-1, TB + 2):
                    if 0 <= t < TB:
                        pe.wait_ge(hlo_made, b * TB + t + 1)
                        if t == 0:
                            pe.wait_ge(gu_lo, GU * (b + 1))
                        else:
                            pe.wait_ge(shifted, b * TB + t)
                        passes = [(hh, g, c) for hh, g in ((hThi, Ghi), (hThi, Glo), (hTlo, Ghi)) for c in range(CC)]
                        for n, (hh, g, c) in enumerate(passes):
                            for j, (c0, c1) in enumerate(SCOLS):
                                ins = pe.matmul(banks_s[j][:, 0:c1 - c0], hh[:, t % 2, P * c:P * (c + 1)],
                                                g[:, c, c0:c1], start=(n == 0), stop=(n == len(passes) - 1))
                        ins.then_inc(scored, 1)
                    if t + 1 < TB:
                        pe.wait_ge(h_made, b * TB + t + 2)
                        if t == -1:
                            pe.wait_ge(pool_once, 2)
                        for c in range(CC):
                            ins = pe.transpose(bank_h[:, P * c:P * (c + 1)], h[:, (t + 1) % 2, P * c:P * (c + 1)], ident[:])
                        ins.then_inc(h_turned, 1)
                    if t >= 2:
                        u = t - 2
                        i = b * TB + u
                        pe.wait_ge(probs_made, i + 1)
                        for q in range(KT):
                            ins = pe.transpose(banks_p[q // 4][:, P * (q % 4):P * (q % 4 + 1)],
                                               probs[:, u % 4, P * q:P * (q + 1)], ident[:])
                            if q % 4 == 3 or q == KT - 1:
                                ins.then_inc(p_turned, 1)
                        if u >= 1:
                            pe.wait_ge(x1_made, i)
                        for q in range(KT):
                            if q % 4 == 0:
                                pe.wait_ge(plo_made, 3 * i + q // 4 + 1)
                            for n, (pt, uu) in enumerate(((pThi, Uhi), (pThi, Ulo), (pTlo, Uhi))):
                                ins = pe.matmul(bank_o[:, 0:C], pt[:, P * q:P * (q + 1)], uu[:, q],
                                                start=(q == 0 and n == 0), stop=(q == KT - 1 and n == 2))
                        ins.then_inc(pv_done, 1)


def rsqrt_step(dve, out, r, a, tmp, sem, n):
    dve.tensor_tensor(tmp[:], r[:], r[:], ALU.mult).then_inc(sem, 1)
    dve.wait_ge(sem, n + 1)
    dve.tensor_tensor(tmp[:], tmp[:], a[:], ALU.mult).then_inc(sem, 1)
    dve.wait_ge(sem, n + 2)
    dve.tensor_scalar(tmp[:], tmp[:], -0.5, 1.5, ALU.mult, ALU.add).then_inc(sem, 1)
    dve.wait_ge(sem, n + 3)
    dve.tensor_tensor(out[:], r[:], tmp[:], ALU.mult).then_inc(sem, 1)
    dve.wait_ge(sem, n + 4)


def routing(nc, k, ps, d):
    MV, RS, ident, sraw, IDX = k["MV"], k["RS"], k["ident"], k["sraw"], k["IDX"]
    R = 2 * B
    with ExitStack() as stack:
        s = Space(nc, stack, "route")
        S, D, Wt, J = (s.sb(n, [R, N]) for n in ("S", "D", "Wt", "J"))
        V, LT, EQ, Z = (s.sb(n, [R, N]) for n in ("V", "LT", "EQ", "Z"))
        LA, LB, LC = s.sb("rLA", [P, NT]), s.sb("rLB", [P, NT]), s.sb("rLC", [P, NT])
        S64 = s.sb("S64", [2 * NT, P])
        rows = s.sb("rows", [R, 4])
        bits = s.sb("bits", [R, 32], I32)
        smax, T, base, c, lnc, cnt, need = (s.sb(n, [R, 1]) for n in ("smax", "T", "base", "c", "lnc", "cnt", "need"))
        cs = s.sb("cs", [R, 1])
        prefix, cand, fewer = (s.sb(n, [R, 1], I32) for n in ("prefix", "cand", "fewer"))
        posT = s.sb("posT", [P, TB, R])
        ranks = s.sb("ranks", [P, NKV])
        token = s.sb("token", [P, TB], F16)
        hot = s.sb("hot", [P, 4, NKV], F16)
        k1, inv_k, kk = rows[:, 0:1], rows[:, 1:2], rows[:, 2:3]

        loaded, stored, pool_once, vec, act_s, turned = (s.sem(n) for n in (
            "r_loaded", "r_stored", "r_pool", "r_vec", "r_act", "r_turned"))
        shifted, exp_made, summed, ln_made = s.sem("r_shifted"), s.sem("r_exp"), s.sem("r_summed"), s.sem("r_ln")
        bit_step, picked, hot_made, found = s.sem("r_bit"), s.sem("r_picked"), s.sem("r_hot"), s.sem("r_found")
        block = stack.enter_context(nc.Block())

        @block.sync
        def _(sp):
            sp.dma_start(rows[:], d["rows8"]).then_inc(loaded, 16)
            sp.dma_start(bits[:], d["bits8"]).then_inc(loaded, 16)
            sp.wait_ge(act_s, 3)
            sp.dma_start(d["s_rows"], S64[:]).then_inc(stored, 16)
            sp.wait_ge(stored, 16)
            sp.dma_start(S[:], d["s_rows"].rearrange("(r t) n -> r (t n)", t=TB)).then_inc(stored, 16)

        @block.gpsimd
        def _(pool):
            pool.memset(Z[:], 0.0).then_inc(pool_once, 1)
            pool.iota(ranks[:], pattern=[[1, NKV]], base=1, channel_multiplier=0,
                      allow_small_or_imprecise_dtypes=True).then_inc(pool_once, 1)
            pool.iota(token[:], pattern=[[P, TB]], base=0, channel_multiplier=1,
                      allow_small_or_imprecise_dtypes=True).then_inc(pool_once, 1)

        @block.scalar
        def _(act):
            act.wait_ge(vec, 1)
            act.activation(LB[:], LA[:], ACT.Ln).then_inc(act_s, 1)
            act.wait_ge(act_s, 1)
            act.activation(LC[:], LB[:], ACT.Exp, scale=-0.5).then_inc(act_s, 1)
            act.wait_ge(turned, 1)
            act.activation(S64[:], ps[0][0:2 * NT, 0:P], ACT.Copy).then_inc(act_s, 1)
            with act.Fori(0, BLOCKS) as n:
                act.wait_ge(shifted, 3 * n + 3)
                act.activation(Wt[:], D[:], ACT.Exp).then_inc(exp_made, 1)
                act.wait_ge(summed, 2 * UPD * n + 2 * UPD)
                act.activation(lnc[:], c[:], ACT.Ln).then_inc(ln_made, 1)

        @block.tensor
        def _(pe):
            pe.wait_ge(vec, 7)
            pe.transpose(ps[0][0:2 * NT, 0:P], sraw[:].rearrange("p j t -> p (j t)"), ident[:]).then_inc(turned, 1)
            pe.wait_ge(picked, 7)
            for t in range(TB):
                ins = pe.transpose(ps[1][:, R * t:R * (t + 1)], D[:, P * t:P * (t + 1)], ident[0:R, 0:R])
            ins.then_inc(turned, 1)
            pe.wait_ge(pool_once, 3)
            n = 0
            for r in range(R):
                for t in range(TB):
                    n += 1
                    pe.wait_ge(hot_made, n)
                    if r < B:
                        ins = pe.matmul(ps[2][:, r:r + 1], hot[:, (n - 1) % 4, 0:NQ], token[:, t:t + 1],
                                        start=(t == 0), stop=(t == TB - 1))
                    else:
                        for j in range(2):
                            ins = pe.matmul(ps[3 + j][:, r - B:r - B + 1], hot[:, (n - 1) % 4, P * j:P * (j + 1)],
                                            token[:, t:t + 1], start=(t == 0), stop=(t == TB - 1))
                    ins.then_inc(found, 1)

        @block.vector
        def _(dve):
            dve.tensor_scalar(LA[:], MV[:, :, 1], EPS, None, ALU.add).then_inc(vec, 1)
            dve.wait_ge(act_s, 2)
            dve.wait_ge(vec, 1)
            rsqrt_step(dve, RS, LC, LA, LB, vec, 1)
            for j in range(2):
                dve.tensor_tensor(sraw[:, j], sraw[:, j], RS[:], ALU.mult).then_inc(vec, 1)
            dve.wait_ge(loaded, 32)
            dve.wait_ge(stored, 32)
            dve.tensor_reduce(smax[:], S[:], AX_X, ALU.max).then_inc(vec, 1)
            dve.tensor_scalar(T[:], k1, 0.0, None, ALU.add).then_inc(vec, 1)
            dve.wait_ge(vec, 9)
            with dve.Fori(0, BLOCKS) as n:
                dve.tensor_tensor(base[:], T[:], smax[:], ALU.min).then_inc(shifted, 1)
                dve.wait_ge(shifted, 3 * n + 1)
                dve.tensor_scalar(D[:], S[:], base[:], CAP, ALU.subtract, ALU.min).then_inc(shifted, 1)
                dve.tensor_scalar(c[:], base[:], 0.0, 1.0, ALU.mult, ALU.add).then_inc(shifted, 1)
                dve.wait_ge(exp_made, n + 1)
                dve.wait_ge(shifted, 3 * n + 3)
                for u in range(UPD):
                    dve.tensor_scalar(J[:], Wt[:], c[:], None, ALU.min, ALU.add, accum_out=cs[:]).then_inc(summed, 1)
                    dve.wait_ge(summed, 2 * UPD * n + 2 * u + 1)
                    dve.tensor_tensor(c[:], cs[:], inv_k, ALU.mult).then_inc(summed, 1)
                    dve.wait_ge(summed, 2 * UPD * n + 2 * u + 2)
                dve.wait_ge(ln_made, n + 1)
                dve.tensor_tensor(T[:], base[:], lnc[:], ALU.add).then_inc(bit_step, 1)
                dve.wait_ge(bit_step, n + 1)
            dve.tensor_scalar(D[:], S[:], T[:], 0.0, ALU.subtract, ALU.min).then_inc(vec, 1)
            dve.wait_ge(vec, 10)
            dve.tensor_scalar(V[:], D[:], -1.0, SMALLEST, ALU.mult, ALU.min).then_inc(vec, 1)
            dve.memset(prefix[:], 0).then_inc(vec, 1)
            dve.wait_ge(vec, 12)
            with dve.Fori(0, 31) as n:
                dve.tensor_tensor(cand[:], prefix[:], bits[:, bass.ds(n, 1)], ALU.bitwise_or).then_inc(bit_step, 1)
                dve.wait_ge(bit_step, 4 * n + BLOCKS + 1)
                dve.tensor_scalar(J[:], V[:], cand[:].bitcast(F32), None, ALU.is_lt, ALU.add, accum_out=cnt[:]).then_inc(bit_step, 1)
                dve.wait_ge(bit_step, 4 * n + BLOCKS + 2)
                dve.scalar_tensor_tensor(fewer[:], cnt[:], kk, bits[:, bass.ds(n, 1)], ALU.is_lt, ALU.mult).then_inc(bit_step, 1)
                dve.wait_ge(bit_step, 4 * n + BLOCKS + 3)
                dve.tensor_tensor(prefix[:], prefix[:], fewer[:], ALU.bitwise_or).then_inc(bit_step, 1)
                dve.wait_ge(bit_step, 4 * n + BLOCKS + 4)
            kth = prefix[:].bitcast(F32)
            dve.tensor_scalar(LT[:], V[:], kth, None, ALU.is_lt, ALU.add, accum_out=cnt[:]).then_inc(picked, 1)
            dve.tensor_scalar(EQ[:], V[:], kth, None, ALU.is_equal).then_inc(picked, 1)
            dve.wait_ge(picked, 2)
            dve.wait_ge(pool_once, 3)
            dve.tensor_tensor(need[:], kk, cnt[:], ALU.subtract).then_inc(picked, 1)
            dve.tensor_tensor_scan(J[:], EQ[:], Z[:], 0.0, ALU.add, ALU.add).then_inc(picked, 1)
            dve.wait_ge(picked, 4)
            dve.scalar_tensor_tensor(D[:], J[:], need[:], EQ[:], ALU.is_le, ALU.mult).then_inc(picked, 1)
            dve.wait_ge(picked, 5)
            dve.tensor_tensor(LT[:], LT[:], D[:], ALU.add).then_inc(picked, 1)
            dve.wait_ge(picked, 6)
            dve.tensor_tensor_scan(J[:], LT[:], Z[:], 0.0, ALU.add, ALU.add).then_inc(vec, 1)
            dve.wait_ge(vec, 13)
            dve.tensor_tensor(D[:], J[:], LT[:], ALU.mult).then_inc(picked, 1)
            dve.wait_ge(turned, 2)
            dve.tensor_copy(posT[:].rearrange("p t r -> p (t r)"), ps[1][:, 0:TB * R]).then_inc(vec, 1)
            dve.wait_ge(vec, 14)
            n = 0
            for r in range(R):
                for t in range(TB):
                    n += 1
                    if n > 4:
                        dve.wait_ge(found, n - 4)
                    w = NQ if r < B else NKV
                    dve.tensor_scalar(hot[:, (n - 1) % 4, 0:w], ranks[:, 0:w], posT[:, t, r:r + 1], None,
                                      ALU.is_equal).then_inc(hot_made, 1)
            dve.wait_ge(found, R * TB)
            for b in range(B):
                for j in range(3):
                    src = ps[2][:, b:b + 1] if j == 0 else ps[2 + j][:, b:b + 1]
                    dve.tensor_scalar(IDX[:, 3 * b + j:3 * b + j + 1], src, float(N * b), None, ALU.add).then_inc(vec, 1)


def windowed_attention(nc, k, ps, d):
    XR, MV, ident, tg = k["XR"], k["MV"], k["ident"], k["tg"]
    with ExitStack() as stack:
        s = Space(nc, stack, "window")
        Whi, Wlo = s.sb("Whi", [P, CC, 3 * IN], F32R), s.sb("Wlo", [P, CC, 3 * IN], F32R)
        QT = s.sb("QT", [P, HP, N])
        KD = s.sb("KD", [P, HP, 2, N])
        V = s.sb("V", [P, TB, IN])
        VX = s.sb("VX", [P, TB, IN])
        WoT = s.sb("WoT", [P, HP, C])
        y = s.sb("y", [P, 2, C])
        yT = s.sb("yT", [P, 2, CC, P])
        OT = s.sb("OT", [P, HP * P])
        outb = s.sb("outb", [P, 2, C])
        null = s.sb("null", [P, C])
        R2, LA, LB, LC = (s.sb(n, [P, NT]) for n in ("R2", "wLA", "wLB", "wLC"))
        wb = s.sb("wb", [P, 2, CC])
        edge = s.sb("edge", [P, 2])
        mx, sm, rc = s.sb("wmx", [P, 2, H]), s.sb("wsm", [P, 2, H]), s.sb("wrc", [P, 2, H])
        mxe = s.sb("wmxe", [P, H])
        with ExitStack() as early:
            Wst = Space(nc, early, "window").sb("Wst", [P, CC, 3 * IN])
        with ExitStack() as early:
            e = Space(nc, early, "window")
            yhi, ylo = e.sb("yhi", [P, CC, N], F32R), e.sb("ylo", [P, CC, N], F32R)
        E = s.sb("E", [P, 2, H, 3 * W])
        probs = s.sb("wprobs", [P, 2, H, 2 * P])
        pT = s.sb("wpT", [P, H, 2, P])
        banks_s, bank_e, banks_p, bank_v, bank_o = ps[0:2], ps[2], ps[3:6], ps[6], ps[7]

        loaded, w_loaded, once, split = s.sem("w_loaded2"), s.sem("w_loaded3"), s.sem("w_once"), s.sem("w_split")
        pool_once, z_stored = s.sem("w_pool"), s.sem("z_stored")
        out_stored = [s.sem("out_stored_0"), s.sem("out_stored_1")]
        y_made, y_turned, yT_made, yhi_made, ylo_made = (s.sem(n) for n in (
            "y_made", "y_turned", "yT_made", "yhi_made", "ylo_made"))
        qkv_mult, qkv_evac, vx_made = s.sem("qkv_mult"), s.sem("qkv_evac"), s.sem("vx_made")
        scored, max_made, max_joined, shifted, exp_made = (s.sem(n) for n in (
            "w_scored", "w_max", "w_max_joined", "w_shifted", "w_exp"))
        sum_made, recip_made, probs_made = s.sem("w_sum"), s.sem("w_recip"), s.sem("w_probs")
        p_turned, pT_made, pv_done, oT_made = s.sem("w_p_turned"), s.sem("w_pT"), s.sem("w_pv"), s.sem("w_oT")
        projected, z_made, out_made = s.sem("w_projected"), s.sem("z_made"), s.sem("out_made")
        NQK = 16
        NG = NQK + TB
        NEV = NQK + 8 + TB
        block = stack.enter_context(nc.Block())

        def evacs(n):
            if n < NQK:
                half, m = n // 8, n % 8
                return half * 12 + (m + 1 if m < HP else HP + 2 * (m - HP + 1))
            return 24 + n - NQK + 1

        @block.sync
        def _(sp):
            sp.dma_start(Wst[:], d["WqkvT"].rearrange("(k p) n -> p k n", p=P)).then_inc(w_loaded, 16)
            sp.dma_start(WoT[:], d["WoutlT"].rearrange("(k p) n -> p k n", p=P)).then_inc(w_loaded, 16)
            for j in range(2):
                sp.dma_start(outb[:, j], d["x"][0:P, :]).then_inc(out_stored[j], 16)
            zv = d["z_rows"].rearrange("(t p) c -> p t c", p=P)
            ov = d["out"].rearrange("(t p) c -> p t c", p=P)
            with sp.Fori(0, NT // 2) as i:
                for j in range(2):
                    sp.wait_ge(z_made, 2 * i + j + 1)
                    sp.dma_start(zv[:, bass.ds(2 * i + j, 1)], XR[:, bass.ds(2 * i + j, 1)]).then_inc(z_stored, 16)
                    sp.wait_ge(out_made, 2 * i + j + 1)
                    sp.dma_start(ov[:, bass.ds(2 * i + j, 1)], outb[:, j]).then_inc(out_stored[j], 16)
            sp.wait_ge(z_stored, 16 * NT)
            for j in range(2):
                sp.wait_ge(out_stored[j], 16 * (NT // 2 + 1))

        @block.gpsimd
        def _(pool):
            pool.memset(KD[:], 0.0).then_inc(pool_once, 1)
            pool.memset(VX[:], 0.0).then_inc(pool_once, 1)
            pool.wait_ge(loaded, 16 * 4)
            pool.tensor_tensor(null[:], null[:], tg[:, 1:2].to_broadcast([P, C]), ALU.mult).then_inc(pool_once, 1)
            pool.wait_ge(pool_once, 3)
            with pool.Fori(0, B) as b:
                for t in range(TB + 2):
                    if t < TB:
                        i = b * TB + t
                        pool.wait_ge(recip_made, i + 1)
                        if t >= 2:
                            pool.wait_ge(p_turned, 4 * (i - 1))
                        r = rc[:, t % 2]
                        pool.tensor_tensor(probs[:, t % 2, :, 0:P], E[:, t % 2, :, 0:P], cols(r, P), ALU.mult).then_inc(probs_made, 1)
                        pool.wait_ge(probs_made, 3 * i + 1)
                        pool.tensor_tensor(probs[0:W, t % 2, :, P + W:2 * P], E[0:W, t % 2, :, P:3 * W],
                                           cols(rc[0:W, t % 2], W), ALU.mult).then_inc(probs_made, 1)
                        pool.tensor_tensor(probs[W:P, t % 2, :, P:P + W], E[W:P, t % 2, :, P:3 * W],
                                           cols(rc[W:P, t % 2], W), ALU.mult).then_inc(probs_made, 1)
                        pool.wait_ge(probs_made, 3 * i + 3)
                    if t >= 2:
                        i = b * TB + t - 2
                        pool.wait_ge(z_made, i + 1)
                        pool.wait_ge(out_stored[t % 2], 16 * (b * (TB // 2) + (t - 2) // 2 + 1))
                        pool.tensor_tensor(outb[:, t % 2], flat(XR[:, bass.ds(i, 1)]), null[:], ALU.add).then_inc(out_made, 1)
                        pool.wait_ge(out_made, i + 1)

        @block.scalar
        def _(act):
            act.dma_start(null[:], d["null_q"].rearrange("(o n) -> o n", o=1).to_broadcast([P, C])).then_inc(loaded, 16)
            act.dma_start(wb[:, 0], d["ln_w"]).then_inc(loaded, 16)
            act.dma_start(wb[:, 1], d["ln_b"]).then_inc(loaded, 16)
            act.dma_start(edge[:], d["edge"]).then_inc(loaded, 16)
            act.wait_ge(once, 3)
            act.activation(LB[:], LA[:], ACT.Ln).then_inc(split, 1)
            act.wait_ge(split, 1)
            act.activation(LC[:], LB[:], ACT.Exp, scale=-0.5).then_inc(split, 1)
            act.wait_ge(w_loaded, 32)
            act.activation(flat(Whi[:]), flat(Wst[:]), ACT.Copy).then_inc(split, 1)
            act.wait_ge(pool_once, 2)

            with act.Fori(0, B) as b:
                def out_of(n):
                    act.wait_ge(qkv_mult, NG * b + n + 1)
                    bank = ps[n % 4]
                    if n >= NQK:
                        act.activation(V[:, n - NQK], bank[:], ACT.Copy).then_inc(qkv_evac, 1)
                        return
                    half, m = n // 8, n % 8
                    at = slice(512 * half, 512 * half + 512)
                    if m < HP:
                        act.activation(QT[:, m, at], bank[:], ACT.Copy, scale=SCALE).then_inc(qkv_evac, 1)
                        return
                    for j in range(2):
                        rows = slice(DH * j, DH * (j + 1))
                        act.activation(KD[rows, m - HP, j, at], bank[rows, :], ACT.Copy).then_inc(qkv_evac, 1)

                for half in range(2):
                    for t in range(4 * half, 4 * half + 4):
                        act.wait_ge(yT_made, 2 * (b * TB + t) + 2)
                        act.activation(yhi[:, :, P * t:P * (t + 1)], yT[:, t % 2], ACT.Copy).then_inc(yhi_made, 1)
                    for n in range(8 * half, 8 * half + 8):
                        out_of(n)
                for n in range(NQK, NG):
                    out_of(n)
                for t in range(TB + 2):
                    if t >= 2:
                        for g in range(4):
                            n = 4 * (t - 2) + g
                            act.wait_ge(p_turned, 4 * TB * b + n + 1)
                            act.activation(pT[:, 2 * g:2 * g + 2].rearrange("p h k n -> p (h k n)"), banks_p[n % 3][:],
                                           ACT.Copy).then_inc(pT_made, 1)
                    if t < TB:
                        act.wait_ge(shifted, b * TB + t + 1)
                        act.activation(E[:, t % 2], E[:, t % 2], ACT.Exp).then_inc(exp_made, 1)

        @block.vector
        def _(dve):
            dve.tensor_scalar(LA[:], MV[:, :, 1], EPS, EPS, ALU.add, ALU.mult).then_inc(once, 1)
            dve.wait_ge(once, 1)
            dve.tensor_tensor(LA[:], LA[:], MV[:, :, 1], ALU.add).then_inc(once, 1)
            dve.wait_ge(once, 2)
            dve.memset(mxe[:], 0.0).then_inc(once, 1)
            dve.wait_ge(split, 2)
            rsqrt_step(dve, R2, LC, LA, LB, once, 3)
            dve.wait_ge(split, 3)
            dve.tensor_tensor(flat(Wlo[:]), flat(Wst[:]), flat(Whi[:]).bitcast(F32), ALU.subtract).then_inc(once, 1)
            dve.wait_ge(loaded, 16 * 4)
            dve.wait_ge(once, 8)
            with dve.Fori(0, B) as b:
                for t in range(-1, TB):
                    if t + 1 < TB:
                        i = b * TB + t + 1
                        if t >= 1:
                            dve.wait_ge(y_turned, i - 1)
                        dve.tensor_scalar(y[:, (t + 1) % 2], flat(XR[:, bass.ds(i, 1)]), MV[:, bass.ds(i, 1), 0],
                                          R2[:, bass.ds(i, 1)], ALU.subtract, ALU.mult).then_inc(y_made, 1)
                    if t >= 0:
                        i = b * TB + t
                        dve.wait_ge(y_turned, i + 1)
                        if t >= 2:
                            dve.wait_ge(ylo_made, i - 1)
                        for c in range(CC):
                            dve.tensor_scalar(yT[:, t % 2, c], ps[6 + t % 2][:, P * c:P * (c + 1)], wb[:, 0, c:c + 1],
                                              wb[:, 1, c:c + 1], ALU.mult, ALU.add).then_inc(yT_made, 1)
                        dve.wait_ge(yhi_made, i + 1)
                        at = slice(P * t, P * (t + 1))
                        dve.tensor_tensor(ylo[:, :, at], yT[:, t % 2], yhi[:, :, at].bitcast(F32), ALU.subtract).then_inc(ylo_made, 1)
                dve.wait_ge(qkv_evac, NEV * (b + 1))
                dve.tensor_copy(VX[0:W, 0:TB - 1], V[0:W, 1:TB]).then_inc(vx_made, 1)
                dve.tensor_copy(VX[W:P, 1:TB], V[W:P, 0:TB - 1]).then_inc(vx_made, 1)
                for j in range(2):
                    dve.memset(probs[0:W, j, :, P:P + W], 0.0).then_inc(vx_made, 1)
                    dve.memset(probs[W:P, j, :, P + W:2 * P], 0.0).then_inc(vx_made, 1)
                for t in range(TB + 2):
                    u = t - 2
                    if t < TB:
                        i = b * TB + t
                        dve.wait_ge(scored, i + 1)
                        own = mx[:, t % 2]
                        for j in range(2):
                            dve.tensor_reduce(own[:, 4 * j:4 * j + 4], banks_s[j][:].rearrange("p (h m) -> p h m", m=P),
                                              AX_X, ALU.max).then_inc(max_made, 1)
                        dve.tensor_reduce(mxe[:], bank_e[:].rearrange("p (h m) -> p h m", m=W), AX_X, ALU.max).then_inc(max_made, 1)
                        dve.wait_ge(max_made, 3 * i + 3)
                        mask = edge[:, 0:1] if t == 0 else edge[:, 1:2] if t == TB - 1 else 0.0
                        dve.scalar_tensor_tensor(own, mxe[:], mask, own, ALU.add, ALU.max).then_inc(max_joined, 1)
                        dve.wait_ge(max_joined, i + 1)
                        if t >= 2:
                            dve.wait_ge(probs_made, 3 * (i - 1))
                        for j in range(2):
                            dve.tensor_tensor(E[:, t % 2, 4 * j:4 * j + 4, 0:P], banks_s[j][:].rearrange("p (h m) -> p h m", m=P),
                                              cols(mx[:, t % 2, 4 * j:4 * j + 4], P), ALU.subtract)
                        dve.scalar_tensor_tensor(E[:, t % 2, :, P:3 * W], bank_e[:].rearrange("p (h m) -> p h m", m=W), mask,
                                                 cols(own, W), ALU.add, ALU.subtract).then_inc(shifted, 1)
                    if u >= 0:
                        dve.wait_ge(pv_done, b * TB + u + 1)
                        dve.tensor_copy(OT[:], bank_v[:]).then_inc(oT_made, 1)
                    if t < TB:
                        dve.wait_ge(exp_made, i + 1)
                        dve.tensor_reduce(sm[:, t % 2], E[:, t % 2], AX_X, ALU.add).then_inc(sum_made, 1)
                        dve.wait_ge(sum_made, i + 1)
                        dve.reciprocal(rc[:, t % 2], sm[:, t % 2]).then_inc(recip_made, 1)
                    if u >= 0:
                        i = b * TB + u
                        xt = flat(XR[:, bass.ds(i, 1)])
                        dve.wait_ge(projected, i + 1)
                        dve.scalar_tensor_tensor(xt, bank_o[:, 0:C], tg[:, 1:2], xt, ALU.mult, ALU.add).then_inc(z_made, 1)

        @block.tensor
        def _(pe):
            pe.wait_ge(once, 8)
            with pe.Fori(0, B) as b:
                def turn(t):
                    i = b * TB + t
                    pe.wait_ge(y_made, i + 1)
                    if t >= 2:
                        pe.wait_ge(yT_made, 2 * (i - 1))
                    for c in range(CC):
                        ins = pe.transpose(ps[6 + t % 2][:, P * c:P * (c + 1)], y[:, t % 2, P * c:P * (c + 1)], ident[:])
                    ins.then_inc(y_turned, 1)

                def project(n):
                    if n >= 4:
                        pe.wait_ge(qkv_evac, NEV * b + evacs(n - 4))
                    passes = [(a, w, c) for a, w in ((yhi, Whi), (yhi, Wlo), (ylo, Whi)) for c in range(CC)]
                    for q, (a, w, c) in enumerate(passes):
                        if n < NQK:
                            half, m = n // 8, n % 8
                            lhs, rhs = w[:, c, P * m:P * (m + 1)], a[:, c, 512 * half:512 * half + 512]
                        else:
                            t = n - NQK
                            lhs, rhs = a[:, c, P * t:P * (t + 1)], w[:, c, 2 * IN:3 * IN]
                        ins = pe.matmul(ps[n % 4][:], lhs, rhs, start=(q == 0), stop=(q == len(passes) - 1))
                    ins.then_inc(qkv_mult, 1)

                for half in range(2):
                    for t in range(4 * half, 4 * half + 4):
                        turn(t)
                    pe.wait_ge(ylo_made, b * TB + 4 * half + 4)
                    for n in range(8 * half, 8 * half + 8):
                        project(n)
                for n in range(NQK, NG):
                    project(n)
                pe.wait_ge(qkv_evac, NEV * (b + 1))
                for t in range(TB + 2):
                    u = t - 2
                    if t < TB:
                        if t >= 1:
                            pe.wait_ge(shifted, b * TB + t)
                        for p in range(HP):
                            pe.matmul(banks_s[p // 2][:, 2 * P * (p % 2):2 * P * (p % 2 + 1)], QT[:, p, P * t:P * (t + 1)],
                                      KD[:, p, :, P * t:P * (t + 1)], start=True, stop=True)
                        before, after = max(2 * t - 1, 0), min(2 * t + 2, 2 * TB - 1)
                        for p in range(HP):
                            for j, w in enumerate((before, after)):
                                ins = pe.matmul(bank_e[W * j:W * (j + 1), 2 * W * p:2 * W * (p + 1)],
                                                QT[:, p, P * t + W * j:P * t + W * (j + 1)],
                                                KD[:, p, :, W * w:W * (w + 1)], start=True, stop=True)
                        ins.then_inc(scored, 1)
                    if u >= 0:
                        i = b * TB + u
                        pe.wait_ge(probs_made, 3 * (i + 1))
                        pe.wait_ge(vx_made, 6 * (b + 1))
                        for g in range(4):
                            n = 4 * u + g
                            if n >= 3:
                                pe.wait_ge(pT_made, 4 * TB * b + n - 2)
                            for q in range(4):
                                hh, kc = 2 * g + q // 2, q % 2
                                ins = pe.transpose(banks_p[n % 3][:, P * q:P * (q + 1)],
                                                   probs[:, u % 2, hh, P * kc:P * (kc + 1)], ident[:])
                            ins.then_inc(p_turned, 1)
                        pe.wait_ge(pT_made, 4 * (i + 1))
                        for p in range(HP):
                            for kc, v in enumerate((V, VX)):
                                for j in range(2):
                                    hh = 2 * p + j
                                    ins = pe.matmul(bank_v[DH * j:DH * (j + 1), P * p:P * (p + 1)],
                                                    v[:, u, DH * hh:DH * (hh + 1)], pT[:, hh, kc],
                                                    start=(kc == 0), stop=(kc == 1))
                        ins.then_inc(pv_done, 1)
                        pe.wait_ge(oT_made, i + 1)
                        if u >= 1:
                            pe.wait_ge(z_made, i)
                        for p in range(HP):
                            ins = pe.matmul(bank_o[:, 0:C], OT[:, P * p:P * (p + 1)], WoT[:, p], start=(p == 0), stop=(p == HP - 1))
                        ins.then_inc(projected, 1)


def chosen_attention(nc, k, ps, d):
    ident, tg, IDX = k["ident"], k["tg"], k["IDX"]
    G = 3 * B
    TINY = (1e-12 / C ** 0.5) ** 2
    LIFT = 30
    with ExitStack() as stack:
        s = Space(nc, stack, "chosen")
        Wq, Wkv, Wo = s.sb("Wq", [P, CC, IN]), s.sb("Wkv", [P, CC, 2 * IN]), s.sb("Wo", [P, HP, C])
        X, Z, out_rows = s.sb("X", [P, G, C]), s.sb("Z", [P, B, C]), s.sb("out_rows", [P, B, C])
        bst, mv = s.sb("bst", [P, G, 6]), s.sb("mv", [P, G, 2])
        r, ms, LA, LB, LC, scl = (s.sb(n, [P, G]) for n in ("r", "ms", "LA", "LB", "LC", "scl"))
        gam = s.sb("gam", [P, CC])
        xn, xT = s.sb("xn", [P, 3, C]), s.sb("xT", [P, CC, 3 * P])
        QT, KD, V = s.sb("QT", [P, HP, P]), s.sb("KD", [P, HP, 2, NKV]), s.sb("V", [P, 2, IN])
        NK, nk, NV = s.sb("NK", [P, HP * H]), s.sb("nk", [P, HP]), s.sb("NV", [H, IN])
        E, e0 = s.sb("E", [P, H, NKV]), s.sb("e0", [P, H])
        mx, sm, rc = s.sb("mx", [P, H]), s.sb("sm", [P, H]), s.sb("rc", [P, H])
        pT, p0T, OT = s.sb("pT", [P, H, 2, P]), s.sb("p0T", [H, P]), s.sb("OT", [P, HP * P])

        w_loaded, null_loaded, x_gathered, z_gathered, scattered = (s.sem(n) for n in (
            "w_loaded", "null_loaded", "x_gathered", "z_gathered", "scattered"))
        pool_once, stats, vec, lns = s.sem("pool_once"), s.sem("stats"), s.sem("vec"), s.sem("lns")
        xn_made, x_turned, xT_made = s.sem("xn_made"), s.sem("x_turned"), s.sem("xT_made")
        proj, q_made, kd_made, v_made = s.sem("proj"), s.sem("q_made"), s.sem("kd_made"), s.sem("v_made")
        scored, max_made, shifted, exp_made = s.sem("scored"), s.sem("max_made"), s.sem("shifted"), s.sem("exp_made")
        sum_made, probs_made = s.sem("sum_made"), s.sem("probs_made")
        p_turned, pT_made, pv_done, oT_made = s.sem("p_turned"), s.sem("pT_made"), s.sem("pv_done"), s.sem("oT_made")
        projected, rows_made, null_placed = s.sem("projected"), s.sem("rows_made"), s.sem("null_placed")
        block = stack.enter_context(nc.Block())

        @block.sync
        def _(sp):
            sp.dma_start(gam[:], d["gamma"]).then_inc(w_loaded, 16)
            sp.dma_start(Wq[:], d["hWqT"].rearrange("(k p) n -> p k n", p=P)).then_inc(w_loaded, 16)
            sp.dma_start(Wkv[:], d["hWkvT"].rearrange("(k p) n -> p k n", p=P)).then_inc(w_loaded, 16)
            sp.dma_start(Wo[:], d["hWoutT"].rearrange("(k p) n -> p k n", p=P)).then_inc(w_loaded, 16)
            sp.dma_start(nk[:], d["null_k"]).then_inc(w_loaded, 16)
            sp.wait_ge(vec, 2)
            for h in range(H):
                sp.dma_start(NV[h:h + 1, DH * h:DH * (h + 1)], d["null_v"][h:h + 1, :]).then_inc(null_loaded, 16)

        @block.gpsimd
        def _(pool):
            def rows_of(g):
                return bass.IndirectOffsetOnAxis(ap=IDX[:, g:g + 1].bitcast(U32), axis=0)

            for b in range(B):
                for j in range(3):
                    pool.indirect_dma_start(X[:, 3 * b + j], None, d["x1_rows"], rows_of(3 * b + j)).then_inc(x_gathered, 16)
            for b in range(B):
                pool.indirect_dma_start(Z[:, b], None, d["z_rows"], rows_of(3 * b)).then_inc(z_gathered, 16)
            pool.memset(KD[:], 0.0).then_inc(pool_once, 1)
            for b in range(B):
                pool.wait_ge(rows_made, b + 1)
                pool.indirect_dma_start(d["out"], rows_of(3 * b), out_rows[:, b], None).then_inc(scattered, 16)
            pool.wait_ge(scattered, 16 * B)

        @block.scalar
        def _(act):
            act.wait_ge(vec, 3)
            act.activation(LB[:], LA[:], ACT.Ln).then_inc(lns, 1)
            act.wait_ge(lns, 1)
            act.activation(LC[:], LB[:], ACT.Exp, scale=-0.5).then_inc(lns, 1)
            act.wait_ge(vec, 10)
            act.activation(LB[:], ms[:], ACT.Ln, scale=float(4 ** LIFT)).then_inc(lns, 1)
            act.wait_ge(lns, 3)
            act.activation(LC[:], LB[:], ACT.Exp, scale=-0.5).then_inc(lns, 1)
            act.wait_ge(pool_once, 1)
            with act.Fori(0, B) as b:
                act.wait_ge(proj, 7 * b + 1)
                act.activation(QT[:].rearrange("p k n -> p (k n)"), ps[2][:], ACT.Copy, scale=SCALE).then_inc(q_made, 1)
                for m in range(HP):
                    act.wait_ge(proj, 7 * b + 3 + 2 * (m // 2))
                    for j in range(2):
                        rows = slice(DH * j, DH * (j + 1))
                        act.activation(KD[rows, m, j], ps[3 + m // 2][rows, NKV * (m % 2):NKV * (m % 2 + 1)],
                                       ACT.Copy).then_inc(kd_made, 1)
                act.wait_ge(shifted, 5 * b + 5)
                act.activation(E[:], E[:], ACT.Exp).then_inc(exp_made, 1)
                act.activation(e0[:], e0[:], ACT.Exp).then_inc(exp_made, 1)
                act.wait_ge(p_turned, 5 * b + 1)
                act.activation(p0T[:], ps[7][0:H, P:2 * P], ACT.Copy).then_inc(pT_made, 1)
                for g in range(4):
                    act.wait_ge(p_turned, 5 * b + 2 + g)
                    act.activation(pT[:, 2 * g:2 * g + 2].rearrange("p h k n -> p (h k n)"), ps[4 + g % 3][:], ACT.Copy).then_inc(pT_made, 1)

        @block.vector
        def _(dve):
            dve.memset(NK[:], 0.0).then_inc(vec, 1)
            dve.memset(NV[:], 0.0).then_inc(vec, 1)
            dve.wait_ge(x_gathered, 16 * G)
            for g in range(G):
                dve.bn_stats(bst[:, g], X[:, g]).then_inc(stats, 1)
            dve.wait_ge(stats, G)
            dve.wait_ge(vec, 2)
            dve.memset(sm[:], 0.0)
            for g in range(G):
                dve.bn_aggr(mv[:, g], bst[:, g]).then_inc(stats, 1)
            dve.wait_ge(stats, 2 * G)
            dve.tensor_scalar(LA[:], mv[:, :, 1], EPS, None, ALU.add).then_inc(vec, 1)
            dve.wait_ge(lns, 2)
            dve.wait_ge(vec, 3)
            rsqrt_step(dve, r, LC, LA, LB, vec, 3)
            dve.tensor_tensor(ms[:], mv[:, :, 1], r[:], ALU.mult).then_inc(vec, 1)
            dve.wait_ge(vec, 8)
            dve.tensor_tensor(ms[:], ms[:], r[:], ALU.mult).then_inc(vec, 1)
            dve.wait_ge(vec, 9)
            dve.tensor_scalar(ms[:], ms[:], TINY, None, ALU.max).then_inc(vec, 1)
            dve.wait_ge(lns, 4)
            dve.wait_ge(vec, 10)
            dve.tensor_scalar(LC[:], LC[:], float(2 ** LIFT), None, ALU.mult).then_inc(vec, 1)
            dve.wait_ge(vec, 11)
            rsqrt_step(dve, scl, LC, ms, LB, vec, 11)
            dve.tensor_tensor(scl[:], scl[:], r[:], ALU.mult).then_inc(vec, 1)
            dve.wait_ge(vec, 16)
            dve.wait_ge(w_loaded, 16 * 5)
            for j in range(2):
                dve.tensor_copy(NK[DH * j:DH * (j + 1), j::H + 2], nk[DH * j:DH * (j + 1), :]).then_inc(null_placed, 1)
            with dve.Fori(0, B) as b:
                for j in range(3):
                    g = 3 * b + j
                    dve.tensor_scalar(xn[:, j], flat(X[:, bass.ds(g, 1)]), mv[:, bass.ds(g, 1), 0], scl[:, bass.ds(g, 1)],
                                      ALU.subtract, ALU.mult).then_inc(xn_made, 1)
                for c in range(CC):
                    dve.wait_ge(x_turned, 2 * b + c + 1)
                    dve.tensor_scalar(xT[:, c], ps[c][:, 0:3 * P], gam[:, c:c + 1], None, ALU.mult).then_inc(xT_made, 1)
                for j in range(2):
                    dve.wait_ge(proj, 7 * b + 6 + j)
                    dve.tensor_copy(V[:, j], ps[5 + j][:]).then_inc(v_made, 1)
                for p in range(HP):
                    if p == 0:
                        dve.wait_ge(scored, b + 1)
                    dve.tensor_reduce(mx[:, 2 * p:2 * p + 2], ps[p][:].rearrange("p (h m) -> p h m", m=NKV), AX_X, ALU.max).then_inc(max_made, 1)
                dve.wait_ge(max_made, 5 * b + 4)
                dve.tensor_tensor(mx[:], ps[7][:, 0:H], mx[:], ALU.max).then_inc(max_made, 1)
                dve.wait_ge(max_made, 5 * b + 5)
                for p in range(HP):
                    dve.tensor_tensor(E[:, 2 * p:2 * p + 2], ps[p][:].rearrange("p (h m) -> p h m", m=NKV),
                                      cols(mx[:, 2 * p:2 * p + 2], NKV), ALU.subtract).then_inc(shifted, 1)
                dve.tensor_tensor(e0[:], ps[7][:, 0:H], mx[:], ALU.subtract).then_inc(shifted, 1)
                dve.wait_ge(exp_made, 2 * b + 2)
                dve.tensor_reduce(sm[:], E[:], AX_X, ALU.add).then_inc(sum_made, 1)
                dve.wait_ge(sum_made, 3 * b + 1)
                dve.tensor_tensor(sm[:], sm[:], e0[:], ALU.add).then_inc(sum_made, 1)
                dve.wait_ge(sum_made, 3 * b + 2)
                dve.reciprocal(rc[:], sm[:]).then_inc(sum_made, 1)
                dve.wait_ge(sum_made, 3 * b + 3)
                dve.tensor_tensor(e0[:], e0[:], rc[:], ALU.mult).then_inc(probs_made, 1)
                for g in range(4):
                    at = slice(2 * g, 2 * g + 2)
                    dve.tensor_tensor(E[:, at], E[:, at], cols(rc[:, at], NKV), ALU.mult).then_inc(probs_made, 1)
                dve.wait_ge(pv_done, b + 1)
                dve.tensor_copy(OT[:], ps[0][:]).then_inc(oT_made, 1)
                dve.wait_ge(projected, b + 1)
                dve.wait_ge(z_gathered, 16 * B)
                dve.scalar_tensor_tensor(flat(out_rows[:, bass.ds(b, 1)]), ps[1][:, 0:C], tg[:, 1:2],
                                         flat(Z[:, bass.ds(b, 1)]), ALU.mult, ALU.add).then_inc(rows_made, 1)

        @block.tensor
        def _(pe):
            pe.wait_ge(w_loaded, 16 * 5)
            pe.wait_ge(null_loaded, 16 * H)
            pe.wait_ge(null_placed, 2)
            with pe.Fori(0, B) as b:
                pe.wait_ge(xn_made, 3 * b + 3)
                for c in range(CC):
                    for j in range(3):
                        ins = pe.transpose(ps[c][:, P * j:P * (j + 1)], xn[:, j, P * c:P * (c + 1)], ident[:])
                    ins.then_inc(x_turned, 1)
                pe.wait_ge(xT_made, 2 * b + 2)
                for m in range(HP):
                    for c in range(CC):
                        ins = pe.matmul(ps[2][:, P * m:P * (m + 1)], Wq[:, c, P * m:P * (m + 1)], xT[:, c, 0:P],
                                        start=(c == 0), stop=(c == CC - 1))
                ins.then_inc(proj, 1)
                for m in range(HP):
                    for c in range(CC):
                        ins = pe.matmul(ps[3 + m // 2][:, NKV * (m % 2):NKV * (m % 2 + 1)], Wkv[:, c, P * m:P * (m + 1)],
                                        xT[:, c, P:3 * P], start=(c == 0), stop=(c == CC - 1))
                    ins.then_inc(proj, 1)
                for j in range(2):
                    for c in range(CC):
                        ins = pe.matmul(ps[5 + j][:], xT[:, c, P * (j + 1):P * (j + 2)], Wkv[:, c, IN:2 * IN],
                                        start=(c == 0), stop=(c == CC - 1))
                    ins.then_inc(proj, 1)
                pe.wait_ge(q_made, b + 1)
                pe.wait_ge(kd_made, 8 * b + 8)
                for p in range(HP):
                    pe.matmul(ps[7][:, 0:H], QT[:, p], NK[:, H * p:H * (p + 1)], start=(p == 0), stop=(p == HP - 1))
                for p in range(HP):
                    ins = pe.matmul(ps[p][:], QT[:, p], KD[:, p].rearrange("p h n -> p (h n)"), start=True, stop=True)
                ins.then_inc(scored, 1)
                pe.wait_ge(v_made, 2 * b + 2)
                pe.wait_ge(probs_made, 5 * b + 1)
                pe.transpose(ps[7][0:H, P:2 * P], e0[:], ident[:]).then_inc(p_turned, 1)
                for g in range(4):
                    pe.wait_ge(probs_made, 5 * b + 2 + g)
                    if g == 3:
                        pe.wait_ge(pT_made, 5 * b + 2)
                    for q in range(4):
                        hh, kc = 2 * g + q // 2, q % 2
                        ins = pe.transpose(ps[4 + g % 3][:, P * q:P * (q + 1)], E[:, hh, P * kc:P * (kc + 1)], ident[:])
                    ins.then_inc(p_turned, 1)
                pe.wait_ge(pT_made, 5 * b + 5)
                for p in range(HP):
                    for kc in range(3):
                        for j in range(2):
                            hh = 2 * p + j
                            dst = ps[0][DH * j:DH * (j + 1), P * p:P * (p + 1)]
                            if kc < 2:
                                ins = pe.matmul(dst, V[:, kc, DH * hh:DH * (hh + 1)], pT[:, hh, kc], start=(kc == 0), stop=False)
                            else:
                                ins = pe.matmul(dst, NV[:, DH * hh:DH * (hh + 1)], p0T[:], start=False, stop=True)
                ins.then_inc(pv_done, 1)
                pe.wait_ge(oT_made, b + 1)
                for p in range(HP):
                    ins = pe.matmul(ps[1][:, 0:C], OT[:, P * p:P * (p + 1)], Wo[:, p], start=(p == 0), stop=(p == HP - 1))
                ins.then_inc(projected, 1)


def build_program(nc, d):
    with ExitStack() as stack:
        s = Space(nc, stack, "all")
        k = {"XR": s.sb("XR", [P, NT, C]), "ident": s.sb("ident", [P, P]), "MV": s.sb("MV", [P, NT, 2]),
             "RS": s.sb("RS", [P, NT]), "tg": s.sb("tg", [P, 2]), "sraw": s.sb("sraw", [P, 2, NT]),
             "IDX": s.sb("IDX", [P, 3 * B], I32)}
        ps = [stack.enter_context(nc.psum_tensor(f"ps{i}", [P, 512], F32)) for i in range(8)]
        for name in ("x1_rows", "z_rows"):
            d[name] = nc.dram_tensor(name, (B * N, C), F32, kind="Internal").ap()
        cross_attention(nc, k, ps, d)
        if d.get("debug") == "x1":
            o = s.sem("dbg")
            with nc.Block() as block:
                @block.sync
                def _(sp):
                    sp.dma_start(d["out"].rearrange("(t p) c -> p t c", p=P), k["XR"][:]).then_inc(o, 16)
                    sp.wait_ge(o, 16)
            return
        d["s_rows"] = nc.dram_tensor("s_rows", (2 * NT, P), F32, kind="Internal").ap()
        routing(nc, k, ps, d)
        if d.get("debug") == "idx":
            o = s.sem("dbg")
            with nc.Block() as block:
                @block.sync
                def _(sp):
                    sp.dma_start(d["out"][0:P, 0:12], k["IDX"][:].bitcast(F32)).then_inc(o, 16)
                    sp.wait_ge(o, 16)
            return
        windowed_attention(nc, k, ps, d)
        if d.get("debug") == "light":
            return
        chosen_attention(nc, k, ps, d)


DEBUG = ""


def kernel(x, ctx_768, g_xattn, g_ffn, L0_xattn_Wq, L0_xattn_Wk, L0_xattn_Wv, L0_xattn_Wo, L0_xattn_bo,
           L0_ffn_ln_w, L0_ffn_ln_b, L0_ffn_Wqkv, L0_ffn_Wout_l, L0_ffn_rt_q, L0_ffn_rt_kv, L0_ffn_gamma,
           L0_ffn_Wq, L0_ffn_Wkv, L0_ffn_Wout_h, L0_ffn_null_kv, L0_ffn_null_q):
    import numpy as np
    import concourse.bacc as bacc
    from concourse.bass_utils import run_bass_kernel_spmd

    def lay(a):
        return np.ascontiguousarray(a)

    def by_row(a):
        return lay(np.reshape(a, (CC, P)).T)

    ks = [NQ] * B + [NKV] * B
    arrays = {
        "x": lay(np.reshape(x, (B * N, C))),
        "ctxT": lay(np.reshape(ctx_768, (B * M, XC)).T),
        "g_xattn": lay(g_xattn), "g_ffn": lay(g_ffn),
        "xWqT": lay(np.transpose(L0_xattn_Wq)), "xWk": lay(L0_xattn_Wk), "xWv": lay(L0_xattn_Wv),
        "xWo": lay(L0_xattn_Wo), "xbo": lay(L0_xattn_bo),
        "ln_w": by_row(L0_ffn_ln_w), "ln_b": by_row(L0_ffn_ln_b),
        "WqkvT": lay(np.transpose(L0_ffn_Wqkv)), "WoutlT": lay(np.transpose(L0_ffn_Wout_l)),
        "rt_q": lay(L0_ffn_rt_q), "rt_kv": lay(L0_ffn_rt_kv), "gamma": by_row(L0_ffn_gamma),
        "hWqT": lay(np.transpose(L0_ffn_Wq)),
        "hWkvT": lay(np.reshape(L0_ffn_Wkv, (H, 2, DH, C)).transpose(3, 1, 0, 2).reshape(C, 2 * IN)),
        "hWoutT": lay(np.transpose(L0_ffn_Wout_h)),
        "null_k": lay(np.reshape(L0_ffn_null_kv[0], (HP, P)).T), "null_v": lay(L0_ffn_null_kv[1]), "null_q": lay(L0_ffn_null_q),
        "rows8": np.array([[log(N) - log(q * FETCH), 1.0 / (q * FETCH), q, 0.0] for q in ks], np.float32),
        "bits8": np.array([[1 << i for i in range(30, -1, -1)] + [0]] * (2 * B), np.int32),
        "edge": np.array([[NEG * (p < W), NEG * (p >= W)] for p in range(P)], np.float32),
    }
    nc = bacc.Bacc("TRN2", target_bir_lowering=False, num_devices=1)
    d = {n: nc.dram_tensor(n, a.shape, mybir.dt.from_np(a.dtype), kind="ExternalInput").ap() for n, a in arrays.items()}
    d["out"] = nc.dram_tensor("out", (B * N, C), F32, kind="ExternalOutput").ap()
    if DEBUG:
        d["debug"] = DEBUG
    build_program(nc, d)
    r = run_bass_kernel_spmd(nc, [arrays], core_ids=[0])
    return r.results[0]["out"].reshape(B, N, C)
```

```python
from contextlib import ExitStack
from math import log

import concourse.bass as bass
from concourse import mybir

F32 = mybir.dt.float32
F32R = mybir.dt.float32r
F16 = mybir.dt.float16
I32 = mybir.dt.int32
U32 = mybir.dt.uint32
ACT = mybir.ActivationFunctionType
ALU = mybir.AluOpType
AX_X = mybir.AxisListType.X

P = 128
B, N, C = 4, 1024, 256
CC = C // P
TB = N // P
NT = B * TB
EPS = 1e-5

XH, XD, M, XC = 16, 64, 77, 192
XI = XH * XD
XP = XH // 2
XKC = XC // 2
S1 = XH * M
KT = -(-S1 // P)
S1P = KT * P
PW = 2 * M
VW = P - 1 + PW + P - 1
SCOLS = [(0, 6 * M), (6 * M, 12 * M), (12 * M, 16 * M)]
GPAIRS = [(0, 3), (3, 6), (6, 8)]
GN = CC * len(GPAIRS)
UN = KT // 2
GU = GN + UN

H, DH, W = 8, 64, 64
HP = H // 2
IN = H * DH
SCALE = DH ** -0.5
NQ, NKV = 128, 256
FETCH = 9.0 / 8.0
UPD = 3 * TB // 2
ROUTED = 2
CAP = 80.0
R = 2 * B
SEG = N * R // P
NEG = -1e9
SMALLEST = 87.33655


def flat(ap):
    return ap.rearrange("p a b -> p (a b)")


def cols(ap, m):
    return ap.rearrange("p (h o) -> p h o", o=1).to_broadcast([ap.shape[0], ap.shape[1], m])


class Space:

    def __init__(self, nc, stack, phase):
        self.nc, self.stack, self.phase = nc, stack, phase

    def sb(self, name, shape, dt=F32):
        return self.stack.enter_context(self.nc.sbuf_tensor(f"{self.phase}_{name}", shape, dt))

    def sem(self, name):
        return self.stack.enter_context(self.nc.semaphore(f"{self.phase}_{name}"))


def cross_attention(nc, k, ps, d):
    XR, MV, RS, ident, tg, sraw = k["XR"], k["MV"], k["RS"], k["ident"], k["tg"], k["sraw"]
    with ExitStack() as stack:
        s = Space(nc, stack, "cross")
        KBD = s.sb("KBD", [P, B, XP, PW])
        vT = s.sb("vT", [P, XP, B, M])
        VBD = s.sb("VBD", [P, XP, VW])
        WqT = s.sb("WqT", [P, XP, C])
        Wo = s.sb("Wo", [P, XP, C])
        Ghi, Glo = s.sb("Ghi", [P, CC, S1], F32R), s.sb("Glo", [P, CC, S1], F32R)
        Uhi, Ulo = s.sb("Uhi", [P, KT, C], F32R), s.sb("Ulo", [P, KT, C], F32R)
        probs = s.sb("probs", [P, 4, S1P])
        pThi, pTlo = s.sb("pThi", [P, S1P], F32R), s.sb("pTlo", [P, S1P], F32R)
        h = s.sb("h", [P, 2, C])
        hThi, hTlo = s.sb("hThi", [P, 2, C], F32R), s.sb("hTlo", [P, 2, C], F32R)
        mx, sm, rc = s.sb("mx", [P, 2, XH]), s.sb("sm", [P, 2, XH]), s.sb("rc", [P, 2, XH])
        Wkv = s.sb("Wkv", [XKC, 2, 2, XI])
        ctx = s.sb("ctx", [XKC, 2, B * M])
        RT = s.sb("RT", [P, 2, C])
        junk = s.sb("junk", [P, 2, 2, C])
        bo = s.sb("bo", [P, C])
        bst = s.sb("bst", [P, 2, 6])
        x1b, mvb = s.sb("x1b", [P, 2, C]), s.sb("mvb", [P, TB, 2])
        sb8 = s.sb("sb8", [P, 2, TB])
        LA, LB, LC = s.sb("LA", [P, NT]), s.sb("LB", [P, NT]), s.sb("LC", [P, NT])
        banks_s, banks_p, bank_h, bank_o = ps[0:3], ps[3:6], ps[6], ps[7]

        w_loaded, x_loaded, c_loaded, x1_stored = (s.sem(n) for n in (
            "w_loaded", "x_loaded", "c_loaded", "x1_stored"))
        pool_once, vec_once, act_once = s.sem("pool_once"), s.sem("vec_once"), s.sem("act_once")
        kv_mult, kv_evac = s.sem("kv_mult"), s.sem("kv_evac")
        gu_mult, gu_hi, gu_lo, vbd_made = s.sem("gu_mult"), s.sem("gu_hi"), s.sem("gu_lo"), s.sem("vbd_made")
        h_made, h_turned, hhi_made, hlo_made = s.sem("h_made"), s.sem("h_turned"), s.sem("hhi_made"), s.sem("hlo_made")
        scored, max_made, shifted, exp_made = s.sem("scored"), s.sem("max_made"), s.sem("shifted"), s.sem("exp_made")
        sum_made, recip_made, probs_made = s.sem("sum_made"), s.sem("recip_made"), s.sem("probs_made")
        p_turned, phi_made, plo_made = s.sem("p_turned"), s.sem("phi_made"), s.sem("plo_made")
        pv_done, bias_added, x1_made = s.sem("pv_done"), s.sem("bias_added"), s.sem("x1_made")
        stats_made, mv_made, routed = s.sem("stats_made"), s.sem("mv_made"), s.sem("routed")
        x1_kept, mv_kept, spaced = s.sem("x1_kept"), s.sem("mv_kept"), s.sem("spaced")

        def gu_group(n):
            bank = ps[n % 4]
            if n < GN:
                c, (p0, p1) = n // len(GPAIRS), GPAIRS[n % len(GPAIRS)]
                at = slice(PW * p0, PW * p1)
                return bank[:, 0:PW * (p1 - p0)], Ghi[:, c, at], Glo[:, c, at]
            t = 2 * (n - GN)
            return bank[:, 0:2 * C], flat(Uhi[:, t:t + 2]), flat(Ulo[:, t:t + 2])

        block = stack.enter_context(nc.Block())

        @block.sync
        def _(sp):
            sp.dma_start(ctx[:], d["ctxT"].rearrange("(k p) n -> p k n", p=XKC)).then_inc(w_loaded, 16)
            sp.dma_start(Wkv[:, 0], d["xWk"].rearrange("(k p) n -> p k n", p=XKC)).then_inc(w_loaded, 16)
            sp.dma_start(Wkv[:, 1], d["xWv"].rearrange("(k p) n -> p k n", p=XKC)).then_inc(w_loaded, 16)
            xv = d["x"].rearrange("(t p) c -> p t c", p=P)
            for q in range(B):
                sp.dma_start(XR[:, q * TB:(q + 1) * TB], xv[:, q * TB:(q + 1) * TB]).then_inc(x_loaded, 16)
            sp.dma_start(WqT[:], d["xWqT"].rearrange("(k p) n -> p k n", p=P)).then_inc(w_loaded, 16)
            sp.dma_start(Wo[:], d["xWo"].rearrange("(k p) n -> p k n", p=P)).then_inc(w_loaded, 16)
            x1v = d["x1_rows"].rearrange("(t p) c -> p t c", p=P)
            with sp.Fori(0, NT) as i:
                sp.wait_ge(x1_kept, i + 1)
                sp.dma_start(x1v[:, bass.ds(i, 1)], XR[:, bass.ds(i, 1)]).then_inc(x1_stored, 16)
            sp.wait_ge(x1_stored, 16 * NT)

        @block.gpsimd
        def _(pool):
            pool.memset(ident[:], 0.0).then_inc(pool_once, 1)
            pool.wait_ge(pool_once, 1)
            pool.affine_select(out=ident[:], in_=ident[:], compare_op=ALU.not_equal, fill=1.0, base=0,
                               pattern=[[-1, P]], channel_multiplier=1).then_inc(pool_once, 1)
            pool.memset(KBD[:], 0.0).then_inc(pool_once, 1)
            pool.memset(VBD[:], 0.0).then_inc(pool_once, 1)
            pool.memset(probs[:, :, S1:S1P], 0.0).then_inc(pool_once, 1)
            pool.wait_ge(pool_once, 5)
            pool.wait_ge(act_once, 1)
            pool.tensor_tensor(bo[:], bo[:], tg[:, 0:1].to_broadcast([P, C]), ALU.mult).then_inc(pool_once, 1)
            pool.wait_ge(pool_once, 6)
            with pool.Fori(0, B) as b:
                for t in range(TB):
                    i = b * TB + t
                    if t < TB:
                        pool.wait_ge(h_made, i + 1)
                        xt = flat(XR[:, bass.ds(i, 1)])
                        pool.tensor_tensor(xt, xt, bo[:], ALU.add).then_inc(bias_added, 1)
                        pool.wait_ge(recip_made, i + 1)
                        pr = probs[:, t % 4, 0:S1].rearrange("p (h m) -> p h m", m=M)
                        pool.tensor_tensor(pr, pr, cols(rc[:, t % 2], M), ALU.mult).then_inc(probs_made, 1)

        @block.scalar
        def _(act):
            for src, dst in ((d["g_xattn"].rearrange("(o n) -> o n", o=1).to_broadcast([P, 1]), tg[:, 0:1]),
                             (d["g_ffn"].rearrange("(o n) -> o n", o=1).to_broadcast([P, 1]), tg[:, 1:2]),
                             (d["xbo"].rearrange("(o n) -> o n", o=1).to_broadcast([P, C]), bo[:]),
                             (d["rt_q"].to_broadcast([P, C]), RT[:, 0]),
                             (d["rt_kv"].to_broadcast([P, C]), RT[:, 1])):
                act.dma_start(dst, src).then_inc(c_loaded, 16)
            act.wait_ge(c_loaded, 16 * 5)
            act.activation(tg[:], tg[:], ACT.Tanh).then_inc(act_once, 1)
            act.wait_ge(vec_once, 1)
            act.activation(LB[:], LA[:], ACT.Ln).then_inc(act_once, 1)
            act.wait_ge(act_once, 2)
            act.activation(LC[:], LB[:], ACT.Exp, scale=-0.5).then_inc(act_once, 1)
            act.wait_ge(pool_once, 3)
            for p in range(XP):
                act.wait_ge(kv_mult, 2 * p + 1)
                for j in range(2):
                    rows = slice(XD * j, XD * (j + 1))
                    act.activation(KBD[rows, :, p, M * j:M * (j + 1)],
                                   ps[(2 * p) % 8][rows, 0:B * M].rearrange("p (b m) -> p b m", m=M),
                                   ACT.Copy, scale=XD ** -0.5).then_inc(kv_evac, 1)
                act.wait_ge(kv_mult, 2 * p + 2)
                act.activation(flat(vT[:, p]), ps[(2 * p + 1) % 8][:, 0:B * M], ACT.Copy).then_inc(kv_evac, 1)
            act.wait_ge(kv_evac, 3 * XP)
            act.wait_ge(pool_once, 4)
            with act.Fori(0, B) as b:
                for j in range(2):
                    rows = slice(XD * j, XD * (j + 1))
                    act.activation(VBD[rows, :, P - 1 + M * j:P - 1 + M * (j + 1)],
                                   vT[rows, :, bass.ds(b, 1), :].rearrange("p x o m -> p x (o m)"),
                                   ACT.Copy).then_inc(vbd_made, 1)
                for n in range(GU):
                    src, hi, _ = gu_group(n)
                    act.wait_ge(gu_mult, GU * b + n + 2)
                    act.activation(hi, src, ACT.Copy).then_inc(gu_hi, 1)
                for t in range(-1, TB + 2):
                    if t + 1 < TB:
                        act.wait_ge(h_turned, b * TB + t + 2)
                        act.activation(hThi[:, (t + 1) % 2], bank_h[:, 0:C], ACT.Copy).then_inc(hhi_made, 1)
                    if t >= 2:
                        for j in range(3):
                            w = min(512, S1P - 512 * j)
                            act.wait_ge(p_turned, 3 * (b * TB + t - 2) + j + 1)
                            act.activation(pThi[:, 512 * j:512 * j + w], banks_p[j][:, 0:w], ACT.Copy).then_inc(phi_made, 1)
                    if 0 <= t < TB:
                        act.wait_ge(shifted, b * TB + t + 1)
                        act.activation(probs[:, t % 4, 0:S1], probs[:, t % 4, 0:S1], ACT.Exp).then_inc(exp_made, 1)

        @block.vector
        def _(dve):
            for i in range(NT):
                if i % TB == 0:
                    dve.wait_ge(x_loaded, 16 * B)
                if i >= 2:
                    dve.wait_ge(mv_made, i - 1)
                dve.bn_stats(bst[:, i % 2], XR[:, i]).then_inc(stats_made, 1)
                dve.wait_ge(stats_made, i + 1)
                dve.bn_aggr(MV[:, i], bst[:, i % 2]).then_inc(mv_made, 1)
            dve.wait_ge(mv_made, NT)
            dve.tensor_scalar(LA[:], MV[:, :, 1], EPS, None, ALU.add).then_inc(vec_once, 1)
            dve.wait_ge(act_once, 3)
            dve.wait_ge(vec_once, 1)
            rsqrt_step(dve, RS, LC, LA, LB, vec_once, 1)

            def route_product(u, j):
                dve.scalar_tensor_tensor(junk[:, u % 2, j], x1b[:, u % 2], mvb[:, u, 0:1], RT[:, j],
                                         ALU.subtract, ALU.mult, accum_out=sb8[:, j, u:u + 1]).then_inc(routed, 1)

            with dve.Fori(0, B) as b:
                for n in range(GU):
                    src, hi, lo = gu_group(n)
                    dve.wait_ge(gu_hi, GU * b + n + 1)
                    dve.tensor_tensor(lo, src, hi.bitcast(F32), ALU.subtract).then_inc(gu_lo, 1)
                for t in range(-1, TB + 2):
                    if t + 1 < TB:
                        i = b * TB + t + 1
                        if t >= 1:
                            dve.wait_ge(h_turned, i - 1)
                        dve.tensor_scalar(h[:, (t + 1) % 2], flat(XR[:, bass.ds(i, 1)]),
                                          MV[:, bass.ds(i, 1), 0], RS[:, bass.ds(i, 1)],
                                          ALU.subtract, ALU.mult).then_inc(h_made, 1)
                    if 0 <= t < TB:
                        dve.wait_ge(scored, b * TB + t + 1)
                        for j, (c0, c1) in enumerate(SCOLS):
                            dve.tensor_reduce(mx[:, t % 2, c0 // M:c1 // M],
                                              banks_s[j][:, 0:c1 - c0].rearrange("p (h m) -> p h m", m=M),
                                              AX_X, ALU.max).then_inc(max_made, 1)
                    if t + 1 < TB:
                        dve.wait_ge(hhi_made, b * TB + t + 2)
                        dve.tensor_tensor(hTlo[:, (t + 1) % 2], bank_h[:, 0:C], hThi[:, (t + 1) % 2].bitcast(F32),
                                          ALU.subtract).then_inc(hlo_made, 1)
                    if t >= 2:
                        for j in range(3):
                            w = min(512, S1P - 512 * j)
                            at = slice(512 * j, 512 * j + w)
                            dve.wait_ge(phi_made, 3 * (b * TB + t - 2) + j + 1)
                            dve.tensor_tensor(pTlo[:, at], banks_p[j][:, 0:w], pThi[:, at].bitcast(F32),
                                              ALU.subtract).then_inc(plo_made, 1)
                    if 0 <= t < TB:
                        dve.wait_ge(max_made, 3 * (b * TB + t + 1))
                        for j, (c0, c1) in enumerate(SCOLS):
                            ins = dve.tensor_tensor(probs[:, t % 4, c0:c1].rearrange("p (h m) -> p h m", m=M),
                                                    banks_s[j][:, 0:c1 - c0].rearrange("p (h m) -> p h m", m=M),
                                                    cols(mx[:, t % 2, c0 // M:c1 // M], M), ALU.subtract)
                        ins.then_inc(shifted, 1)
                        dve.wait_ge(exp_made, b * TB + t + 1)
                        dve.tensor_reduce(sm[:, t % 2], probs[:, t % 4, 0:S1].rearrange("p (h m) -> p h m", m=M),
                                          AX_X, ALU.add).then_inc(sum_made, 1)
                        dve.wait_ge(sum_made, b * TB + t + 1)
                        dve.reciprocal(rc[:, t % 2], sm[:, t % 2]).then_inc(recip_made, 1)
                    if t >= 2:
                        i = b * TB + t - 2
                        u = t - 2
                        xt = flat(XR[:, bass.ds(i, 1)])
                        dve.wait_ge(pv_done, i + 1)
                        dve.wait_ge(bias_added, i + 1)
                        dve.scalar_tensor_tensor(x1b[:, u % 2], bank_o[:, 0:C], tg[:, 0:1], xt, ALU.mult, ALU.add).then_inc(x1_made, 1)
                        dve.scalar_tensor_tensor(xt, bank_o[:, 0:C], tg[:, 0:1], xt, ALU.mult, ALU.add).then_inc(x1_kept, 1)
                        dve.wait_ge(x1_made, i + 1)
                        dve.bn_stats(bst[:, u % 2], x1b[:, u % 2]).then_inc(stats_made, 1)
                        dve.wait_ge(stats_made, i + NT + 1)
                        if u >= 1:
                            dve.wait_ge(mv_made, i + NT)
                            route_product(u - 1, 0)
                        else:
                            dve.tensor_scalar(junk[:, 0, 0, 0:1], tg[:, 0:1], 0.0, None, ALU.mult).then_inc(spaced, 1)
                        dve.bn_aggr(mvb[:, u], bst[:, u % 2]).then_inc(mv_made, 1)
                        if u >= 1:
                            route_product(u - 1, 1)
                dve.wait_ge(mv_made, NT + TB * (b + 1))
                for j in range(2):
                    route_product(TB - 1, j)
                dve.tensor_scalar(MV[:, bass.ds(b * TB, TB)], mvb[:], 0.0, None, ALU.add).then_inc(mv_kept, 1)
                dve.wait_ge(routed, 2 * TB * (b + 1))
                for j in range(2):
                    dve.tensor_scalar(sraw[:, j, bass.ds(b * TB, TB)], sb8[:, j], 0.0, None, ALU.add).then_inc(mv_kept, 1)
                dve.wait_ge(mv_kept, 3 * (b + 1))

        @block.tensor
        def _(pe):
            pe.wait_ge(w_loaded, 16 * 5)
            for p in range(XP):
                for v in range(2):
                    n = 2 * p + v
                    if n >= 8:
                        pe.wait_ge(kv_evac, 3 * (n // 2 - 4) + (2 if v == 0 else 3))
                    for kc in range(2):
                        ins = pe.matmul(ps[n % 8][:, 0:B * M], Wkv[:, v, kc, P * p:P * (p + 1)], ctx[:, kc],
                                        start=(kc == 0), stop=(kc == 1))
                    ins.then_inc(kv_mult, 1)
            pe.wait_ge(kv_evac, 3 * XP)
            pe.wait_ge(pool_once, 5)
            pe.matmul(bank_o[0:1, 0:1], ident[:, 0:1], ident[:, 0:1], start=True, stop=True).then_inc(gu_mult, 1)
            with pe.Fori(0, B) as b:
                for n in range(GU):
                    bank, _, _ = gu_group(n)
                    if n >= 4:
                        pe.wait_ge(gu_lo, GU * b + n - 3)
                    if n < GN:
                        c, (p0, p1) = n // len(GPAIRS), GPAIRS[n % len(GPAIRS)]
                        for p in range(p0, p1):
                            ins = pe.matmul(bank[:, PW * (p - p0):PW * (p - p0 + 1)], WqT[:, p, P * c:P * (c + 1)],
                                            KBD[:, bass.ds(b, 1), p, :].rearrange("p o m -> p (o m)"),
                                            start=True, stop=True)
                    else:
                        if n == GN:
                            pe.wait_ge(vbd_made, 2 * (b + 1))
                        for j in range(2):
                            t = 2 * (n - GN) + j
                            over = [p for p in range(XP) if PW * p < P * (t + 1) and PW * (p + 1) > P * t]
                            for p in over:
                                at = P - 1 + P * t - PW * p
                                ins = pe.matmul(bank[:, C * j:C * (j + 1)], VBD[:, p, at:at + P], Wo[:, p],
                                                start=(p == over[0]), stop=(p == over[-1]))
                    ins.then_inc(gu_mult, 1)
                for t in range(-1, TB + 2):
                    if 0 <= t < TB:
                        pe.wait_ge(hlo_made, b * TB + t + 1)
                        if t == 0:
                            pe.wait_ge(gu_lo, GU * (b + 1))
                        else:
                            pe.wait_ge(shifted, b * TB + t)
                        passes = [(hh, g, c) for hh, g in ((hThi, Ghi), (hThi, Glo), (hTlo, Ghi)) for c in range(CC)]
                        for n, (hh, g, c) in enumerate(passes):
                            for j, (c0, c1) in enumerate(SCOLS):
                                ins = pe.matmul(banks_s[j][:, 0:c1 - c0], hh[:, t % 2, P * c:P * (c + 1)],
                                                g[:, c, c0:c1], start=(n == 0), stop=(n == len(passes) - 1))
                        ins.then_inc(scored, 1)
                    if t + 1 < TB:
                        pe.wait_ge(h_made, b * TB + t + 2)
                        if t == -1:
                            pe.wait_ge(pool_once, 2)
                        for c in range(CC):
                            ins = pe.transpose(bank_h[:, P * c:P * (c + 1)], h[:, (t + 1) % 2, P * c:P * (c + 1)], ident[:])
                        ins.then_inc(h_turned, 1)
                    if t >= 2:
                        u = t - 2
                        i = b * TB + u
                        pe.wait_ge(probs_made, i + 1)
                        for q in range(KT):
                            ins = pe.transpose(banks_p[q // 4][:, P * (q % 4):P * (q % 4 + 1)],
                                               probs[:, u % 4, P * q:P * (q + 1)], ident[:])
                            if q % 4 == 3 or q == KT - 1:
                                ins.then_inc(p_turned, 1)
                        if u >= 1:
                            pe.wait_ge(x1_made, i)
                        for q in range(KT):
                            if q % 4 == 0:
                                pe.wait_ge(plo_made, 3 * i + q // 4 + 1)
                            for n, (pt, uu) in enumerate(((pThi, Uhi), (pThi, Ulo), (pTlo, Uhi))):
                                ins = pe.matmul(bank_o[:, 0:C], pt[:, P * q:P * (q + 1)], uu[:, q],
                                                start=(q == 0 and n == 0), stop=(q == KT - 1 and n == 2))
                        ins.then_inc(pv_done, 1)


def rsqrt_step(dve, out, r, a, tmp, sem, n):
    dve.tensor_tensor(tmp[:], r[:], r[:], ALU.mult).then_inc(sem, 1)
    dve.wait_ge(sem, n + 1)
    dve.tensor_tensor(tmp[:], tmp[:], a[:], ALU.mult).then_inc(sem, 1)
    dve.wait_ge(sem, n + 2)
    dve.tensor_scalar(tmp[:], tmp[:], -0.5, 1.5, ALU.mult, ALU.add).then_inc(sem, 1)
    dve.wait_ge(sem, n + 3)
    dve.tensor_tensor(out[:], r[:], tmp[:], ALU.mult).then_inc(sem, 1)
    dve.wait_ge(sem, n + 4)


def update_slot(b, t, n):
    return (b * TB + t) * 3 + n


def windowed_attention(nc, k, ps, d):
    XR, MV, ident, tg, sraw, IDX, X = k["XR"], k["MV"], k["ident"], k["tg"], k["sraw"], k["IDX"], k["X"]
    with ExitStack() as stack:
        s = Space(nc, stack, "window")
        Whi, Wlo = s.sb("Whi", [P, CC, 3 * IN], F32R), s.sb("Wlo", [P, CC, 3 * IN], F32R)
        QT = s.sb("QT", [P, HP, N])
        KD = s.sb("KD", [P, HP, 2, N])
        V = s.sb("V", [P, TB, IN])
        VX = s.sb("VX", [P, TB, IN])
        WoT = s.sb("WoT", [P, HP, C])
        y = s.sb("y", [P, 2, C])
        yT = s.sb("yT", [P, 2, CC, P])
        OT = s.sb("OT", [P, HP * P])
        outb = s.sb("outb", [P, 2, C])
        null = s.sb("null", [P, C])
        RR, LA, LB, LC = (s.sb(n, [P, 2, NT]) for n in ("RR", "wLA", "wLB", "wLC"))
        RS, R2 = RR[:, 0], RR[:, 1]
        wb = s.sb("wb", [P, 2, CC])
        edge = s.sb("edge", [P, 2])
        mx, sm, rc = s.sb("wmx", [P, 2, H]), s.sb("wsm", [P, 2, H]), s.sb("wrc", [P, 2, H])
        mxe = s.sb("wmxe", [P, H])
        S, D, Wt, J, V_key, LT, EQ, Z = (s.sb(f"r{n}", [P, SEG]) for n in ("S", "D", "Wt", "J", "V", "LT", "EQ", "Z"))
        SM = s.sb("SM", [P, R * TB, 2])
        blocks = s.sb("blocks", [P, 3, P])
        fold = s.sb("fold", [P, SEG])
        rows = s.sb("rows", [P, 4])
        bits = s.sb("bits", [P, 16, 4], I32)
        smax, T, base, one, lnc, need, part, own_max, prefix = (s.sb(n, [P, 1]) for n in (
            "smax", "T", "base", "one", "lnc", "need", "part", "own_max", "prefix"))
        below = s.sb("below", [P, 3, SEG])
        part4, cand, kept = s.sb("part4", [P, 4]), s.sb("cand", [P, 4], I32), s.sb("kept", [P, 4])
        maxes = s.sb("maxes", [1, 2 * P])
        posT, late = s.sb("posT", [P, R, TB]), s.sb("late", [P, R, TB])
        ranks, token = s.sb("ranks", [P, P]), s.sb("token", [P, TB])
        tk = s.sb("tk", [P, R, TB, 2], F16)
        k1, kk = rows[:, 0:1], rows[:, 1:2]
        inv_k, same, prior = blocks[:, 0], blocks[:, 1], blocks[:, 2]
        total = ps[7][:, C:C + 4]
        counts, found_ps, ranks_ps = ps[4][:, 0:4], ps[4][:, 16:16 + 2 * R], ps[5][:, 0:R * TB]
        r_loaded, turned, renewed, r_exp, parted, summed, ln_made = (s.sem(n) for n in (
            "r_loaded", "r_turned", "r_renewed", "r_exp", "r_parted", "r_summed", "r_ln"))
        bit_step, compared, counted, picked, hot_made, found, idx_made, x_gathered = (s.sem(n) for n in (
            "r_bit", "r_compared", "r_counted", "r_picked", "r_hot", "r_found", "r_idx", "x_gathered"))

        with ExitStack() as early:
            Wst = Space(nc, early, "window").sb("Wst", [P, CC, 3 * IN])
        with ExitStack() as early:
            ysplit = Space(nc, early, "window").sb("ysplit", [P, 2, 2, CC, 4 * P], F32R)
        probs = s.sb("wprobs", [P, 2, H, 2 * P])
        E = s.sb("E", [P, 2, H, 3 * W])
        with ExitStack() as early:
            hot = Space(nc, early, "window").sb("hot", [P, 2, TB, P], F16)
        pT = s.sb("wpT", [P, H, 2, P])
        banks_s, bank_e, banks_p, bank_v, bank_o = ps[0:2], ps[2], ps[3:6], ps[6], ps[7]

        loaded, w_loaded, once, split = s.sem("w_loaded2"), s.sem("w_loaded3"), s.sem("w_once"), s.sem("w_split")
        pool_once, z_stored, cleared = s.sem("w_pool"), s.sem("z_stored"), s.sem("w_cleared")
        out_stored = [s.sem("out_stored_0"), s.sem("out_stored_1")]
        y_made, y_turned, yT_made, yhi_made, ylo_made = (s.sem(n) for n in (
            "y_made", "y_turned", "yT_made", "yhi_made", "ylo_made"))
        qkv_mult, qkv_evac, vx_made = s.sem("qkv_mult"), s.sem("qkv_evac"), s.sem("vx_made")
        scored, max_made, max_joined, shifted, exp_made = (s.sem(n) for n in (
            "w_scored", "w_max", "w_max_joined", "w_shifted", "w_exp"))
        sum_made, recip_made, probs_made = s.sem("w_sum"), s.sem("w_recip"), s.sem("w_probs")
        p_turned, pT_made, pv_done, oT_made = s.sem("w_p_turned"), s.sem("w_pT"), s.sem("w_pv"), s.sem("w_oT")
        projected, z_made, out_made = s.sem("w_projected"), s.sem("z_made"), s.sem("out_made")
        HB = TB // 2
        GROUPS = [(half, kind, m) for half in range(2) for kind in "qkv" for m in range(4)]
        NG, GH = len(GROUPS), len(GROUPS) // 2
        NEV = NG + 2 * HP
        NVX = 2 * TB - 2
        block = stack.enter_context(nc.Block())

        def evacs(n):
            return sum(2 if kind == "k" else 1 for _, kind, _ in GROUPS[:n + 1])

        def group_bank(n):
            return ps[n % 4] if n < GH else ps[3 + n % 4]

        def fills(t):
            return range(GH + t * GH // 2, GH + (t + 1) * GH // 2)

        @block.sync
        def _(sp):
            sp.dma_start(rows[:], d["rows128"]).then_inc(r_loaded, 16)
            sp.dma_start(bits[:], d["bits128"]).then_inc(r_loaded, 16)
            sp.dma_start(blocks[:], d["blocks"]).then_inc(r_loaded, 16)
            sp.dma_start(fold[:], d["fold"]).then_inc(r_loaded, 16)
            sp.dma_start(Wst[:], d["WqkvT"].rearrange("(k p) n -> p k n", p=P)).then_inc(w_loaded, 16)
            sp.dma_start(WoT[:], d["WoutlT"].rearrange("(k p) n -> p k n", p=P)).then_inc(w_loaded, 16)
            for j in range(2):
                sp.dma_start(outb[:, j], d["x"][0:P, :]).then_inc(out_stored[j], 16)
            zv = d["z_rows"].rearrange("(t p) c -> p t c", p=P)
            ov = d["out"].rearrange("(t p) c -> p t c", p=P)
            with sp.Fori(0, NT // 2) as i:
                for j in range(2):
                    sp.wait_ge(z_made, 2 * i + j + 1)
                    sp.dma_start(zv[:, bass.ds(2 * i + j, 1)], XR[:, bass.ds(2 * i + j, 1)]).then_inc(z_stored, 16)
                    sp.wait_ge(out_made, 2 * i + j + 1)
                    sp.dma_start(ov[:, bass.ds(2 * i + j, 1)], outb[:, j]).then_inc(out_stored[j], 16)
            sp.wait_ge(z_stored, 16 * NT)
            for j in range(2):
                sp.wait_ge(out_stored[j], 16 * (NT // 2 + 1))

        @block.gpsimd
        def _(pool):
            pool.memset(SM[:], 0.0).then_inc(pool_once, 1)
            pool.memset(Z[:], 0.0).then_inc(pool_once, 1)
            pool.memset(one[:], 1.0).then_inc(pool_once, 1)
            pool.memset(part4[:], 0.0).then_inc(pool_once, 1)
            pool.iota(ranks[:], pattern=[[1, P]], base=1, channel_multiplier=0,
                      allow_small_or_imprecise_dtypes=True).then_inc(pool_once, 1)
            pool.iota(token[:], pattern=[[P, TB]], base=0, channel_multiplier=1,
                      allow_small_or_imprecise_dtypes=True).then_inc(pool_once, 1)
            pool.memset(KD[:], 0.0).then_inc(pool_once, 1)
            pool.memset(VX[:], 0.0).then_inc(pool_once, 1)
            pool.wait_ge(loaded, 16 * 4)
            pool.tensor_tensor(null[:], null[:], tg[:, 1:2].to_broadcast([P, C]), ALU.mult).then_inc(pool_once, 1)
            pool.wait_ge(pool_once, 9)

            def gather(g):
                if g == 0:
                    pool.wait_ge(idx_made, 1)
                pool.indirect_dma_start(X[:, g], None, d["x1_rows"],
                                        bass.IndirectOffsetOnAxis(ap=IDX[:, g:g + 1].bitcast(U32), axis=0)).then_inc(x_gathered, 16)

            def spread_values(b, half):
                for m in range(HB):
                    t = HB * half + m
                    n = NVX * b + max(2 * t - 1, 0)
                    pool.wait_ge(qkv_evac, NEV * b + evacs(GROUPS.index((half, "v", m))))
                    if t >= 1:
                        pool.wait_ge(vx_made, n)
                        pool.tensor_tensor(VX[0:W, t - 1], V[0:W, t], Z[0:W, 0:1].to_broadcast([W, IN]), ALU.add).then_inc(vx_made, 1)
                        n = n + 1
                    if t < TB - 1:
                        if t >= 1:
                            pool.wait_ge(vx_made, n)
                        pool.tensor_tensor(VX[W:P, t + 1], V[W:P, t], Z[W:P, 0:1].to_broadcast([W, IN]), ALU.add).then_inc(vx_made, 1)

            def clear(b, half):
                pool.wait_ge(vx_made, NVX * b + (2 * HB - 1 if half == 0 else NVX))
                pool.wait_ge(qkv_mult, NG * b + GH * (half + 1))
                zero = Z[:].rearrange("p (o n) -> p o n", o=1).to_broadcast([P, H, W])
                pool.tensor_tensor(probs[0:W, half, :, P:P + W], zero[0:W], zero[0:W], ALU.mult).then_inc(cleared, 1)
                pool.wait_ge(cleared, 4 * b + 2 * half + 1)
                pool.tensor_tensor(probs[W:P, half, :, P + W:2 * P], zero[W:P], zero[W:P], ALU.mult).then_inc(cleared, 1)
                pool.wait_ge(cleared, 4 * b + 2 * half + 2)

            def tiles(b, gathers):
                for t in range(TB + 3):
                    if t < 2:
                        spread_values(b, t)
                        clear(b, t)
                    if t < TB:
                        i = b * TB + t
                        pool.wait_ge(recip_made, i + 1)
                        if t >= 2:
                            pool.wait_ge(p_turned, 4 * (i - 1))
                        r = rc[:, t % 2]
                        pool.tensor_tensor(probs[:, t % 2, :, 0:P], E[:, t % 2, :, 0:P], cols(r, P), ALU.mult).then_inc(probs_made, 1)
                        pool.wait_ge(probs_made, 3 * i + 1)
                        pool.tensor_tensor(probs[0:W, t % 2, :, P + W:2 * P], E[0:W, t % 2, :, P:3 * W],
                                           cols(rc[0:W, t % 2], W), ALU.mult).then_inc(probs_made, 1)
                        pool.tensor_tensor(probs[W:P, t % 2, :, P:P + W], E[W:P, t % 2, :, P:3 * W],
                                           cols(rc[W:P, t % 2], W), ALU.mult).then_inc(probs_made, 1)
                        pool.wait_ge(probs_made, 3 * i + 3)
                    if gathers and 0 < t <= 3 * B // 2:
                        for g in (2 * t - 2, 2 * t - 1):
                            gather(g)
                        pool.wait_ge(x_gathered, 32 * t)
                    v = t - 3
                    if v >= 0:
                        i = b * TB + v
                        pool.wait_ge(z_made, i + 1)
                        pool.wait_ge(out_stored[v % 2], 16 * (b * (TB // 2) + v // 2 + 1))
                        pool.tensor_tensor(outb[:, v % 2], flat(XR[:, bass.ds(i, 1)]), null[:], ALU.add).then_inc(out_made, 1)
                        pool.wait_ge(out_made, i + 1)

            with pool.Fori(0, B - 1) as b:
                tiles(b, False)
            tiles(B - 1, True)

        @block.scalar
        def _(act):
            act.dma_start(null[:], d["null_q"].rearrange("(o n) -> o n", o=1).to_broadcast([P, C])).then_inc(loaded, 16)
            act.dma_start(wb[:, 0], d["ln_w"]).then_inc(loaded, 16)
            act.dma_start(wb[:, 1], d["ln_b"]).then_inc(loaded, 16)
            act.dma_start(edge[:], d["edge"]).then_inc(loaded, 16)
            act.wait_ge(once, 3)
            act.activation(LB[:], LA[:], ACT.Ln).then_inc(split, 1)
            act.wait_ge(split, 1)
            act.activation(LC[:], LB[:], ACT.Exp, scale=-0.5).then_inc(split, 1)
            act.wait_ge(turned, 1)
            act.activation(S[:], ps[0][:, 0:SEG], ACT.Copy).then_inc(split, 1)
            act.wait_ge(w_loaded, 32)
            act.activation(flat(Whi[:]), flat(Wst[:]), ACT.Copy).then_inc(split, 1)
            act.wait_ge(pool_once, 8)

            def renew(n):
                act.activation(lnc[:], total[:, 0:1], ACT.Ln).then_inc(ln_made, 1)
                act.wait_ge(renewed, 3 * n)
                act.activation(Wt[:], D[:], ACT.Exp).then_inc(r_exp, 1)

            act.wait_ge(once, 17)
            act.activation(Wt[:], D[:], ACT.Exp).then_inc(r_exp, 1)
            act.wait_ge(summed, 1)
            renew(1)

            def batch_row(b, stage):
                def out_of(n):
                    act.wait_ge(qkv_mult, NG * b + n + 1)
                    bank = group_bank(n)
                    half, kind, m = GROUPS[n]
                    at = slice(512 * half, 512 * half + 512)
                    if kind == "v":
                        act.activation(V[:, HB * half + m], bank[:], ACT.Copy).then_inc(qkv_evac, 1)
                    elif kind == "q":
                        act.activation(QT[:, m, at], bank[:], ACT.Copy, scale=SCALE).then_inc(qkv_evac, 1)
                    else:
                        for j in range(2):
                            rows = slice(DH * j, DH * (j + 1))
                            act.activation(KD[rows, m, j, at], bank[rows, :], ACT.Copy).then_inc(qkv_evac, 1)

                def high(t):
                    act.wait_ge(yT_made, 2 * (b * TB + t) + 2)
                    act.activation(ysplit[:, t // HB, 0, :, P * (t % HB):P * (t % HB + 1)], yT[:, t % 2], ACT.Copy).then_inc(yhi_made, 1)

                for t in range(HB):
                    high(t)
                for n in range(GH):
                    out_of(n)
                    if n >= 2 and n % 2 == 0 and n <= 8:
                        high(HB + n // 2 - 1)
                for t in range(TB + 2):
                    u = t - 2
                    if t < 2:
                        for n in fills(t)[0:HP]:
                            out_of(n)
                    if u >= 0:
                        for g in range(4):
                            n = 4 * u + g
                            act.wait_ge(p_turned, 4 * TB * b + n + 1)
                            act.activation(pT[:, 2 * g:2 * g + 2].rearrange("p h k n -> p (h k n)"), banks_p[n % 3][:],
                                           ACT.Copy).then_inc(pT_made, 1)
                    if t < TB:
                        act.wait_ge(shifted, b * TB + t + 1)
                        act.activation(E[:, t % 2], E[:, t % 2], ACT.Exp).then_inc(exp_made, 1)
                    if t < 2:
                        for n in fills(t)[HP:]:
                            out_of(n)
                    if u >= 0:
                        act.wait_ge(pv_done, b * TB + u + 1)
                        act.activation(OT[:], bank_v[:], ACT.Copy).then_inc(oT_made, 1)
                    if stage == "descend" and t % (TB // 2) == TB // 2 - 1 and t < TB:
                        act.wait_ge(summed, update_slot(b, t, 2) + 2)
                        renew(b * 2 + (t // (TB // 2) + 2))

            with act.Fori(0, ROUTED) as b:
                batch_row(b, "descend")
            with act.Fori(ROUTED, B) as b:
                batch_row(b, "bisect")

        @block.vector
        def _(dve):
            dve.tensor_scalar(LA[:, 1], MV[:, :, 1], EPS, EPS, ALU.add, ALU.mult).then_inc(once, 1)
            dve.tensor_scalar(LA[:, 0], MV[:, :, 1], EPS, None, ALU.add).then_inc(once, 1)
            dve.wait_ge(once, 2)
            dve.tensor_tensor(LA[:, 1], LA[:, 1], MV[:, :, 1], ALU.add).then_inc(once, 1)
            dve.memset(mxe[:], 0.0).then_inc(once, 1)
            dve.wait_ge(split, 2)
            dve.wait_ge(once, 4)
            rsqrt_step(dve, RR, LC, LA, LB, once, 4)
            dve.wait_ge(pool_once, 6)
            for half in range(2):
                at = slice(SEG * half, SEG * (half + 1))
                dve.tensor_tensor(SM[at, :, half].rearrange("p (j i) -> p j i", j=2), sraw[at],
                                  RS[at].rearrange("p (o i) -> p o i", o=1).to_broadcast([SEG, 2, NT]),
                                  ALU.mult).then_inc(once, 1)
            dve.wait_ge(r_loaded, 16 * 4)
            dve.wait_ge(split, 3)
            dve.tensor_reduce(own_max[:], S[:], AX_X, ALU.max).then_inc(once, 1)
            dve.wait_ge(turned, 2)
            dve.tensor_reduce(maxes[:, 0:R], ps[4][0:1, 0:P].rearrange("p (r q) -> p r q", r=R), AX_X, ALU.max).then_inc(once, 1)
            dve.wait_ge(once, 12)
            dve.tensor_copy(maxes[:, P:2 * P].rearrange("p (r q) -> p r q", r=R), cols(maxes[:, 0:R], P // R)).then_inc(once, 1)
            dve.wait_ge(turned, 3)
            dve.tensor_copy(smax[:], ps[4][:, P:P + 1]).then_inc(once, 1)
            dve.tensor_scalar(T[:], k1, 0.0, None, ALU.add).then_inc(once, 1)
            dve.wait_ge(once, 15)
            dve.tensor_tensor(base[:], T[:], smax[:], ALU.min).then_inc(once, 1)
            dve.wait_ge(once, 16)
            dve.tensor_scalar(D[:], S[:], base[:], CAP, ALU.subtract, ALU.min).then_inc(once, 1)
            dve.wait_ge(split, 4)
            dve.tensor_tensor(flat(Wlo[:]), flat(Wst[:]), flat(Whi[:]).bitcast(F32), ALU.subtract).then_inc(once, 1)

            def first_sum(n):
                dve.wait_ge(r_exp, n + 1)
                dve.tensor_scalar(J[:], Wt[:], one[:], None, ALU.min, ALU.add, accum_out=part[:]).then_inc(parted, 1)

            def next_sum(n):
                dve.wait_ge(summed, n + 1)
                dve.tensor_scalar(J[:], Wt[:], total[:, 0:1], None, ALU.min, ALU.add, accum_out=part[:]).then_inc(parted, 1)

            def renew(n):
                dve.wait_ge(ln_made, n)
                dve.tensor_tensor(T[:], base[:], lnc[:], ALU.add).then_inc(renewed, 1)
                dve.wait_ge(renewed, 3 * n - 2)
                dve.tensor_tensor(base[:], T[:], smax[:], ALU.min).then_inc(renewed, 1)
                dve.wait_ge(renewed, 3 * n - 1)
                dve.tensor_scalar(D[:], S[:], base[:], CAP, ALU.subtract, ALU.min).then_inc(renewed, 1)

            first_sum(0)
            renew(1)
            dve.wait_ge(loaded, 16 * 4)
            dve.wait_ge(once, 18)

            def keys():
                dve.tensor_scalar(J[:], S[:], T[:], 0.0, ALU.subtract, ALU.min).then_inc(bit_step, 1)
                dve.wait_ge(bit_step, 1)
                dve.tensor_scalar(V_key[:], J[:], -1.0, SMALLEST, ALU.mult, ALU.min).then_inc(bit_step, 1)
                dve.memset(prefix[:], 0.0).then_inc(bit_step, 1)
                dve.wait_ge(bit_step, 3)

            def compare(n):
                dve.tensor_tensor(cand[:], prefix[:].bitcast(I32).to_broadcast([P, 4]), bits[:, n], ALU.bitwise_or).then_inc(bit_step, 1)
                dve.wait_ge(bit_step, 3 * n + 4)
                for j in range(1, 4):
                    ins = dve.tensor_scalar(below[:, j - 1], V_key[:], cand[:, j:j + 1].bitcast(F32), None, ALU.is_lt, ALU.add, accum_out=part4[:, j:j + 1])
                ins.then_inc(compared, 1)

            def keep(n):
                dve.wait_ge(counted, n + 1)
                dve.scalar_tensor_tensor(kept[:], total[:, 0:4], kk, cand[:].bitcast(F32), ALU.is_lt, ALU.mult).then_inc(bit_step, 1)
                dve.wait_ge(bit_step, 3 * n + 5)
                dve.tensor_reduce(prefix[:], kept[:], AX_X, ALU.max).then_inc(bit_step, 1)
                dve.wait_ge(bit_step, 3 * n + 6)

            def rank():
                kth = prefix[:]
                dve.tensor_scalar(LT[:], V_key[:], kth, None, ALU.is_lt, ALU.add, accum_out=part[:]).then_inc(picked, 1)
                dve.tensor_scalar(EQ[:], V_key[:], kth, None, ALU.is_equal).then_inc(picked, 1)
                dve.wait_ge(picked, 2)
                dve.tensor_tensor_scan(J[:], EQ[:], Z[:], 0.0, ALU.add, ALU.add).then_inc(picked, 1)
                dve.wait_ge(turned, 4)
                dve.tensor_tensor(need[:], kk, counts[:, 0:1], ALU.subtract).then_inc(picked, 1)
                dve.wait_ge(picked, 4)
                dve.tensor_tensor(need[:], need[:], counts[:, 1:2], ALU.subtract).then_inc(picked, 1)
                dve.wait_ge(picked, 5)
                dve.scalar_tensor_tensor(D[:], J[:], need[:], EQ[:], ALU.is_le, ALU.mult).then_inc(picked, 1)
                dve.wait_ge(picked, 6)
                dve.tensor_tensor(LT[:], LT[:], D[:], ALU.add).then_inc(picked, 1)
                dve.wait_ge(picked, 7)
                dve.tensor_tensor_scan(J[:], LT[:], Z[:], 0.0, ALU.add, ALU.add).then_inc(picked, 1)
                dve.wait_ge(picked, 8)
                dve.wait_ge(turned, 5)
                dve.scalar_tensor_tensor(D[:], J[:], counts[:, 2:3], LT[:], ALU.add, ALU.mult).then_inc(picked, 1)

            def name_tokens():
                every = lambda ap: ap[:].rearrange("p r t -> p (r t)")
                dve.wait_ge(turned, 6)
                dve.tensor_scalar(every(late), ranks_ps, float(P), None, ALU.is_gt).then_inc(picked, 1)
                dve.wait_ge(picked, 10)
                dve.scalar_tensor_tensor(every(posT), every(late), -float(P), ranks_ps, ALU.mult, ALU.add).then_inc(picked, 1)
                tokens = token[:].rearrange("p (o t) -> p o t", o=1).to_broadcast([P, R, TB])
                dve.tensor_tensor(late[:], late[:], tokens, ALU.mult).then_inc(picked, 1)
                dve.wait_ge(picked, 12)
                dve.tensor_tensor(tk[:, :, :, 0], tokens, late[:], ALU.subtract).then_inc(picked, 1)
                dve.tensor_scalar(tk[:, :, :, 1], late[:], 0.0, None, ALU.add).then_inc(picked, 1)
                dve.wait_ge(picked, 14)
                for r in range(R):
                    if r >= 2:
                        dve.wait_ge(found, r - 1)
                    dve.tensor_tensor(hot[:, r % 2], cols(posT[:, r], P), ranks[:].rearrange("p (o n) -> p o n", o=1).to_broadcast([P, TB, P]),
                                      ALU.is_equal).then_inc(hot_made, 1)
                dve.wait_ge(found, R)
                for b in range(B):
                    dve.tensor_scalar(IDX[:, 3 * b:3 * b + 1], found_ps[:, 2 * b:2 * b + 1], float(N * b), None, ALU.add)
                    ins = dve.tensor_scalar(IDX[:, 3 * b + 1:3 * b + 3], found_ps[:, 2 * (B + b):2 * (B + b) + 2],
                                            float(N * b), None, ALU.add)
                ins.then_inc(idx_made, 1)

            def batch_row(b, stage):
                def normalise(t):
                    i = b * TB + t
                    dve.tensor_scalar(y[:, t % 2], flat(XR[:, bass.ds(i, 1)]), MV[:, bass.ds(i, 1), 0],
                                      R2[:, bass.ds(i, 1)], ALU.subtract, ALU.mult).then_inc(y_made, 1)

                def low(t):
                    dve.wait_ge(yhi_made, b * TB + t + 1)
                    at = slice(P * (t % HB), P * (t % HB + 1))
                    dve.tensor_tensor(ysplit[:, t // HB, 1, :, at], yT[:, t % 2], ysplit[:, t // HB, 0, :, at].bitcast(F32),
                                      ALU.subtract).then_inc(ylo_made, 1)

                normalise(0)
                normalise(1)
                for t in range(TB):
                    dve.wait_ge(y_turned, b * TB + t + 1)
                    if t >= 2:
                        dve.wait_ge(ylo_made, b * TB + t - 1)
                    for c in range(CC):
                        dve.tensor_scalar(yT[:, t % 2, c], ps[6 + t % 2][:, P * c:P * (c + 1)], wb[:, 0, c:c + 1],
                                          wb[:, 1, c:c + 1], ALU.mult, ALU.add).then_inc(yT_made, 1)
                    if t + 2 < TB:
                        normalise(t + 2)
                    if t % HB:
                        low(t - 1)
                    if t % HB == HB - 1:
                        low(t)
                    if stage == "bisect" and t == HB - 1:
                        keys()
                    if stage == "name" and t == HB - 1:
                        rank()
                if stage == "name":
                    name_tokens()
                for t in range(TB + 3):
                    v = t - 3
                    if stage == "descend" and t < TB:
                        if t % (TB // 2) == 0:
                            first_sum(b * 2 + (t // (TB // 2) + 1))
                        next_sum(update_slot(b, t, 1))
                    if stage == "bisect" and t < TB:
                        compare(2 * t)
                    if t < TB:
                        i = b * TB + t
                        dve.wait_ge(scored, i + 1)
                        own = mx[:, t % 2]
                        for j in range(2):
                            dve.tensor_reduce(own[:, 4 * j:4 * j + 4], banks_s[j][:].rearrange("p (h m) -> p h m", m=P),
                                              AX_X, ALU.max).then_inc(max_made, 1)
                        dve.tensor_reduce(mxe[:], bank_e[:].rearrange("p (h m) -> p h m", m=W), AX_X, ALU.max).then_inc(max_made, 1)
                        dve.wait_ge(max_made, 3 * i + 3)
                        mask = edge[:, 0:1] if t == 0 else edge[:, 1:2] if t == TB - 1 else 0.0
                        dve.scalar_tensor_tensor(own, mxe[:], mask, own, ALU.add, ALU.max).then_inc(max_joined, 1)
                        dve.wait_ge(max_joined, i + 1)
                        if t >= 2:
                            dve.wait_ge(probs_made, 3 * (i - 1))
                        for j in range(2):
                            dve.tensor_tensor(E[:, t % 2, 4 * j:4 * j + 4, 0:P], banks_s[j][:].rearrange("p (h m) -> p h m", m=P),
                                              cols(mx[:, t % 2, 4 * j:4 * j + 4], P), ALU.subtract)
                        dve.scalar_tensor_tensor(E[:, t % 2, :, P:3 * W], bank_e[:].rearrange("p (h m) -> p h m", m=W), mask,
                                                 cols(own, W), ALU.add, ALU.subtract).then_inc(shifted, 1)
                    if v >= 0:
                        i = b * TB + v
                        xt = flat(XR[:, bass.ds(i, 1)])
                        dve.wait_ge(projected, i + 1)
                        dve.scalar_tensor_tensor(xt, bank_o[:, 0:C], tg[:, 1:2], xt, ALU.mult, ALU.add).then_inc(z_made, 1)
                    if stage == "descend" and t < TB:
                        next_sum(update_slot(b, t, 2))
                    if stage == "bisect" and t < TB:
                        keep(2 * t)
                        compare(2 * t + 1)
                    if t < TB:
                        i = b * TB + t
                        dve.wait_ge(exp_made, i + 1)
                        dve.tensor_reduce(sm[:, t % 2], E[:, t % 2], AX_X, ALU.add).then_inc(sum_made, 1)
                        dve.wait_ge(sum_made, i + 1)
                        dve.reciprocal(rc[:, t % 2], sm[:, t % 2]).then_inc(recip_made, 1)
                    if stage == "descend" and t < TB:
                        if t % HB < HB - 1:
                            next_sum(update_slot(b, t, 3))
                        else:
                            renew(b * 2 + (t // HB + 2))
                    if stage == "bisect" and t < TB:
                        keep(2 * t + 1)

            with dve.Fori(0, ROUTED) as b:
                batch_row(b, "descend")
            batch_row(ROUTED, "bisect")
            batch_row(ROUTED + 1, "name")

        @block.tensor
        def _(pe):
            pe.wait_ge(once, 10)
            pe.wait_ge(r_loaded, 16 * 4)
            pe.matmul(ps[0][:, 0:SEG], SM[:].rearrange("p n h -> p (n h)"), fold[:], start=True, stop=True).then_inc(turned, 1)
            pe.wait_ge(once, 11)
            pe.matmul(ps[4][0:1, 0:P], own_max[:], ident[:], start=True, stop=True).then_inc(turned, 1)
            pe.wait_ge(once, 13)
            pe.matmul(ps[4][:, P:P + 1], maxes[:, P:2 * P], one[0:1, :], start=True, stop=True).then_inc(turned, 1)

            def update(n):
                pe.wait_ge(parted, n + 2)
                pe.matmul(total[:, 0:1], inv_k, part[:], start=True, stop=True).then_inc(summed, 1)

            def count(n):
                pe.wait_ge(compared, n + 1)
                pe.matmul(total[:, 0:4], same, part4[:], start=True, stop=True).then_inc(counted, 1)

            update(-1)
            pe.wait_ge(once, 18)

            def batch_row(b, stage):
                def slot(t, n):
                    if n == 2 and t >= 3:
                        pe.wait_ge(z_made, b * TB + t - 2)
                    if stage == "descend":
                        update(update_slot(b, t, n))
                    if stage == "bisect" and n >= 1:
                        count(2 * t + n - 1)

                def turn(t):
                    i = b * TB + t
                    pe.wait_ge(y_made, i + 1)
                    if t >= 2:
                        pe.wait_ge(yT_made, 2 * (i - 1))
                    for c in range(CC):
                        ins = pe.transpose(ps[6 + t % 2][:, P * c:P * (c + 1)], y[:, t % 2, P * c:P * (c + 1)], ident[:])
                    ins.then_inc(y_turned, 1)

                def project(n):
                    if n >= 4:
                        pe.wait_ge(qkv_evac, NEV * b + evacs(max(n - 4, GH - 1) if n >= GH else n - 4))
                    if stage == "name" and n == GH:
                        pe.wait_ge(idx_made, 1)
                    passes = [(a, w, c) for a, w in ((0, Whi), (0, Wlo), (1, Whi)) for c in range(CC)]
                    half, kind, m = GROUPS[n]
                    for q, (a, w, c) in enumerate(passes):
                        if kind == "v":
                            lhs, rhs = ysplit[:, half, a, c, P * m:P * (m + 1)], w[:, c, 2 * IN:3 * IN]
                        else:
                            f = IN * (kind == "k") + P * m
                            lhs, rhs = w[:, c, f:f + P], ysplit[:, half, a, c]
                        ins = pe.matmul(group_bank(n)[:], lhs, rhs, start=(q == 0), stop=(q == len(passes) - 1))
                    ins.then_inc(qkv_mult, 1)
                    if stage == "name" and n == 2:
                        pe.wait_ge(picked, 3)
                        pe.matmul(counts[:, 0:1], same, part[:], start=True, stop=True)
                        pe.matmul(counts[:, 1:2], prior, J[:, SEG - 1:SEG], start=True, stop=True).then_inc(turned, 1)
                    if stage == "name" and n == 4:
                        pe.wait_ge(picked, 8)
                        pe.matmul(counts[:, 2:3], prior, J[:, SEG - 1:SEG], start=True, stop=True).then_inc(turned, 1)
                    if stage == "name" and n == 5:
                        pe.wait_ge(picked, 9)
                        for half in range(2):
                            ins = pe.matmul(ranks_ps[SEG * half:SEG * (half + 1)], D[:], ident[:, half::2], start=True, stop=True)
                        ins.then_inc(turned, 1)
                    if stage == "name" and 8 <= n < GH:
                        for r in (2 * (n - 8), 2 * (n - 8) + 1):
                            pe.wait_ge(hot_made, r + 1)
                            for t in range(TB):
                                ins = pe.matmul(found_ps[:, 2 * r:2 * r + 2], hot[:, r % 2, t], tk[:, r, t], start=(t == 0), stop=(t == TB - 1))
                            ins.then_inc(found, 1)

                for t in range(HB):
                    turn(t)
                pe.wait_ge(ylo_made, b * TB + HB)
                for n in range(GH):
                    project(n)
                    if n % 2 == 1 and n < 8:
                        turn(HB + n // 2)
                pe.wait_ge(ylo_made, b * TB + TB)
                pe.wait_ge(qkv_evac, NEV * b + evacs(GH - 1))
                for t in range(TB + 3):
                    u, v = t - 2, t - 3
                    if t < TB:
                        if t >= 1:
                            pe.wait_ge(shifted, b * TB + t)
                        for p in range(HP):
                            pe.matmul(banks_s[p // 2][:, 2 * P * (p % 2):2 * P * (p % 2 + 1)], QT[:, p, P * t:P * (t + 1)],
                                      KD[:, p, :, P * t:P * (t + 1)], start=True, stop=True)
                        slot(t, 0)
                        before, after = max(2 * t - 1, 0), min(2 * t + 2, 2 * TB - 1)
                        for p in range(HP):
                            for j, w in enumerate((before, after)):
                                ins = pe.matmul(bank_e[W * j:W * (j + 1), 2 * W * p:2 * W * (p + 1)],
                                                QT[:, p, P * t + W * j:P * t + W * (j + 1)],
                                                KD[:, p, :, W * w:W * (w + 1)], start=True, stop=True)
                        ins.then_inc(scored, 1)
                    if t < 2:
                        for n in fills(t):
                            project(n)
                    if 0 <= u < TB:
                        i = b * TB + u
                        if u == 0:
                            pe.wait_ge(qkv_evac, NEV * (b + 1))
                        pe.wait_ge(probs_made, 3 * (i + 1))
                        for g in range(4):
                            n = 4 * u + g
                            if n >= 3:
                                pe.wait_ge(pT_made, 4 * TB * b + n - 2)
                            for q in range(4):
                                hh, kc = 2 * g + q // 2, q % 2
                                ins = pe.transpose(banks_p[n % 3][:, P * q:P * (q + 1)],
                                                   probs[:, u % 2, hh, P * kc:P * (kc + 1)], ident[:])
                            ins.then_inc(p_turned, 1)
                    if t < TB:
                        slot(t, 1)
                    if v >= 0:
                        i = b * TB + v
                        pe.wait_ge(oT_made, i + 1)
                        if v >= 1:
                            pe.wait_ge(z_made, i)
                        if stage == "descend" and t in (HB, TB):
                            pe.wait_ge(ln_made, b * 2 + (t // HB + 1))
                        if stage == "bisect" and t == TB:
                            pe.wait_ge(bit_step, 3 * TB * 2 + 3)
                        for p in range(HP):
                            ins = pe.matmul(bank_o[:, 0:C], OT[:, P * p:P * (p + 1)], WoT[:, p], start=(p == 0), stop=(p == HP - 1))
                        ins.then_inc(projected, 1)
                    if 0 <= u < TB:
                        i = b * TB + u
                        pe.wait_ge(pT_made, 4 * (i + 1))
                        pe.wait_ge(vx_made, NVX * b + min(2 * u + 2, NVX))
                        for p in range(HP):
                            for kc, val in enumerate((V, VX)):
                                for j in range(2):
                                    hh = 2 * p + j
                                    ins = pe.matmul(bank_v[DH * j:DH * (j + 1), P * p:P * (p + 1)],
                                                    val[:, u, DH * hh:DH * (hh + 1)], pT[:, hh, kc],
                                                    start=(kc == 0), stop=(kc == 1))
                        ins.then_inc(pv_done, 1)
                    if t < TB:
                        slot(t, 2)

            with pe.Fori(0, ROUTED) as b:
                batch_row(b, "descend")
            batch_row(ROUTED, "bisect")
            batch_row(ROUTED + 1, "name")


def chosen_attention(nc, k, ps, d):
    ident, tg, IDX, X = k["ident"], k["tg"], k["IDX"], k["X"]
    G = 3 * B
    TINY = (1e-12 / C ** 0.5) ** 2
    LIFT = 30
    with ExitStack() as stack:
        s = Space(nc, stack, "chosen")
        Wq, Wkv, Wo = s.sb("Wq", [P, CC, IN]), s.sb("Wkv", [P, CC, 2 * IN]), s.sb("Wo", [P, HP, C])
        Z, out_rows = s.sb("Z", [P, B, C]), s.sb("out_rows", [P, B, C])
        bst, mv = s.sb("bst", [P, G, 6]), s.sb("mv", [P, G, 2])
        r, ms, LA, LB, LC, scl = (s.sb(n, [P, G]) for n in ("r", "ms", "LA", "LB", "LC", "scl"))
        gam = s.sb("gam", [P, CC])
        xn, xT = s.sb("xn", [P, 3, C]), s.sb("xT", [P, CC, 3 * P])
        QT, KD, V = s.sb("QT", [P, HP, P]), s.sb("KD", [P, HP, 2, NKV]), s.sb("V", [P, 2, IN])
        NK, nk, NV = s.sb("NK", [P, HP * H]), s.sb("nk", [P, HP]), s.sb("NV", [H, IN])
        E, e0 = s.sb("E", [P, H, NKV]), s.sb("e0", [P, H])
        mx, sm, rc = s.sb("mx", [P, H]), s.sb("sm", [P, H]), s.sb("rc", [P, H])
        pT, p0T, OT = s.sb("pT", [P, H, 2, P]), s.sb("p0T", [H, P]), s.sb("OT", [P, HP * P])

        w_loaded, null_loaded, z_gathered, scattered = (s.sem(n) for n in (
            "w_loaded", "null_loaded", "z_gathered", "scattered"))
        pool_once, stats, vec, lns = s.sem("pool_once"), s.sem("stats"), s.sem("vec"), s.sem("lns")
        xn_made, x_turned, xT_made = s.sem("xn_made"), s.sem("x_turned"), s.sem("xT_made")
        proj, q_made, kd_made, v_made = s.sem("proj"), s.sem("q_made"), s.sem("kd_made"), s.sem("v_made")
        scored, max_made, shifted, exp_made = s.sem("scored"), s.sem("max_made"), s.sem("shifted"), s.sem("exp_made")
        sum_made, probs_made = s.sem("sum_made"), s.sem("probs_made")
        p_turned, pT_made, pv_done, oT_made = s.sem("p_turned"), s.sem("pT_made"), s.sem("pv_done"), s.sem("oT_made")
        projected, rows_made, null_placed = s.sem("projected"), s.sem("rows_made"), s.sem("null_placed")
        block = stack.enter_context(nc.Block())

        @block.sync
        def _(sp):
            sp.dma_start(gam[:], d["gamma"]).then_inc(w_loaded, 16)
            sp.dma_start(Wq[:], d["hWqT"].rearrange("(k p) n -> p k n", p=P)).then_inc(w_loaded, 16)
            sp.dma_start(Wkv[:], d["hWkvT"].rearrange("(k p) n -> p k n", p=P)).then_inc(w_loaded, 16)
            sp.dma_start(Wo[:], d["hWoutT"].rearrange("(k p) n -> p k n", p=P)).then_inc(w_loaded, 16)
            sp.dma_start(nk[:], d["null_k"]).then_inc(w_loaded, 16)
            sp.wait_ge(vec, 2)
            for h in range(H):
                sp.dma_start(NV[h:h + 1, DH * h:DH * (h + 1)], d["null_v"][h:h + 1, :]).then_inc(null_loaded, 16)

        @block.gpsimd
        def _(pool):
            def rows_of(g):
                return bass.IndirectOffsetOnAxis(ap=IDX[:, g:g + 1].bitcast(U32), axis=0)

            for b in range(B):
                pool.indirect_dma_start(Z[:, b], None, d["z_rows"], rows_of(3 * b)).then_inc(z_gathered, 16)
            pool.memset(KD[:], 0.0).then_inc(pool_once, 1)
            for b in range(B):
                pool.wait_ge(rows_made, b + 1)
                pool.indirect_dma_start(d["out"], rows_of(3 * b), out_rows[:, b], None).then_inc(scattered, 16)
            pool.wait_ge(scattered, 16 * B)

        @block.scalar
        def _(act):
            act.wait_ge(vec, 3)
            act.activation(LB[:], LA[:], ACT.Ln).then_inc(lns, 1)
            act.wait_ge(lns, 1)
            act.activation(LC[:], LB[:], ACT.Exp, scale=-0.5).then_inc(lns, 1)
            act.wait_ge(vec, 10)
            act.activation(LB[:], ms[:], ACT.Ln, scale=float(4 ** LIFT)).then_inc(lns, 1)
            act.wait_ge(lns, 3)
            act.activation(LC[:], LB[:], ACT.Exp, scale=-0.5).then_inc(lns, 1)
            act.wait_ge(pool_once, 1)
            with act.Fori(0, B) as b:
                act.wait_ge(proj, 7 * b + 1)
                act.activation(QT[:].rearrange("p k n -> p (k n)"), ps[2][:], ACT.Copy, scale=SCALE).then_inc(q_made, 1)
                for m in range(HP):
                    act.wait_ge(proj, 7 * b + 3 + 2 * (m // 2))
                    for j in range(2):
                        rows = slice(DH * j, DH * (j + 1))
                        act.activation(KD[rows, m, j], ps[3 + m // 2][rows, NKV * (m % 2):NKV * (m % 2 + 1)],
                                       ACT.Copy).then_inc(kd_made, 1)
                act.wait_ge(shifted, 5 * b + 5)
                act.activation(E[:], E[:], ACT.Exp).then_inc(exp_made, 1)
                act.activation(e0[:], e0[:], ACT.Exp).then_inc(exp_made, 1)
                act.wait_ge(p_turned, 5 * b + 1)
                act.activation(p0T[:], ps[7][0:H, P:2 * P], ACT.Copy).then_inc(pT_made, 1)
                for g in range(4):
                    act.wait_ge(p_turned, 5 * b + 2 + g)
                    act.activation(pT[:, 2 * g:2 * g + 2].rearrange("p h k n -> p (h k n)"), ps[4 + g % 3][:], ACT.Copy).then_inc(pT_made, 1)

        @block.vector
        def _(dve):
            dve.memset(NK[:], 0.0).then_inc(vec, 1)
            dve.memset(NV[:], 0.0).then_inc(vec, 1)
            for g in range(G):
                dve.bn_stats(bst[:, g], X[:, g]).then_inc(stats, 1)
            dve.wait_ge(stats, G)
            dve.wait_ge(vec, 2)
            dve.memset(sm[:], 0.0)
            for g in range(G):
                dve.bn_aggr(mv[:, g], bst[:, g]).then_inc(stats, 1)
            dve.wait_ge(stats, 2 * G)
            dve.tensor_scalar(LA[:], mv[:, :, 1], EPS, None, ALU.add).then_inc(vec, 1)
            dve.wait_ge(lns, 2)
            dve.wait_ge(vec, 3)
            rsqrt_step(dve, r, LC, LA, LB, vec, 3)
            dve.tensor_tensor(ms[:], mv[:, :, 1], r[:], ALU.mult).then_inc(vec, 1)
            dve.wait_ge(vec, 8)
            dve.tensor_tensor(ms[:], ms[:], r[:], ALU.mult).then_inc(vec, 1)
            dve.wait_ge(vec, 9)
            dve.tensor_scalar(ms[:], ms[:], TINY, None, ALU.max).then_inc(vec, 1)
            dve.wait_ge(lns, 4)
            dve.wait_ge(vec, 10)
            dve.tensor_scalar(LC[:], LC[:], float(2 ** LIFT), None, ALU.mult).then_inc(vec, 1)
            dve.wait_ge(vec, 11)
            rsqrt_step(dve, scl, LC, ms, LB, vec, 11)
            dve.tensor_tensor(scl[:], scl[:], r[:], ALU.mult).then_inc(vec, 1)
            dve.wait_ge(vec, 16)
            dve.wait_ge(w_loaded, 16 * 5)
            for j in range(2):
                dve.tensor_copy(NK[DH * j:DH * (j + 1), j::H + 2], nk[DH * j:DH * (j + 1), :]).then_inc(null_placed, 1)
            with dve.Fori(0, B) as b:
                for j in range(3):
                    g = 3 * b + j
                    dve.tensor_scalar(xn[:, j], flat(X[:, bass.ds(g, 1)]), mv[:, bass.ds(g, 1), 0], scl[:, bass.ds(g, 1)],
                                      ALU.subtract, ALU.mult).then_inc(xn_made, 1)
                for c in range(CC):
                    dve.wait_ge(x_turned, 2 * b + c + 1)
                    dve.tensor_scalar(xT[:, c], ps[c][:, 0:3 * P], gam[:, c:c + 1], None, ALU.mult).then_inc(xT_made, 1)
                for j in range(2):
                    dve.wait_ge(proj, 7 * b + 6 + j)
                    dve.tensor_copy(V[:, j], ps[5 + j][:]).then_inc(v_made, 1)
                for p in range(HP):
                    if p == 0:
                        dve.wait_ge(scored, b + 1)
                    dve.tensor_reduce(mx[:, 2 * p:2 * p + 2], ps[p][:].rearrange("p (h m) -> p h m", m=NKV), AX_X, ALU.max).then_inc(max_made, 1)
                dve.wait_ge(max_made, 5 * b + 4)
                dve.tensor_tensor(mx[:], ps[7][:, 0:H], mx[:], ALU.max).then_inc(max_made, 1)
                dve.wait_ge(max_made, 5 * b + 5)
                for p in range(HP):
                    dve.tensor_tensor(E[:, 2 * p:2 * p + 2], ps[p][:].rearrange("p (h m) -> p h m", m=NKV),
                                      cols(mx[:, 2 * p:2 * p + 2], NKV), ALU.subtract).then_inc(shifted, 1)
                dve.tensor_tensor(e0[:], ps[7][:, 0:H], mx[:], ALU.subtract).then_inc(shifted, 1)
                dve.wait_ge(exp_made, 2 * b + 2)
                dve.tensor_reduce(sm[:], E[:], AX_X, ALU.add).then_inc(sum_made, 1)
                dve.wait_ge(sum_made, 3 * b + 1)
                dve.tensor_tensor(sm[:], sm[:], e0[:], ALU.add).then_inc(sum_made, 1)
                dve.wait_ge(sum_made, 3 * b + 2)
                dve.reciprocal(rc[:], sm[:]).then_inc(sum_made, 1)
                dve.wait_ge(sum_made, 3 * b + 3)
                dve.tensor_tensor(e0[:], e0[:], rc[:], ALU.mult).then_inc(probs_made, 1)
                for g in range(4):
                    at = slice(2 * g, 2 * g + 2)
                    dve.tensor_tensor(E[:, at], E[:, at], cols(rc[:, at], NKV), ALU.mult).then_inc(probs_made, 1)
                dve.wait_ge(pv_done, b + 1)
                dve.tensor_copy(OT[:], ps[0][:]).then_inc(oT_made, 1)
                dve.wait_ge(projected, b + 1)
                dve.wait_ge(z_gathered, 16 * B)
                dve.scalar_tensor_tensor(flat(out_rows[:, bass.ds(b, 1)]), ps[1][:, 0:C], tg[:, 1:2],
                                         flat(Z[:, bass.ds(b, 1)]), ALU.mult, ALU.add).then_inc(rows_made, 1)

        @block.tensor
        def _(pe):
            pe.wait_ge(w_loaded, 16 * 5)
            pe.wait_ge(null_loaded, 16 * H)
            pe.wait_ge(null_placed, 2)
            with pe.Fori(0, B) as b:
                pe.wait_ge(xn_made, 3 * b + 3)
                for c in range(CC):
                    for j in range(3):
                        ins = pe.transpose(ps[c][:, P * j:P * (j + 1)], xn[:, j, P * c:P * (c + 1)], ident[:])
                    ins.then_inc(x_turned, 1)
                pe.wait_ge(xT_made, 2 * b + 2)
                for m in range(HP):
                    for c in range(CC):
                        ins = pe.matmul(ps[2][:, P * m:P * (m + 1)], Wq[:, c, P * m:P * (m + 1)], xT[:, c, 0:P],
                                        start=(c == 0), stop=(c == CC - 1))
                ins.then_inc(proj, 1)
                for m in range(HP):
                    for c in range(CC):
                        ins = pe.matmul(ps[3 + m // 2][:, NKV * (m % 2):NKV * (m % 2 + 1)], Wkv[:, c, P * m:P * (m + 1)],
                                        xT[:, c, P:3 * P], start=(c == 0), stop=(c == CC - 1))
                    ins.then_inc(proj, 1)
                for j in range(2):
                    for c in range(CC):
                        ins = pe.matmul(ps[5 + j][:], xT[:, c, P * (j + 1):P * (j + 2)], Wkv[:, c, IN:2 * IN],
                                        start=(c == 0), stop=(c == CC - 1))
                    ins.then_inc(proj, 1)
                pe.wait_ge(q_made, b + 1)
                pe.wait_ge(kd_made, 8 * b + 8)
                for p in range(HP):
                    pe.matmul(ps[7][:, 0:H], QT[:, p], NK[:, H * p:H * (p + 1)], start=(p == 0), stop=(p == HP - 1))
                for p in range(HP):
                    ins = pe.matmul(ps[p][:], QT[:, p], KD[:, p].rearrange("p h n -> p (h n)"), start=True, stop=True)
                ins.then_inc(scored, 1)
                pe.wait_ge(v_made, 2 * b + 2)
                pe.wait_ge(probs_made, 5 * b + 1)
                pe.transpose(ps[7][0:H, P:2 * P], e0[:], ident[:]).then_inc(p_turned, 1)
                for g in range(4):
                    pe.wait_ge(probs_made, 5 * b + 2 + g)
                    if g == 3:
                        pe.wait_ge(pT_made, 5 * b + 2)
                    for q in range(4):
                        hh, kc = 2 * g + q // 2, q % 2
                        ins = pe.transpose(ps[4 + g % 3][:, P * q:P * (q + 1)], E[:, hh, P * kc:P * (kc + 1)], ident[:])
                    ins.then_inc(p_turned, 1)
                pe.wait_ge(pT_made, 5 * b + 5)
                for p in range(HP):
                    for kc in range(3):
                        for j in range(2):
                            hh = 2 * p + j
                            dst = ps[0][DH * j:DH * (j + 1), P * p:P * (p + 1)]
                            if kc < 2:
                                ins = pe.matmul(dst, V[:, kc, DH * hh:DH * (hh + 1)], pT[:, hh, kc], start=(kc == 0), stop=False)
                            else:
                                ins = pe.matmul(dst, NV[:, DH * hh:DH * (hh + 1)], p0T[:], start=False, stop=True)
                ins.then_inc(pv_done, 1)
                pe.wait_ge(oT_made, b + 1)
                for p in range(HP):
                    ins = pe.matmul(ps[1][:, 0:C], OT[:, P * p:P * (p + 1)], Wo[:, p], start=(p == 0), stop=(p == HP - 1))
                ins.then_inc(projected, 1)


def build_program(nc, d):
    with ExitStack() as stack:
        s = Space(nc, stack, "all")
        k = {"XR": s.sb("XR", [P, NT, C]), "ident": s.sb("ident", [P, P]), "MV": s.sb("MV", [P, NT, 2]),
             "RS": s.sb("RS", [P, NT]), "tg": s.sb("tg", [P, 2]), "sraw": s.sb("sraw", [P, 2, NT]),
             "IDX": s.sb("IDX", [P, 3 * B], I32), "X": s.sb("X", [P, 3 * B, C])}
        ps = [stack.enter_context(nc.psum_tensor(f"ps{i}", [P, 512], F32)) for i in range(8)]
        for name in ("x1_rows", "z_rows"):
            d[name] = nc.dram_tensor(name, (B * N, C), F32, kind="Internal").ap()
        cross_attention(nc, k, ps, d)
        windowed_attention(nc, k, ps, d)
        chosen_attention(nc, k, ps, d)


def kernel(x, ctx_768, g_xattn, g_ffn, L0_xattn_Wq, L0_xattn_Wk, L0_xattn_Wv, L0_xattn_Wo, L0_xattn_bo,
           L0_ffn_ln_w, L0_ffn_ln_b, L0_ffn_Wqkv, L0_ffn_Wout_l, L0_ffn_rt_q, L0_ffn_rt_kv, L0_ffn_gamma,
           L0_ffn_Wq, L0_ffn_Wkv, L0_ffn_Wout_h, L0_ffn_null_kv, L0_ffn_null_q):
    import numpy as np
    import concourse.bacc as bacc
    from concourse.bass_utils import run_bass_kernel_spmd

    def lay(a):
        return np.ascontiguousarray(a)

    def by_row(a):
        return lay(np.reshape(a, (CC, P)).T)

    ks = [NQ] * B + [NKV] * B
    same = (np.arange(P)[:, None] // (P // R) == np.arange(P)[None, :] // (P // R)).astype(np.float64)
    arrays = {
        "x": lay(np.reshape(x, (B * N, C))),
        "ctxT": lay(np.reshape(ctx_768, (B * M, XC)).T),
        "g_xattn": lay(g_xattn), "g_ffn": lay(g_ffn),
        "xWqT": lay(np.transpose(L0_xattn_Wq)), "xWk": lay(L0_xattn_Wk), "xWv": lay(L0_xattn_Wv),
        "xWo": lay(L0_xattn_Wo), "xbo": lay(L0_xattn_bo),
        "ln_w": by_row(L0_ffn_ln_w), "ln_b": by_row(L0_ffn_ln_b),
        "WqkvT": lay(np.transpose(L0_ffn_Wqkv)), "WoutlT": lay(np.transpose(L0_ffn_Wout_l)),
        "rt_q": lay(L0_ffn_rt_q), "rt_kv": lay(L0_ffn_rt_kv), "gamma": by_row(L0_ffn_gamma),
        "hWqT": lay(np.transpose(L0_ffn_Wq)),
        "hWkvT": lay(np.reshape(L0_ffn_Wkv, (H, 2, DH, C)).transpose(3, 1, 0, 2).reshape(C, 2 * IN)),
        "hWoutT": lay(np.transpose(L0_ffn_Wout_h)),
        "null_k": lay(np.reshape(L0_ffn_null_kv[0], (HP, P)).T), "null_v": lay(L0_ffn_null_kv[1]), "null_q": lay(L0_ffn_null_q),
        "rows128": np.array([[log(N) - log(q * FETCH), q, 0.0, 0.0] for q in ks for _ in range(P // R)], np.float32),
        "bits128": np.array([[[0, 1 << 30, 1 << 30, 1 << 30]] + [[j << i for j in range(4)] for i in range(28, -1, -2)]] * P, np.int32),
        "blocks": np.stack([same / (np.repeat(ks, P // R)[None, :] * FETCH), same,
                            same * (np.arange(P)[:, None] < np.arange(P)[None, :])], 1).astype(np.float32),
        "fold": np.array([[float(p % SEG == i) for i in range(SEG)] for p in range(P)], np.float32),
        "edge": np.array([[NEG * (p < W), NEG * (p >= W)] for p in range(P)], np.float32),
    }
    nc = bacc.Bacc("TRN2", target_bir_lowering=False, num_devices=1)
    d = {n: nc.dram_tensor(n, a.shape, mybir.dt.from_np(a.dtype), kind="ExternalInput").ap() for n, a in arrays.items()}
    d["out"] = nc.dram_tensor("out", (B * N, C), F32, kind="ExternalOutput").ap()
    build_program(nc, d)
    r = run_bass_kernel_spmd(nc, [arrays], core_ids=[0])
    return r.results[0]["out"].reshape(B, N, C)
```

```python
from contextlib import ExitStack
from math import log

import concourse.bass as bass
from concourse import mybir

F32 = mybir.dt.float32
F32R = mybir.dt.float32r
F16 = mybir.dt.float16
I32 = mybir.dt.int32
U32 = mybir.dt.uint32
ACT = mybir.ActivationFunctionType
ALU = mybir.AluOpType
AX_X = mybir.AxisListType.X

P = 128
B, N, C = 4, 1024, 256
CC = C // P
TB = N // P
NT = B * TB
EPS = 1e-5

XH, XD, M, XC = 16, 64, 77, 192
XI = XH * XD
XP = XH // 2
XKC = XC // 2
S1 = XH * M
KT = -(-S1 // P)
S1P = KT * P
PW = 2 * M
VW = P - 1 + PW + P - 1
SCOLS = [(0, 6 * M), (6 * M, 12 * M), (12 * M, 16 * M)]
GPAIRS = [(0, 3), (3, 6), (6, 8)]
GN = CC * len(GPAIRS)
UN = KT // 2

H, DH, W = 8, 64, 64
HP = H // 2
IN = H * DH
SCALE = DH ** -0.5
NQ, NKV = 128, 256
TINY = (1e-12 / C ** 0.5) ** 2
LIFT = 30
G = 3 * B
FETCH = 9.0 / 8.0
ROUTED = 2
CAP = 80.0
R = 2 * B
SEG = N * R // P
NEG = -1e9
SMALLEST = 87.33655


def flat(ap):
    return ap.rearrange("p a b -> p (a b)")


def cols(ap, m):
    return ap.rearrange("p (h o) -> p h o", o=1).to_broadcast([ap.shape[0], ap.shape[1], m])


class Space:

    def __init__(self, nc, stack, phase):
        self.nc, self.stack, self.phase = nc, stack, phase

    def sb(self, name, shape, dt=F32):
        return self.stack.enter_context(self.nc.sbuf_tensor(f"{self.phase}_{name}", shape, dt))

    def sem(self, name):
        return self.stack.enter_context(self.nc.semaphore(f"{self.phase}_{name}"))


def cross_attention(nc, k, ps, d):
    XR, MV, RS, ident, tg, sraw = k["XR"], k["MV"], k["RS"], k["ident"], k["tg"], k["sraw"]
    with ExitStack() as stack:
        s = Space(nc, stack, "cross")
        Wkv = s.sb("Wkv", [XKC, 2, 2, XI])
        KBD = s.sb("KBD", [P, B, XP, PW])
        vT = s.sb("vT", [P, XP, B, M])
        VBD = s.sb("VBD", [P, XP, VW])
        WqT = s.sb("WqT", [P, XP, C])
        Wo = s.sb("Wo", [P, XP, C])
        Ghi, Glo = s.sb("Ghi", [P, CC, S1], F32R), s.sb("Glo", [P, CC, S1], F32R)
        Uhi, Ulo = s.sb("Uhi", [P, KT, C], F32R), s.sb("Ulo", [P, KT, C], F32R)
        probs = s.sb("probs", [P, 4, S1P])
        pThi, pTlo = s.sb("pThi", [P, S1P], F32R), s.sb("pTlo", [P, S1P], F32R)
        h = s.sb("h", [P, 2, C])
        hThi, hTlo = s.sb("hThi", [P, 2, C], F32R), s.sb("hTlo", [P, 2, C], F32R)
        mx, sm, rc = s.sb("mx", [P, 2, XH]), s.sb("sm", [P, 2, XH]), s.sb("rc", [P, 2, XH])
        ctx = s.sb("ctx", [XKC, 2, B * M])
        RT = s.sb("RT", [P, 2, C])
        junk = s.sb("junk", [P, 2, 2, C])
        bo = s.sb("bo", [P, C])
        bst = s.sb("bst", [P, 4, 6])
        x1b, mvb = s.sb("x1b", [P, 4, C]), s.sb("mvb", [P, TB, 2])
        sb8 = s.sb("sb8", [P, 2, TB])
        LA, LB, LC = s.sb("LA", [P, NT]), s.sb("LB", [P, NT]), s.sb("LC", [P, NT])
        banks_s, banks_p, bank_h, bank_o = ps[0:3], ps[3:6], ps[6], ps[7]

        kv_loaded, wq_loaded, wo_loaded, c_loaded = (s.sem(n) for n in (
            "kv_loaded", "wq_loaded", "wo_loaded", "c_loaded"))
        x_loaded = [s.sem(f"x_loaded_{q}") for q in range(B)]
        x1_stored = [s.sem(f"x1_stored_{q}") for q in range(4)]
        pool_once, vec_once, act_once = s.sem("pool_once"), s.sem("vec_once"), s.sem("act_once")
        kv_mult, kv_evac, wst_loaded = s.sem("kv_mult"), s.sem("kv_evac"), s.sem("wst_loaded")
        g_mult, g_hi, g_lo = s.sem("g_mult"), s.sem("g_hi"), s.sem("g_lo")
        u_mult, u_hi, u_lo, vbd_made = s.sem("u_mult"), s.sem("u_hi"), s.sem("u_lo"), s.sem("vbd_made")
        h_made, h_turned, hhi_made, hlo_made = s.sem("h_made"), s.sem("h_turned"), s.sem("hhi_made"), s.sem("hlo_made")
        scored, max_made, exp_made = s.sem("scored"), s.sem("max_made"), s.sem("exp_made")
        recip_made, probs_made = s.sem("recip_made"), s.sem("probs_made")
        p_turned, phi_made, plo_made = s.sem("p_turned"), s.sem("phi_made"), s.sem("plo_made")
        pv_done, bias_added, x1_made = s.sem("pv_done"), s.sem("bias_added"), s.sem("x1_made")
        stats_made, mv_made, routed = s.sem("stats_made"), s.sem("mv_made"), s.sem("routed")
        mv_kept, spaced = s.sem("mv_kept"), s.sem("spaced")

        def g_group(n):
            c, (p0, p1) = n // len(GPAIRS), GPAIRS[n % len(GPAIRS)]
            at = slice(PW * p0, PW * p1)
            return banks_s[n % 3][:, 0:PW * (p1 - p0)], Ghi[:, c, at], Glo[:, c, at]

        def u_group(n):
            return banks_p[n % 3][:, 0:2 * C], flat(Uhi[:, 2 * n:2 * n + 2]), flat(Ulo[:, 2 * n:2 * n + 2])

        def u_fills(t):
            return range(0, 3) if t == 0 else range(3, UN) if t == 1 else range(0)

        def g_fills(t):
            return range(GN // 2 * (t - TB), GN // 2 * (t - TB + 1)) if t >= TB else range(0)

        block = stack.enter_context(nc.Block())

        @block.sync
        def _(sp):
            xv = d["x"].rearrange("(t p) c -> p t c", p=P)

            def load_x(q):
                sp.dma_start(XR[:, q * TB:(q + 1) * TB], xv[:, q * TB:(q + 1) * TB]).then_inc(x_loaded[q], 16)

            sp.dma_start(ctx[:], d["ctxT"].rearrange("(k p) n -> p k n", p=XKC)).then_inc(kv_loaded, 16)
            sp.dma_start(Wkv[:, 0], d["xWk"].rearrange("(k p) n -> p k n", p=XKC)).then_inc(kv_loaded, 16)
            sp.dma_start(Wkv[:, 1], d["xWv"].rearrange("(k p) n -> p k n", p=XKC)).then_inc(kv_loaded, 16)
            load_x(0)
            load_x(1)
            sp.dma_start(WqT[:], d["xWqT"].rearrange("(k p) n -> p k n", p=P)).then_inc(wq_loaded, 16)
            load_x(2)
            load_x(3)
            sp.dma_start(Wo[:], d["xWo"].rearrange("(k p) n -> p k n", p=P)).then_inc(wo_loaded, 16)
            sp.wait_ge(kv_mult, 2 * XP)
            sp.dma_start(k["Wst"][:], d["WqkvT"].rearrange("(k p) n -> p k n", p=P)).then_inc(wst_loaded, 16)
            for q in range(4):
                for _ in range(2):
                    sp.dma_start(x1b[:, q], d["x"][0:P, :]).then_inc(x1_stored[q], 16)
                    sp.wait_ge(x1_stored[q], 16 * (_ + 1))
            x1v = d["x1_rows"].rearrange("(t p) c -> p t c", p=P)
            with sp.Fori(0, NT // 4) as i:
                for q in range(4):
                    sp.wait_ge(x1_made, 4 * i + q + 1)
                    sp.dma_start(x1v[:, bass.ds(4 * i + q, 1)], x1b[:, q:q + 1]).then_inc(x1_stored[q], 16)
                    sp.dma_start(XR[:, bass.ds(4 * i + q, 1)], x1b[:, q:q + 1]).then_inc(x1_stored[q], 16)
            for q in range(4):
                sp.wait_ge(x1_stored[q], 32 * (NT // 4 + 1))
            sp.wait_ge(wst_loaded, 16)

        @block.gpsimd
        def _(pool):
            pool.memset(ident[:], 0.0).then_inc(pool_once, 1)
            pool.wait_ge(pool_once, 1)
            pool.affine_select(out=ident[:], in_=ident[:], compare_op=ALU.not_equal, fill=1.0, base=0,
                               pattern=[[-1, P]], channel_multiplier=1).then_inc(pool_once, 1)
            pool.memset(KBD[:], 0.0).then_inc(pool_once, 1)
            pool.memset(VBD[:], 0.0).then_inc(pool_once, 1)
            pool.memset(probs[:, :, S1:S1P], 0.0).then_inc(pool_once, 1)
            pool.wait_ge(pool_once, 5)
            pool.wait_ge(act_once, 1)
            pool.tensor_tensor(bo[:], bo[:], tg[:, 0:1].to_broadcast([P, C]), ALU.mult).then_inc(pool_once, 1)
            pool.wait_ge(pool_once, 6)
            with pool.Fori(0, B) as b:
                for t in range(TB):
                    i = b * TB + t
                    pool.wait_ge(h_made, i + 1)
                    xt = flat(XR[:, bass.ds(i, 1)])
                    pool.tensor_tensor(xt, xt, bo[:], ALU.add).then_inc(bias_added, 1)
                    pool.wait_ge(recip_made, i + 1)
                    pr = probs[:, t % 4, 0:S1].rearrange("p (h m) -> p h m", m=M)
                    pool.tensor_tensor(pr, pr, cols(rc[:, t % 2], M), ALU.mult).then_inc(probs_made, 1)

        @block.scalar
        def _(act):
            for src, dst in ((d["g_xattn"].rearrange("(o n) -> o n", o=1).to_broadcast([P, 1]), tg[:, 0:1]),
                             (d["g_ffn"].rearrange("(o n) -> o n", o=1).to_broadcast([P, 1]), tg[:, 1:2]),
                             (d["xbo"].rearrange("(o n) -> o n", o=1).to_broadcast([P, C]), bo[:]),
                             (d["rt_q"].to_broadcast([P, C]), RT[:, 0]),
                             (d["rt_kv"].to_broadcast([P, C]), RT[:, 1])):
                act.dma_start(dst, src).then_inc(c_loaded, 16)
            act.wait_ge(pool_once, 3)
            for p in range(XP):
                act.wait_ge(kv_mult, 2 * p + 1)
                for j in range(2):
                    rows = slice(XD * j, XD * (j + 1))
                    act.activation(KBD[rows, :, p, M * j:M * (j + 1)],
                                   ps[(2 * p) % 8][rows, 0:B * M].rearrange("p (b m) -> p b m", m=M),
                                   ACT.Copy, scale=XD ** -0.5).then_inc(kv_evac, 1)
                act.wait_ge(kv_mult, 2 * p + 2)
                act.activation(flat(vT[:, p]), ps[(2 * p + 1) % 8][:, 0:B * M], ACT.Copy).then_inc(kv_evac, 1)
            act.wait_ge(kv_evac, 3 * XP)
            act.wait_ge(pool_once, 4)

            def high_g(b, n):
                bank, hi, _ = g_group(n)
                act.wait_ge(g_mult, GN * (b + 1) + n + 1)
                act.activation(hi, bank, ACT.Copy).then_inc(g_hi, 1)

            def high_u(b, n):
                bank, hi, _ = u_group(n)
                act.wait_ge(u_mult, UN * b + n + 1)
                act.activation(hi, bank, ACT.Copy).then_inc(u_hi, 1)

            def high_h(i, t):
                act.wait_ge(h_turned, i + 1)
                act.activation(hThi[:, t % 2], bank_h[:, 0:C], ACT.Copy).then_inc(hhi_made, 1)

            act.wait_ge(c_loaded, 16 * 5)
            act.activation(tg[:], tg[:], ACT.Tanh).then_inc(act_once, 1)
            act.wait_ge(vec_once, 1)
            act.activation(LB[:], LA[:], ACT.Ln).then_inc(act_once, 1)
            act.wait_ge(act_once, 2)
            act.activation(LC[:], LB[:], ACT.Exp, scale=-0.5).then_inc(act_once, 1)
            for n in range(GN):
                high_g(-1, n)
            high_h(0, 0)

            def batch_row(b, last):
                for j in range(2):
                    rows = slice(XD * j, XD * (j + 1))
                    act.activation(VBD[rows, :, P - 1 + M * j:P - 1 + M * (j + 1)],
                                   vT[rows, :, b:b + 1, :].rearrange("p x o m -> p x (o m)") if last else
                                   vT[rows, :, bass.ds(b, 1), :].rearrange("p x o m -> p x (o m)"),
                                   ACT.Copy).then_inc(vbd_made, 1)
                for t in range(TB + 2):
                    if t >= 2:
                        for j in range(3):
                            w = min(512, S1P - 512 * j)
                            act.wait_ge(p_turned, 3 * (b * TB + t - 2) + j + 1)
                            act.activation(pThi[:, 512 * j:512 * j + w], banks_p[j][:, 0:w], ACT.Copy).then_inc(phi_made, 1)
                    if t < TB:
                        for j, (c0, c1) in enumerate(SCOLS):
                            if j == 1 and t < (TB - 1 if last else TB):
                                high_h(b * TB + t + 1, t + 1)
                            if j == 1 and t == 1:
                                for n in u_fills(t):
                                    high_u(b, n)
                            act.wait_ge(max_made, 3 * (b * TB + t) + j + 1)
                            for hd in range(c0 // M, c1 // M):
                                at = slice(M * hd, M * (hd + 1))
                                ins = act.activation(probs[:, t % 4, at], banks_s[j][:, M * hd - c0:M * (hd + 1) - c0], ACT.Exp,
                                                     bias=mx[:, t % 2, hd:hd + 1], accum_out=sm[:, t % 2, hd:hd + 1])
                            ins.then_inc(exp_made, 1)
                    if t == 0:
                        for n in u_fills(t):
                            high_u(b, n)
                    if not last:
                        for n in g_fills(t):
                            high_g(b, n)

            with act.Fori(0, B - 1) as b:
                batch_row(b, False)
            batch_row(B - 1, True)

        @block.vector
        def _(dve):
            def aggregate(i):
                dve.wait_ge(stats_made, i + 1)
                dve.bn_aggr(MV[:, i], bst[:, i % 4]).then_inc(mv_made, 1)

            for i in range(NT):
                if i % TB == 0:
                    dve.wait_ge(x_loaded[i // TB], 16)
                if i >= 4:
                    dve.wait_ge(mv_made, i - 3)
                dve.bn_stats(bst[:, i % 4], XR[:, i]).then_inc(stats_made, 1)
                if i >= 1:
                    aggregate(i - 1)
            aggregate(NT - 1)
            dve.wait_ge(mv_made, NT)
            dve.tensor_scalar(LA[:], MV[:, :, 1], EPS, None, ALU.add).then_inc(vec_once, 1)

            def low_u(b, t):
                for n in u_fills(t):
                    bank, hi, lo = u_group(n)
                    dve.wait_ge(u_hi, UN * b + n + 1)
                    dve.tensor_tensor(lo, bank, hi.bitcast(F32), ALU.subtract).then_inc(u_lo, 1)

            def low_g(b, n):
                bank, hi, lo = g_group(n)
                dve.wait_ge(g_hi, GN * (b + 1) + n + 1)
                dve.tensor_tensor(lo, bank, hi.bitcast(F32), ALU.subtract).then_inc(g_lo, 1)

            def normalise(i, t):
                dve.tensor_scalar(h[:, t % 2], flat(XR[:, i:i + 1] if type(i) is int else XR[:, bass.ds(i, 1)]),
                                  MV[:, i:i + 1, 0] if type(i) is int else MV[:, bass.ds(i, 1), 0],
                                  RS[:, i:i + 1] if type(i) is int else RS[:, bass.ds(i, 1)],
                                  ALU.subtract, ALU.mult).then_inc(h_made, 1)

            def low_h(i, t):
                dve.wait_ge(hhi_made, i + 1)
                dve.tensor_tensor(hTlo[:, t % 2], bank_h[:, 0:C], hThi[:, t % 2].bitcast(F32), ALU.subtract).then_inc(hlo_made, 1)

            dve.wait_ge(act_once, 3)
            dve.wait_ge(vec_once, 1)
            rsqrt_step(dve, RS, LC, LA, LB, vec_once, 1)
            normalise(0, 0)
            normalise(1, 1)
            for n in range(GN):
                low_g(-1, n)
            low_h(0, 0)

            def route_product(u, j):
                dve.scalar_tensor_tensor(junk[:, u % 2, j], x1b[:, u % 4], mvb[:, u, 0:1], RT[:, j],
                                         ALU.subtract, ALU.mult, accum_out=sb8[:, j, u:u + 1]).then_inc(routed, 1)

            def batch_row(b, last):
                for t in range(TB + 2):
                    if 1 <= t < (TB - 1 if last else TB):
                        dve.wait_ge(h_turned, b * TB + t)
                        normalise(b * TB + t + 1, t + 1)
                    if t == TB + 1 and not last:
                        dve.wait_ge(h_turned, b * TB + TB)
                        normalise(b * TB + TB + 1, TB + 1)
                    for j, (c0, c1) in enumerate(SCOLS):
                        if t < TB:
                            dve.wait_ge(scored, 3 * (b * TB + t) + j + 1)
                            dve.tensor_reduce(mx[:, t % 2, c0 // M:c1 // M],
                                              banks_s[j][:, 0:c1 - c0].rearrange("p (h m) -> p h m", m=M),
                                              AX_X, ALU.max, negate=True).then_inc(max_made, 1)
                        if j == 0 and t >= 2:
                            for q in range(3):
                                w = min(512, S1P - 512 * q)
                                at = slice(512 * q, 512 * q + w)
                                dve.wait_ge(phi_made, 3 * (b * TB + t - 2) + q + 1)
                                dve.tensor_tensor(pTlo[:, at], banks_p[q][:, 0:w], pThi[:, at].bitcast(F32),
                                                  ALU.subtract).then_inc(plo_made, 1)
                    if t < (TB - 1 if last else TB):
                        low_h(b * TB + t + 1, t + 1)
                    if not last:
                        for n in g_fills(t):
                            low_g(b, n)
                    if t >= 2:
                        u = t - 2
                        i = b * TB + u
                        dve.wait_ge(pv_done, i + 1)
                        dve.wait_ge(bias_added, i + 1)
                        dve.wait_ge(x1_stored[u % 4], 32 * (b * (TB // 4) + u // 4 + 1))
                        dve.scalar_tensor_tensor(x1b[:, u % 4], bank_o[:, 0:C], tg[:, 0:1],
                                                 flat(XR[:, bass.ds(i, 1)] if not last else XR[:, i:i + 1]),
                                                 ALU.mult, ALU.add).then_inc(x1_made, 1)
                        dve.wait_ge(x1_made, i + 1)
                        dve.bn_stats(bst[:, u % 2], x1b[:, u % 4]).then_inc(stats_made, 1)
                        dve.wait_ge(stats_made, i + NT + 1)
                        if u >= 1:
                            dve.wait_ge(mv_made, i + NT)
                            route_product(u - 1, 0)
                        else:
                            dve.tensor_scalar(junk[:, 0, 0, 0:1], tg[:, 0:1], 0.0, None, ALU.mult).then_inc(spaced, 1)
                        dve.bn_aggr(mvb[:, u], bst[:, u % 2]).then_inc(mv_made, 1)
                        if u >= 1:
                            route_product(u - 1, 1)
                    if t == 1:
                        low_u(b, t)
                    if t < TB:
                        dve.wait_ge(exp_made, 3 * (b * TB + t + 1))
                        dve.reciprocal(rc[:, t % 2], sm[:, t % 2]).then_inc(recip_made, 1)
                    if t == 0:
                        low_u(b, t)
                dve.wait_ge(mv_made, NT + TB * (b + 1))
                for j in range(2):
                    route_product(TB - 1, j)
                rows = slice(b * TB, (b + 1) * TB) if last else bass.ds(b * TB, TB)
                dve.tensor_scalar(MV[:, rows], mvb[:], 0.0, None, ALU.add).then_inc(mv_kept, 1)
                dve.wait_ge(routed, 2 * TB * (b + 1))
                for j in range(2):
                    dve.tensor_scalar(sraw[:, j, rows], sb8[:, j], 0.0, None, ALU.add).then_inc(mv_kept, 1)
                dve.wait_ge(mv_kept, 3 * (b + 1))

            with dve.Fori(0, B - 1) as b:
                batch_row(b, False)
            batch_row(B - 1, True)

        @block.tensor
        def _(pe):
            pe.wait_ge(kv_loaded, 16 * 3)
            for p in range(XP):
                for v in range(2):
                    n = 2 * p + v
                    if n >= 8:
                        pe.wait_ge(kv_evac, 3 * (n // 2 - 4) + (2 if v == 0 else 3))
                    for kc in range(2):
                        ins = pe.matmul(ps[n % 8][:, 0:B * M], Wkv[:, v, kc, P * p:P * (p + 1)], ctx[:, kc],
                                        start=(kc == 0), stop=(kc == 1))
                    ins.then_inc(kv_mult, 1)
            pe.wait_ge(kv_evac, 3 * XP)
            pe.wait_ge(pool_once, 5)
            pe.wait_ge(wq_loaded, 16)

            def make_g(b, n):
                bank, _, _ = g_group(n)
                if n >= 3:
                    pe.wait_ge(g_lo, GN * (b + 1) + n - 2)
                c, (p0, p1) = n // len(GPAIRS), GPAIRS[n % len(GPAIRS)]
                for p in range(p0, p1):
                    keys = KBD[:, b + 1, p] if type(b) is int else KBD[:, bass.ds(b + 1, 1), p, :].rearrange("p o m -> p (o m)")
                    ins = pe.matmul(bank[:, PW * (p - p0):PW * (p - p0 + 1)], WqT[:, p, P * c:P * (c + 1)], keys,
                                    start=True, stop=True)
                ins.then_inc(g_mult, 1)

            def turn(i, t):
                pe.wait_ge(h_made, i + 1)
                for c in range(CC):
                    ins = pe.transpose(bank_h[:, P * c:P * (c + 1)], h[:, t % 2, P * c:P * (c + 1)], ident[:])
                ins.then_inc(h_turned, 1)

            for n in range(GN):
                make_g(-1, n)
            turn(0, 0)
            pe.wait_ge(wo_loaded, 16)

            def batch_row(b, last):
                for t in range(TB + 2):
                    u = t - 2
                    i = b * TB + u
                    if u >= 0:
                        if u == 0:
                            pe.wait_ge(u_lo, UN * (b + 1))
                        pe.wait_ge(probs_made, i + 1)
                        for q in range(KT):
                            ins = pe.transpose(banks_p[q // 4][:, P * (q % 4):P * (q % 4 + 1)],
                                               probs[:, u % 4, P * q:P * (q + 1)], ident[:])
                            if q % 4 == 3 or q == KT - 1:
                                ins.then_inc(p_turned, 1)
                    if t < TB:
                        pe.wait_ge(hlo_made, b * TB + t + 1)
                        if t == 0:
                            pe.wait_ge(g_lo, GN * (b + 1))
                        passes = [(hh, g, c) for hh, g in ((hThi, Ghi), (hThi, Glo), (hTlo, Ghi)) for c in range(CC)]
                        for j, (c0, c1) in enumerate(SCOLS):
                            if t >= 1:
                                pe.wait_ge(exp_made, 3 * (b * TB + t - 1) + j + 1)
                            for n, (hh, g, c) in enumerate(passes):
                                ins = pe.matmul(banks_s[j][:, 0:c1 - c0], hh[:, t % 2, P * c:P * (c + 1)],
                                                g[:, c, c0:c1], start=(n == 0), stop=(n == len(passes) - 1))
                            ins.then_inc(scored, 1)
                    if t < (TB - 1 if last else TB):
                        turn(b * TB + t + 1, t + 1)
                    for n in u_fills(t):
                        if n == 0:
                            pe.wait_ge(vbd_made, 2 * (b + 1))
                        if n >= 3:
                            pe.wait_ge(u_lo, UN * b + n - 2)
                        bank, _, _ = u_group(n)
                        for j in range(2):
                            q = 2 * n + j
                            over = [p for p in range(XP) if PW * p < P * (q + 1) and PW * (p + 1) > P * q]
                            for p in over:
                                at = P - 1 + P * q - PW * p
                                ins = pe.matmul(bank[:, C * j:C * (j + 1)], VBD[:, p, at:at + P], Wo[:, p],
                                                start=(p == over[0]), stop=(p == over[-1]))
                        ins.then_inc(u_mult, 1)
                    if not last:
                        for n in g_fills(t):
                            if n == 0:
                                pe.wait_ge(exp_made, 3 * TB * (b + 1))
                            make_g(b, n)
                    if u >= 0:
                        if u >= 1:
                            pe.wait_ge(x1_made, i)
                        for q in range(KT):
                            if q % 4 == 0:
                                pe.wait_ge(plo_made, 3 * i + q // 4 + 1)
                            for n, (pt, uu) in enumerate(((pThi, Uhi), (pThi, Ulo), (pTlo, Uhi))):
                                ins = pe.matmul(bank_o[:, 0:C], pt[:, P * q:P * (q + 1)], uu[:, q],
                                                start=(q == 0 and n == 0), stop=(q == KT - 1 and n == 2))
                        ins.then_inc(pv_done, 1)

            with pe.Fori(0, B - 1) as b:
                batch_row(b, False)
            batch_row(B - 1, True)


def rsqrt_step(dve, out, r, a, tmp, sem, n):
    dve.tensor_tensor(tmp[:], r[:], r[:], ALU.mult).then_inc(sem, 1)
    dve.wait_ge(sem, n + 1)
    dve.tensor_tensor(tmp[:], tmp[:], a[:], ALU.mult).then_inc(sem, 1)
    dve.wait_ge(sem, n + 2)
    dve.tensor_scalar(tmp[:], tmp[:], -0.5, 1.5, ALU.mult, ALU.add).then_inc(sem, 1)
    dve.wait_ge(sem, n + 3)
    dve.tensor_tensor(out[:], r[:], tmp[:], ALU.mult).then_inc(sem, 1)
    dve.wait_ge(sem, n + 4)


def update_slot(b, t, n):
    return (b * TB + t) * 3 + n


def windowed_attention(nc, k, ps, d):
    XR, MV, ident, tg, sraw, IDX, X = k["XR"], k["MV"], k["ident"], k["tg"], k["sraw"], k["IDX"], k["X"]
    with ExitStack() as stack:
        s = Space(nc, stack, "window")
        Whi, Wlo = s.sb("Whi", [P, CC, 3 * IN], F32R), s.sb("Wlo", [P, CC, 3 * IN], F32R)
        QT = s.sb("QT", [P, HP, N])
        KD = s.sb("KD", [P, HP, 2, N])
        V = s.sb("V", [P, TB, IN])
        VX = s.sb("VX", [P, TB, IN])
        WoT = s.sb("WoT", [P, HP, C])
        y = s.sb("y", [P, 2, C])
        yT = s.sb("yT", [P, 2, CC, P])
        OT = s.sb("OT", [P, HP * P])
        outb = s.sb("outb", [P, 2, C])
        null = s.sb("null", [P, C])
        RR, LA, LB, LC = (s.sb(n, [P, 2, NT]) for n in ("RR", "wLA", "wLB", "wLC"))
        RS, R2 = RR[:, 0], RR[:, 1]
        wb = s.sb("wb", [P, 2, CC])
        edge = s.sb("edge", [P, 2])
        mx, sm, rc = s.sb("wmx", [P, 2, H]), s.sb("wsm", [P, 2, H]), s.sb("wrc", [P, 2, H])
        mxe = s.sb("wmxe", [P, H])
        bst = s.sb("wbst", [P, 2, 6])
        hA, hB, hC = (s.sb(n, [P, G]) for n in ("hA", "hB", "hC"))
        S, D, Wt, J, V_key, LT, EQ, Z = (s.sb(f"r{n}", [P, SEG]) for n in ("S", "D", "Wt", "J", "V", "LT", "EQ", "Z"))
        SM = s.sb("SM", [P, R * TB, 2])
        blocks = s.sb("blocks", [P, 3, P])
        fold = s.sb("fold", [P, SEG])
        rows = s.sb("rows", [P, 4])
        bits = s.sb("bits", [P, 16, 4], I32)
        smax, T, base, one, lnc, need, part, own_max, prefix = (s.sb(n, [P, 1]) for n in (
            "smax", "T", "base", "one", "lnc", "need", "part", "own_max", "prefix"))
        below = s.sb("below", [P, 3, SEG])
        part4, cand, kept = s.sb("part4", [P, 4]), s.sb("cand", [P, 4], I32), s.sb("kept", [P, 4])
        maxes = s.sb("maxes", [1, 2 * P])
        posT, late = s.sb("posT", [P, R, TB]), s.sb("late", [P, R, TB])
        ranks, token = s.sb("ranks", [P, P]), s.sb("token", [P, TB])
        tk = s.sb("tk", [P, R, TB, 2], F16)
        k1, kk, lift, log_lift = (rows[:, n:n + 1] for n in range(4))
        inv_k, same, prior = blocks[:, 0], blocks[:, 1], blocks[:, 2]
        total = ps[7][:, C:C + 4]
        counts, found_ps, ranks_ps = ps[4][:, 0:4], ps[4][:, 16:16 + 2 * R], ps[5][:, 0:R * TB]
        r_loaded, turned, renewed, r_exp, parted, summed, ln_made = (s.sem(n) for n in (
            "r_loaded", "r_turned", "r_renewed", "r_exp", "r_parted", "r_summed", "r_ln"))
        bit_step, compared, counted, picked, hot_made, found, idx_made, x_gathered = (s.sem(n) for n in (
            "r_bit", "r_compared", "r_counted", "r_picked", "r_hot", "r_found", "r_idx", "x_gathered"))

        Wst = k["Wst"]
        with ExitStack() as early:
            ysplit = Space(nc, early, "window").sb("ysplit", [P, 2, 2, CC, 4 * P], F32R)
        probs = s.sb("wprobs", [P, 2, H, 2 * P])
        E = s.sb("E", [P, 2, H, 3 * W])
        with ExitStack() as early:
            hot = Space(nc, early, "window").sb("hot", [P, 2, TB, P], F16)
        pT = s.sb("wpT", [P, H, 2, P])
        banks_s, bank_e, banks_p, bank_v, bank_o = ps[0:2], ps[2], ps[3:6], ps[6], ps[7]

        loaded, w_loaded, once, split = s.sem("w_loaded2"), s.sem("w_loaded3"), s.sem("w_once"), s.sem("w_split")
        pool_once, z_stored, cleared = s.sem("w_pool"), s.sem("z_stored"), s.sem("w_cleared")
        hw_loaded, x_stats, wlo_made = s.sem("hw_loaded"), s.sem("x_stats"), s.sem("wlo_made")
        scale_step, lns = s.sem("w_scale_step"), s.sem("w_lns")
        out_stored = [s.sem("out_stored_0"), s.sem("out_stored_1")]
        y_made, y_turned, yT_made, yhi_made, ylo_made = (s.sem(n) for n in (
            "y_made", "y_turned", "yT_made", "yhi_made", "ylo_made"))
        qkv_mult, qkv_evac, vx_made = s.sem("qkv_mult"), s.sem("qkv_evac"), s.sem("vx_made")
        scored, max_made, max_joined, shifted, exp_made = (s.sem(n) for n in (
            "w_scored", "w_max", "w_max_joined", "w_shifted", "w_exp"))
        sum_made, recip_made, probs_made = s.sem("w_sum"), s.sem("w_recip"), s.sem("w_probs")
        p_turned, pT_made, pv_done, oT_made = s.sem("w_p_turned"), s.sem("w_pT"), s.sem("w_pv"), s.sem("w_oT")
        projected, z_made, out_made = s.sem("w_projected"), s.sem("z_made"), s.sem("out_made")
        HB = TB // 2
        GROUPS = [(half, kind, m) for half in range(2) for kind in "qkv" for m in range(4)]
        NG, GH = len(GROUPS), len(GROUPS) // 2
        NEV = NG + 2 * HP
        NAMED = {GH - 3: (0,), GH - 2: (1, 2), GH - 1: (3, 4), GH: (5, 6, 7)}
        NVX = 2 * TB - 2
        block = stack.enter_context(nc.Block())

        def evacs(n):
            return sum(2 if kind == "k" else 1 for _, kind, _ in GROUPS[:n + 1])

        def group_bank(n):
            return ps[n % 4] if n < GH else ps[3 + n % 4]

        def y_bank(t):
            return ps[t % 2] if t < HB else ps[6 + t % 2]

        def fills(t):
            return range(GH + t * GH // 2, GH + (t + 1) * GH // 2)

        @block.sync
        def _(sp):
            sp.dma_start(rows[:], d["rows128"]).then_inc(r_loaded, 16)
            sp.dma_start(bits[:], d["bits128"]).then_inc(r_loaded, 16)
            sp.dma_start(blocks[:], d["blocks"]).then_inc(r_loaded, 16)
            sp.dma_start(fold[:], d["fold"]).then_inc(r_loaded, 16)
            sp.dma_start(null[:], d["null_q"].rearrange("(o n) -> o n", o=1).to_broadcast([P, C])).then_inc(loaded, 16)
            sp.dma_start(wb[:, 0], d["ln_w"]).then_inc(loaded, 16)
            sp.dma_start(wb[:, 1], d["ln_b"]).then_inc(loaded, 16)
            sp.dma_start(edge[:], d["edge"]).then_inc(loaded, 16)
            sp.dma_start(WoT[:], d["WoutlT"].rearrange("(k p) n -> p k n", p=P)).then_inc(w_loaded, 16)
            for j in range(2):
                sp.dma_start(outb[:, j], d["x"][0:P, :]).then_inc(out_stored[j], 16)
            zv = d["z_rows"].rearrange("(t p) c -> p t c", p=P)
            ov = d["out"].rearrange("(t p) c -> p t c", p=P)
            def store(i):
                for j in range(2):
                    sp.wait_ge(z_made, 2 * i + j + 1)
                    sp.dma_start(zv[:, bass.ds(2 * i + j, 1)], XR[:, bass.ds(2 * i + j, 1)]).then_inc(z_stored, 16)
                    sp.wait_ge(out_made, 2 * i + j + 1)
                    sp.dma_start(ov[:, bass.ds(2 * i + j, 1)], outb[:, j]).then_inc(out_stored[j], 16)

            with sp.Fori(0, (B - 1) * TB // 2) as i:
                store(i)
            sp.wait_ge(qkv_mult, NG * B)
            sp.dma_start(k["hWq"][:], d["hWqT"].rearrange("(k p) n -> p k n", p=P)).then_inc(hw_loaded, 16)
            sp.dma_start(k["hWkv"][:], d["hWkvT"].rearrange("(k p) n -> p k n", p=P)).then_inc(hw_loaded, 16)
            sp.dma_start(k["hWo"][:], d["hWoutT"].rearrange("(k p) n -> p k n", p=P)).then_inc(hw_loaded, 16)
            with sp.Fori((B - 1) * TB // 2, NT // 2) as i:
                store(i)
            sp.wait_ge(hw_loaded, 16 * 3)
            sp.wait_ge(z_stored, 16 * NT)
            for j in range(2):
                sp.wait_ge(out_stored[j], 16 * (NT // 2 + 1))

        @block.gpsimd
        def _(pool):
            pool.memset(SM[:], 0.0).then_inc(pool_once, 1)
            pool.memset(Z[:], 0.0).then_inc(pool_once, 1)
            pool.memset(one[:], 1.0).then_inc(pool_once, 1)
            pool.memset(part4[:], 0.0).then_inc(pool_once, 1)
            pool.iota(ranks[:], pattern=[[1, P]], base=1, channel_multiplier=0,
                      allow_small_or_imprecise_dtypes=True).then_inc(pool_once, 1)
            pool.iota(token[:], pattern=[[P, TB]], base=0, channel_multiplier=1,
                      allow_small_or_imprecise_dtypes=True).then_inc(pool_once, 1)
            pool.memset(KD[:], 0.0).then_inc(pool_once, 1)
            pool.wait_ge(split, 3)
            pool.tensor_tensor(flat(Wlo[:]), flat(Wst[:]), flat(Whi[:]).bitcast(F32), ALU.subtract).then_inc(wlo_made, 1)
            pool.memset(VX[:], 0.0).then_inc(pool_once, 1)
            pool.wait_ge(wlo_made, 1)
            pool.wait_ge(loaded, 16 * 4)
            pool.tensor_tensor(null[:], null[:], tg[:, 1:2].to_broadcast([P, C]), ALU.mult).then_inc(pool_once, 1)
            pool.wait_ge(pool_once, 9)

            def gather(g):
                if g == 0:
                    pool.wait_ge(idx_made, 1)
                pool.indirect_dma_start(X[:, g], None, d["x1_rows"],
                                        bass.IndirectOffsetOnAxis(ap=IDX[:, g:g + 1].bitcast(U32), axis=0)).then_inc(x_gathered, 16)

            def spread_values(b, half):
                for m in range(HB):
                    t = HB * half + m
                    n = NVX * b + max(2 * t - 1, 0)
                    pool.wait_ge(qkv_evac, NEV * b + evacs(GROUPS.index((half, "v", m))))
                    if t >= 1:
                        pool.wait_ge(vx_made, n)
                        pool.tensor_tensor(VX[0:W, t - 1], V[0:W, t], Z[0:W, 0:1].to_broadcast([W, IN]), ALU.add).then_inc(vx_made, 1)
                        n = n + 1
                    if t < TB - 1:
                        if t >= 1:
                            pool.wait_ge(vx_made, n)
                        pool.tensor_tensor(VX[W:P, t + 1], V[W:P, t], Z[W:P, 0:1].to_broadcast([W, IN]), ALU.add).then_inc(vx_made, 1)

            def clear(b, half):
                pool.wait_ge(vx_made, NVX * b + (2 * HB - 1 if half == 0 else NVX))
                pool.wait_ge(qkv_mult, NG * b + GH * (half + 1))
                zero = Z[:].rearrange("p (o n) -> p o n", o=1).to_broadcast([P, H, W])
                pool.tensor_tensor(probs[0:W, half, :, P:P + W], zero[0:W], zero[0:W], ALU.mult).then_inc(cleared, 1)
                pool.wait_ge(cleared, 4 * b + 2 * half + 1)
                pool.tensor_tensor(probs[W:P, half, :, P + W:2 * P], zero[W:P], zero[W:P], ALU.mult).then_inc(cleared, 1)
                pool.wait_ge(cleared, 4 * b + 2 * half + 2)

            def tiles(b, gathers):
                for t in range(TB + 3):
                    if t < 2:
                        spread_values(b, t)
                        clear(b, t)
                    if t < TB:
                        i = b * TB + t
                        pool.wait_ge(recip_made, i + 1)
                        if t >= 2:
                            pool.wait_ge(p_turned, 4 * (i - 1))
                        r = rc[:, t % 2]
                        pool.tensor_tensor(probs[:, t % 2, :, 0:P], E[:, t % 2, :, 0:P], cols(r, P), ALU.mult).then_inc(probs_made, 1)
                        pool.wait_ge(probs_made, 3 * i + 1)
                        pool.tensor_tensor(probs[0:W, t % 2, :, P + W:2 * P], E[0:W, t % 2, :, P:3 * W],
                                           cols(rc[0:W, t % 2], W), ALU.mult).then_inc(probs_made, 1)
                        pool.tensor_tensor(probs[W:P, t % 2, :, P:P + W], E[W:P, t % 2, :, P:3 * W],
                                           cols(rc[W:P, t % 2], W), ALU.mult).then_inc(probs_made, 1)
                        pool.wait_ge(probs_made, 3 * i + 3)
                    if gathers and 0 < t <= 3 * B // 2:
                        for g in (2 * t - 2, 2 * t - 1):
                            gather(g)
                        pool.wait_ge(x_gathered, 32 * t)
                    v = t - 3
                    if v >= 0:
                        i = b * TB + v
                        pool.wait_ge(z_made, i + 1)
                        pool.wait_ge(out_stored[v % 2], 16 * (b * (TB // 2) + v // 2 + 1))
                        pool.tensor_tensor(outb[:, v % 2], flat(XR[:, bass.ds(i, 1)]), null[:], ALU.add).then_inc(out_made, 1)
                        pool.wait_ge(out_made, i + 1)

            with pool.Fori(0, B - 1) as b:
                tiles(b, False)
            tiles(B - 1, True)

        @block.scalar
        def _(act):
            act.wait_ge(once, 3)
            act.activation(LB[:], LA[:], ACT.Ln).then_inc(split, 1)
            act.wait_ge(split, 1)
            act.activation(LC[:], LB[:], ACT.Exp, scale=-0.5).then_inc(split, 1)
            act.activation(flat(Whi[:]), flat(Wst[:]), ACT.Copy).then_inc(split, 1)
            act.wait_ge(turned, 1)
            act.activation(S[:], ps[2][:, 0:SEG], ACT.Copy).then_inc(split, 1)

            def log_sum():
                act.activation(lnc[:], total[:, 0:1], ACT.Ln, scale=lift).then_inc(ln_made, 1)

            def renew(n):
                act.wait_ge(renewed, 3 * n)
                act.activation(Wt[:], D[:], ACT.Exp).then_inc(r_exp, 1)

            def high(b, t):
                act.wait_ge(yT_made, 2 * (b * TB + t) + 2)
                act.activation(ysplit[:, t // HB, 0, :, P * (t % HB):P * (t % HB + 1)], yT[:, t % 2], ACT.Copy).then_inc(yhi_made, 1)

            act.wait_ge(once, 17)
            act.activation(Wt[:], D[:], ACT.Exp).then_inc(r_exp, 1)
            for t in range(HB):
                high(0, t)
            act.wait_ge(summed, 1)
            log_sum()
            renew(1)
            act.wait_ge(pool_once, 7)

            def batch_row(b, stage, last=False):
                def out_of(n):
                    act.wait_ge(qkv_mult, NG * b + n + 1)
                    bank = group_bank(n)
                    half, kind, m = GROUPS[n]
                    at = slice(512 * half, 512 * half + 512)
                    if kind == "v":
                        act.activation(V[:, HB * half + m], bank[:], ACT.Copy).then_inc(qkv_evac, 1)
                    elif kind == "q":
                        act.activation(QT[:, m, at], bank[:], ACT.Copy, scale=SCALE).then_inc(qkv_evac, 1)
                    else:
                        for j in range(2):
                            rows = slice(DH * j, DH * (j + 1))
                            act.activation(KD[rows, m, j, at], bank[rows, :], ACT.Copy).then_inc(qkv_evac, 1)

                for n in range(GH):
                    out_of(n)
                    if n >= 2 and n % 2 == 0 and n <= 8:
                        high(b, HB + n // 2 - 1)
                for t in range(TB + 2):
                    u = t - 2
                    if t < 2:
                        for n in fills(t)[0:HP]:
                            out_of(n)
                    if u >= 0:
                        for g in range(4):
                            n = 4 * u + g
                            act.wait_ge(p_turned, 4 * TB * b + n + 1)
                            act.activation(pT[:, 2 * g:2 * g + 2].rearrange("p h k n -> p (h k n)"), banks_p[n % 3][:],
                                           ACT.Copy).then_inc(pT_made, 1)
                    if t < TB:
                        act.wait_ge(shifted, b * TB + t + 1)
                        act.activation(E[:, t % 2], E[:, t % 2], ACT.Exp).then_inc(exp_made, 1)
                    if t < 2:
                        for n in fills(t)[HP:]:
                            out_of(n)
                    ahead = t == TB + 1 and not last
                    if ahead:
                        for m in range(3):
                            high(b + 1, m)
                    if u >= 0:
                        act.wait_ge(pv_done, b * TB + u + 1)
                        act.activation(OT[:], bank_v[:], ACT.Copy).then_inc(oT_made, 1)
                    if ahead:
                        high(b + 1, 3)
                    if stage == "descend" and t % (TB // 2) == TB // 2 - 1 and t < TB:
                        act.wait_ge(summed, update_slot(b, t, 2) + 2)
                        log_sum()
                        if t < TB - 1:
                            renew(b * 2 + (t // (TB // 2) + 2))
                if stage == "descend":
                    renew(b * 2 + 3)

            with act.Fori(0, ROUTED) as b:
                batch_row(b, "descend")
            batch_row(ROUTED, "bisect")
            batch_row(ROUTED + 1, "name", last=True)
            act.wait_ge(scale_step, 2)
            act.activation(hB[:], hA[:], ACT.Ln, scale=float(4 ** LIFT)).then_inc(lns, 1)
            act.wait_ge(lns, 1)
            act.activation(hC[:], hB[:], ACT.Exp, scale=-0.5).then_inc(lns, 1)

        @block.vector
        def _(dve):
            def normalise(b, t):
                i = b * TB + t
                dve.tensor_scalar(y[:, t % 2], flat(XR[:, bass.ds(i, 1)]), MV[:, bass.ds(i, 1), 0],
                                  R2[:, bass.ds(i, 1)], ALU.subtract, ALU.mult).then_inc(y_made, 1)

            def scale_shift(b, t):
                dve.wait_ge(y_turned, b * TB + t + 1)
                if t >= 2:
                    dve.wait_ge(ylo_made, b * TB + t - 1)
                for c in range(CC):
                    dve.tensor_scalar(yT[:, t % 2, c], y_bank(t)[:, P * c:P * (c + 1)], wb[:, 0, c:c + 1],
                                      wb[:, 1, c:c + 1], ALU.mult, ALU.add).then_inc(yT_made, 1)

            def low(b, t):
                dve.wait_ge(yhi_made, b * TB + t + 1)
                at = slice(P * (t % HB), P * (t % HB + 1))
                dve.tensor_tensor(ysplit[:, t // HB, 1, :, at], yT[:, t % 2], ysplit[:, t // HB, 0, :, at].bitcast(F32),
                                  ALU.subtract).then_inc(ylo_made, 1)

            dve.tensor_scalar(LA[:, 1], MV[:, :, 1], EPS, EPS, ALU.add, ALU.mult).then_inc(once, 1)
            dve.tensor_scalar(LA[:, 0], MV[:, :, 1], EPS, None, ALU.add).then_inc(once, 1)
            dve.wait_ge(once, 2)
            dve.tensor_tensor(LA[:, 1], LA[:, 1], MV[:, :, 1], ALU.add).then_inc(once, 1)
            dve.memset(mxe[:], 0.0).then_inc(once, 1)
            dve.wait_ge(split, 2)
            dve.wait_ge(once, 4)
            rsqrt_step(dve, RR, LC, LA, LB, once, 4)
            dve.wait_ge(pool_once, 6)
            for half in range(2):
                at = slice(SEG * half, SEG * (half + 1))
                dve.tensor_tensor(SM[at, :, half].rearrange("p (j i) -> p j i", j=2), sraw[at],
                                  RS[at].rearrange("p (o i) -> p o i", o=1).to_broadcast([SEG, 2, NT]),
                                  ALU.mult).then_inc(once, 1)
            normalise(0, 0)
            normalise(0, 1)
            dve.wait_ge(r_loaded, 16 * 4)
            dve.wait_ge(split, 4)
            dve.tensor_reduce(own_max[:], S[:], AX_X, ALU.max).then_inc(once, 1)
            dve.wait_ge(turned, 2)
            dve.tensor_reduce(maxes[:, 0:R], ps[4][0:1, 0:P].rearrange("p (r q) -> p r q", r=R), AX_X, ALU.max).then_inc(once, 1)
            dve.wait_ge(once, 12)
            dve.tensor_copy(maxes[:, P:2 * P].rearrange("p (r q) -> p r q", r=R), cols(maxes[:, 0:R], P // R)).then_inc(once, 1)
            dve.wait_ge(turned, 3)
            dve.tensor_copy(smax[:], ps[4][:, P:P + 1]).then_inc(once, 1)
            dve.tensor_scalar(T[:], k1, 0.0, None, ALU.add).then_inc(once, 1)
            dve.wait_ge(once, 15)
            dve.tensor_tensor(base[:], T[:], smax[:], ALU.min).then_inc(once, 1)
            dve.wait_ge(once, 16)
            dve.tensor_scalar(D[:], S[:], base[:], CAP, ALU.subtract, ALU.min).then_inc(once, 1)
            def first_sum(n):
                dve.wait_ge(r_exp, n + 1)
                dve.tensor_scalar(J[:], Wt[:], one[:], None, ALU.min, ALU.add, accum_out=part[:]).then_inc(parted, 1)

            def next_sum(n):
                dve.wait_ge(summed, n + 1)
                dve.tensor_scalar(J[:], Wt[:], total[:, 0:1], None, ALU.min, ALU.add, accum_out=part[:]).then_inc(parted, 1)

            def renew(n):
                dve.wait_ge(ln_made, n)
                dve.scalar_tensor_tensor(T[:], lnc[:], log_lift, base[:], ALU.subtract, ALU.add).then_inc(renewed, 1)
                dve.wait_ge(renewed, 3 * n - 2)
                dve.tensor_tensor(base[:], T[:], smax[:], ALU.min).then_inc(renewed, 1)
                dve.wait_ge(renewed, 3 * n - 1)
                dve.tensor_scalar(D[:], S[:], base[:], CAP, ALU.subtract, ALU.min).then_inc(renewed, 1)

            dve.wait_ge(loaded, 16 * 4)
            for t in range(HB):
                scale_shift(0, t)
                if t + 2 < HB:
                    normalise(0, t + 2)
                if t == 0:
                    first_sum(0)
                if t >= 1:
                    low(0, t - 1)
            low(0, HB - 1)
            renew(1)

            def keys():
                dve.tensor_scalar(J[:], S[:], T[:], 0.0, ALU.subtract, ALU.min).then_inc(bit_step, 1)
                dve.wait_ge(bit_step, 1)
                dve.tensor_scalar(V_key[:], J[:], -1.0, SMALLEST, ALU.mult, ALU.min).then_inc(bit_step, 1)
                dve.memset(prefix[:], 0.0).then_inc(bit_step, 1)
                dve.wait_ge(bit_step, 3)

            def compare(n):
                dve.tensor_tensor(cand[:], prefix[:].bitcast(I32).to_broadcast([P, 4]), bits[:, n], ALU.bitwise_or).then_inc(bit_step, 1)
                dve.wait_ge(bit_step, 3 * n + 4)
                for j in range(1, 4):
                    ins = dve.tensor_scalar(below[:, j - 1], V_key[:], cand[:, j:j + 1].bitcast(F32), None, ALU.is_lt, ALU.add, accum_out=part4[:, j:j + 1])
                ins.then_inc(compared, 1)

            def keep(n):
                dve.wait_ge(counted, n + 1)
                dve.scalar_tensor_tensor(kept[:], total[:, 0:4], kk, cand[:].bitcast(F32), ALU.is_lt, ALU.mult).then_inc(bit_step, 1)
                dve.wait_ge(bit_step, 3 * n + 5)
                dve.tensor_reduce(prefix[:], kept[:], AX_X, ALU.max).then_inc(bit_step, 1)
                dve.wait_ge(bit_step, 3 * n + 6)

            def rank():
                kth = prefix[:]
                dve.tensor_scalar(LT[:], V_key[:], kth, None, ALU.is_lt, ALU.add, accum_out=part[:]).then_inc(picked, 1)
                dve.tensor_scalar(EQ[:], V_key[:], kth, None, ALU.is_equal).then_inc(picked, 1)
                dve.wait_ge(picked, 2)
                dve.tensor_tensor_scan(J[:], EQ[:], Z[:], 0.0, ALU.add, ALU.add).then_inc(picked, 1)
                dve.wait_ge(turned, 4)
                dve.tensor_tensor(need[:], kk, counts[:, 0:1], ALU.subtract).then_inc(picked, 1)
                dve.wait_ge(picked, 4)
                dve.tensor_tensor(need[:], need[:], counts[:, 1:2], ALU.subtract).then_inc(picked, 1)
                dve.wait_ge(picked, 5)
                dve.scalar_tensor_tensor(D[:], J[:], need[:], EQ[:], ALU.is_le, ALU.mult).then_inc(picked, 1)
                dve.wait_ge(picked, 6)
                dve.tensor_tensor(LT[:], LT[:], D[:], ALU.add).then_inc(picked, 1)
                dve.wait_ge(picked, 7)
                dve.tensor_tensor_scan(J[:], LT[:], Z[:], 0.0, ALU.add, ALU.add).then_inc(picked, 1)
                dve.wait_ge(picked, 8)
                dve.wait_ge(turned, 5)
                dve.scalar_tensor_tensor(D[:], J[:], counts[:, 2:3], LT[:], ALU.add, ALU.mult).then_inc(picked, 1)

            def name_tokens():
                every = lambda ap: ap[:].rearrange("p r t -> p (r t)")
                dve.wait_ge(turned, 6)
                dve.tensor_scalar(every(late), ranks_ps, float(P), None, ALU.is_gt).then_inc(picked, 1)
                dve.wait_ge(picked, 10)
                dve.scalar_tensor_tensor(every(posT), every(late), -float(P), ranks_ps, ALU.mult, ALU.add).then_inc(picked, 1)
                tokens = token[:].rearrange("p (o t) -> p o t", o=1).to_broadcast([P, R, TB])
                dve.tensor_tensor(late[:], late[:], tokens, ALU.mult).then_inc(picked, 1)
                dve.wait_ge(picked, 12)
                dve.tensor_tensor(tk[:, :, :, 0], tokens, late[:], ALU.subtract).then_inc(picked, 1)
                dve.tensor_scalar(tk[:, :, :, 1], late[:], 0.0, None, ALU.add).then_inc(picked, 1)
                dve.wait_ge(picked, 14)
                for r in range(R):
                    if r >= 2:
                        dve.wait_ge(found, r - 1)
                    dve.tensor_tensor(hot[:, r % 2], cols(posT[:, r], P), ranks[:].rearrange("p (o n) -> p o n", o=1).to_broadcast([P, TB, P]),
                                      ALU.is_equal).then_inc(hot_made, 1)
                dve.wait_ge(found, R)
                for b in range(B):
                    dve.tensor_scalar(IDX[:, 3 * b:3 * b + 1], found_ps[:, 2 * b:2 * b + 1], float(N * b), None, ALU.add)
                    ins = dve.tensor_scalar(IDX[:, 3 * b + 1:3 * b + 3], found_ps[:, 2 * (B + b):2 * (B + b) + 2],
                                            float(N * b), None, ALU.add)
                ins.then_inc(idx_made, 1)

            def batch_row(b, stage, last=False):
                normalise(b, HB)
                normalise(b, HB + 1)
                if stage == "bisect":
                    keys()
                if stage == "name":
                    rank()
                for t in range(HB, TB):
                    scale_shift(b, t)
                    if t + 2 < TB:
                        normalise(b, t + 2)
                    if t > HB:
                        low(b, t - 1)
                low(b, TB - 1)
                if stage == "name":
                    name_tokens()
                for t in range(TB + 3):
                    v = t - 3
                    if stage == "descend" and t < TB:
                        if t % (TB // 2) == 0:
                            first_sum(b * 2 + (t // (TB // 2) + 1))
                        next_sum(update_slot(b, t, 1))
                    if stage == "bisect" and t < TB:
                        compare(2 * t)
                    if t < TB:
                        i = b * TB + t
                        dve.wait_ge(scored, i + 1)
                        own = mx[:, t % 2]
                        for j in range(2):
                            dve.tensor_reduce(own[:, 4 * j:4 * j + 4], banks_s[j][:].rearrange("p (h m) -> p h m", m=P),
                                              AX_X, ALU.max).then_inc(max_made, 1)
                        dve.tensor_reduce(mxe[:], bank_e[:].rearrange("p (h m) -> p h m", m=W), AX_X, ALU.max).then_inc(max_made, 1)
                        dve.wait_ge(max_made, 3 * i + 3)
                        mask = edge[:, 0:1] if t == 0 else edge[:, 1:2] if t == TB - 1 else 0.0
                        dve.scalar_tensor_tensor(own, mxe[:], mask, own, ALU.add, ALU.max).then_inc(max_joined, 1)
                        dve.wait_ge(max_joined, i + 1)
                        if t >= 2:
                            dve.wait_ge(probs_made, 3 * (i - 1))
                        for j in range(2):
                            dve.tensor_tensor(E[:, t % 2, 4 * j:4 * j + 4, 0:P], banks_s[j][:].rearrange("p (h m) -> p h m", m=P),
                                              cols(mx[:, t % 2, 4 * j:4 * j + 4], P), ALU.subtract)
                        dve.scalar_tensor_tensor(E[:, t % 2, :, P:3 * W], bank_e[:].rearrange("p (h m) -> p h m", m=W), mask,
                                                 cols(own, W), ALU.add, ALU.subtract).then_inc(shifted, 1)
                    if t == TB + 1 and last:
                        dve.tensor_scalar(hA[:], k["xmv"][:, :, 1], EPS, TINY, ALU.add, ALU.mult).then_inc(scale_step, 1)
                        dve.wait_ge(scale_step, 1)
                        dve.tensor_tensor(hA[:], hA[:], k["xmv"][:, :, 1], ALU.max).then_inc(scale_step, 1)
                    ahead = t == TB + 1 and not last
                    if ahead:
                        scale_shift(b + 1, 0)
                        normalise(b + 1, 2)
                        scale_shift(b + 1, 1)
                        normalise(b + 1, 3)
                        low(b + 1, 0)
                    if v >= 0:
                        i = b * TB + v
                        xt = flat(XR[:, bass.ds(i, 1)])
                        dve.wait_ge(projected, i + 1)
                        dve.scalar_tensor_tensor(xt, bank_o[:, 0:C], tg[:, 1:2], xt, ALU.mult, ALU.add).then_inc(z_made, 1)
                    if t == TB and not last:
                        normalise(b + 1, 0)
                        normalise(b + 1, 1)
                    if ahead:
                        scale_shift(b + 1, 2)
                        low(b + 1, 1)
                        scale_shift(b + 1, 3)
                        low(b + 1, 2)
                        low(b + 1, 3)
                    if stage == "descend" and t < TB:
                        next_sum(update_slot(b, t, 2))
                    if stage == "bisect" and t < TB:
                        keep(2 * t)
                        compare(2 * t + 1)
                    if t < TB:
                        i = b * TB + t
                        dve.wait_ge(exp_made, i + 1)
                        dve.tensor_reduce(sm[:, t % 2], E[:, t % 2], AX_X, ALU.add).then_inc(sum_made, 1)
                        dve.wait_ge(sum_made, i + 1)
                        dve.reciprocal(rc[:, t % 2], sm[:, t % 2]).then_inc(recip_made, 1)
                    if stage == "descend" and t < TB:
                        if t % HB < HB - 1:
                            next_sum(update_slot(b, t, 3))
                        else:
                            renew(b * 2 + (t // HB + 2))
                    if stage == "bisect" and t < TB:
                        keep(2 * t + 1)
                    if stage == "name" and 3 <= t < 3 + G // 2:
                        dve.wait_ge(x_gathered, 32 * (t - 2))
                        for g in (2 * t - 6, 2 * t - 5):
                            dve.bn_stats(bst[:, g % 2], X[:, g]).then_inc(x_stats, 1)
                        for g in (2 * t - 6, 2 * t - 5):
                            dve.wait_ge(x_stats, 4 * (t - 3) + 2)
                            dve.bn_aggr(k["xmv"][:, g], bst[:, g % 2]).then_inc(x_stats, 1)
                        dve.wait_ge(x_stats, 4 * (t - 2))

            with dve.Fori(0, ROUTED) as b:
                batch_row(b, "descend")
            batch_row(ROUTED, "bisect")
            batch_row(ROUTED + 1, "name", last=True)
            dve.wait_ge(lns, 2)
            dve.wait_ge(scale_step, 2)
            dve.tensor_scalar(hC[:], hC[:], float(2 ** LIFT), None, ALU.mult).then_inc(scale_step, 1)
            dve.wait_ge(scale_step, 3)
            rsqrt_step(dve, k["scl"], hC, hA, hB, scale_step, 3)

        @block.tensor
        def _(pe):
            pe.wait_ge(once, 10)
            pe.wait_ge(r_loaded, 16 * 4)
            pe.matmul(ps[2][:, 0:SEG], SM[:].rearrange("p n h -> p (n h)"), fold[:], start=True, stop=True).then_inc(turned, 1)
            pe.wait_ge(once, 11)
            pe.matmul(ps[4][0:1, 0:P], own_max[:], ident[:], start=True, stop=True).then_inc(turned, 1)
            pe.wait_ge(once, 13)
            pe.matmul(ps[4][:, P:P + 1], maxes[:, P:2 * P], one[0:1, :], start=True, stop=True).then_inc(turned, 1)

            def update(n):
                pe.wait_ge(parted, n + 2)
                pe.matmul(total[:, 0:1], inv_k, part[:], start=True, stop=True).then_inc(summed, 1)

            def count(n):
                pe.wait_ge(compared, n + 1)
                pe.matmul(total[:, 0:4], same, part4[:], start=True, stop=True).then_inc(counted, 1)

            def turn(b, t):
                i = b * TB + t
                pe.wait_ge(y_made, i + 1)
                if t >= 2:
                    pe.wait_ge(yT_made, 2 * (i - 1))
                for c in range(CC):
                    ins = pe.transpose(y_bank(t)[:, P * c:P * (c + 1)], y[:, t % 2, P * c:P * (c + 1)], ident[:])
                ins.then_inc(y_turned, 1)

            for t in range(HB):
                turn(0, t)
                if t == 1:
                    update(-1)
            pe.wait_ge(wlo_made, 1)
            pe.wait_ge(w_loaded, 16)

            def batch_row(b, stage, last=False):
                def slot(t, n):
                    if n == 2 and t >= 3:
                        pe.wait_ge(z_made, b * TB + t - 2)
                    if stage == "descend":
                        update(update_slot(b, t, n))
                    if stage == "bisect" and n >= 1:
                        count(2 * t + n - 1)

                def project(n):
                    if n >= 4:
                        pe.wait_ge(qkv_evac, NEV * b + evacs(max(n - 4, GH - 1) if n >= GH else n - 4))
                    if stage == "name" and n == GH + 1:
                        pe.wait_ge(idx_made, 1)
                    passes = [(a, w, c) for a, w in ((0, Whi), (0, Wlo), (1, Whi)) for c in range(CC)]
                    half, kind, m = GROUPS[n]
                    for q, (a, w, c) in enumerate(passes):
                        if kind == "v":
                            lhs, rhs = ysplit[:, half, a, c, P * m:P * (m + 1)], w[:, c, 2 * IN:3 * IN]
                        else:
                            f = IN * (kind == "k") + P * m
                            lhs, rhs = w[:, c, f:f + P], ysplit[:, half, a, c]
                        ins = pe.matmul(group_bank(n)[:], lhs, rhs, start=(q == 0), stop=(q == len(passes) - 1))
                    ins.then_inc(qkv_mult, 1)
                    if stage == "name" and n == 2:
                        pe.wait_ge(picked, 3)
                        pe.matmul(counts[:, 0:1], same, part[:], start=True, stop=True)
                        pe.matmul(counts[:, 1:2], prior, J[:, SEG - 1:SEG], start=True, stop=True).then_inc(turned, 1)
                    if stage == "name" and n == 4:
                        pe.wait_ge(picked, 8)
                        pe.matmul(counts[:, 2:3], prior, J[:, SEG - 1:SEG], start=True, stop=True).then_inc(turned, 1)
                    if stage == "name" and n == 5:
                        pe.wait_ge(picked, 9)
                        for half in range(2):
                            ins = pe.matmul(ranks_ps[SEG * half:SEG * (half + 1)], D[:], ident[:, half::2], start=True, stop=True)
                        ins.then_inc(turned, 1)
                    if stage == "name" and n in NAMED:
                        for r in NAMED[n]:
                            pe.wait_ge(hot_made, r + 1)
                            for t in range(TB):
                                ins = pe.matmul(found_ps[:, 2 * r:2 * r + 2], hot[:, r % 2, t], tk[:, r, t], start=(t == 0), stop=(t == TB - 1))
                            ins.then_inc(found, 1)

                pe.wait_ge(ylo_made, b * TB + HB)
                for n in range(GH):
                    project(n)
                    if n % 2 == 1 and n < 8:
                        turn(b, HB + n // 2)
                pe.wait_ge(ylo_made, b * TB + TB)
                pe.wait_ge(qkv_evac, NEV * b + evacs(GH - 1))
                for t in range(TB + 3):
                    u, v = t - 2, t - 3
                    if t < TB:
                        if t >= 1:
                            pe.wait_ge(shifted, b * TB + t)
                        for p in range(HP):
                            pe.matmul(banks_s[p // 2][:, 2 * P * (p % 2):2 * P * (p % 2 + 1)], QT[:, p, P * t:P * (t + 1)],
                                      KD[:, p, :, P * t:P * (t + 1)], start=True, stop=True)
                        slot(t, 0)
                        before, after = max(2 * t - 1, 0), min(2 * t + 2, 2 * TB - 1)
                        for p in range(HP):
                            for j, w in enumerate((before, after)):
                                ins = pe.matmul(bank_e[W * j:W * (j + 1), 2 * W * p:2 * W * (p + 1)],
                                                QT[:, p, P * t + W * j:P * t + W * (j + 1)],
                                                KD[:, p, :, W * w:W * (w + 1)], start=True, stop=True)
                        ins.then_inc(scored, 1)
                    if t < 2:
                        for n in fills(t):
                            project(n)
                    if 0 <= u < TB:
                        i = b * TB + u
                        if u == 0:
                            pe.wait_ge(qkv_evac, NEV * (b + 1))
                        pe.wait_ge(probs_made, 3 * (i + 1))
                        for g in range(4):
                            n = 4 * u + g
                            if n >= 3:
                                pe.wait_ge(pT_made, 4 * TB * b + n - 2)
                            for q in range(4):
                                hh, kc = 2 * g + q // 2, q % 2
                                ins = pe.transpose(banks_p[n % 3][:, P * q:P * (q + 1)],
                                                   probs[:, u % 2, hh, P * kc:P * (kc + 1)], ident[:])
                            ins.then_inc(p_turned, 1)
                    if t < TB:
                        slot(t, 1)
                    ahead = t == TB + 1 and not last
                    if ahead:
                        turn(b + 1, 0)
                        turn(b + 1, 1)
                    if v >= 0:
                        i = b * TB + v
                        pe.wait_ge(oT_made, i + 1)
                        if v >= 1:
                            pe.wait_ge(z_made, i)
                        if stage == "descend" and t in (HB, TB):
                            pe.wait_ge(ln_made, b * 2 + (t // HB + 1))
                        if stage == "bisect" and t == TB:
                            pe.wait_ge(bit_step, 3 * TB * 2 + 3)
                        for p in range(HP):
                            ins = pe.matmul(bank_o[:, 0:C], OT[:, P * p:P * (p + 1)], WoT[:, p], start=(p == 0), stop=(p == HP - 1))
                        ins.then_inc(projected, 1)
                    if ahead:
                        turn(b + 1, 2)
                    if 0 <= u < TB:
                        i = b * TB + u
                        pe.wait_ge(pT_made, 4 * (i + 1))
                        pe.wait_ge(vx_made, NVX * b + min(2 * u + 2, NVX))
                        for p in range(HP):
                            for kc, val in enumerate((V, VX)):
                                for j in range(2):
                                    hh = 2 * p + j
                                    ins = pe.matmul(bank_v[DH * j:DH * (j + 1), P * p:P * (p + 1)],
                                                    val[:, u, DH * hh:DH * (hh + 1)], pT[:, hh, kc],
                                                    start=(kc == 0), stop=(kc == 1))
                        ins.then_inc(pv_done, 1)
                    if ahead:
                        turn(b + 1, 3)
                    if t < TB:
                        slot(t, 2)

            with pe.Fori(0, ROUTED) as b:
                batch_row(b, "descend")
            batch_row(ROUTED, "bisect")
            batch_row(ROUTED + 1, "name", last=True)


def chosen_attention(nc, k, ps, d):
    ident, tg, IDX, X, mv, scl = k["ident"], k["tg"], k["IDX"], k["X"], k["xmv"], k["scl"]
    Wq, Wkv, Wo = k["hWq"], k["hWkv"], k["hWo"]
    with ExitStack() as stack:
        s = Space(nc, stack, "chosen")
        s.sb("weights", [P, 3 * CC * IN + HP * C])
        Z, out_rows = s.sb("Z", [P, B, C]), s.sb("out_rows", [P, B, C])
        gam = s.sb("gam", [P, CC])
        xn, xT = s.sb("xn", [P, 3, C]), s.sb("xT", [P, CC, 3 * P])
        QT, KD, V = s.sb("QT", [P, HP, P]), s.sb("KD", [P, HP, 2, NKV]), s.sb("V", [P, 2, IN])
        NK, nk, NV = s.sb("NK", [P, HP * H]), s.sb("nk", [P, HP]), s.sb("NV", [H, IN])
        E, e0 = s.sb("E", [P, H, NKV]), s.sb("e0", [P, H])
        mx, sm, rc = s.sb("mx", [P, H]), s.sb("sm", [P, H]), s.sb("rc", [P, H])
        pT, p0T, OT = s.sb("pT", [P, H, 2, P]), s.sb("p0T", [H, P]), s.sb("OT", [P, HP * P])
        null_ps, p0_ps = ps[7][:, 0:H], ps[7][0:H, P:2 * P]
        bank_v, bank_o = ps[0], ps[1]

        def v_bank(n, j):
            return ps[2 + j] if type(n) is int and n == 0 else ps[5 + j]

        def p_bank(g):
            return ps[(6, 4, 5, 6)[g]]

        loaded, null_loaded, z_gathered, scattered = (s.sem(n) for n in (
            "h_loaded", "null_loaded", "z_gathered", "scattered"))
        pool_once = s.sem("pool_once")
        centred, xn_made, x_turned, xT_made = s.sem("centred"), s.sem("xn_made"), s.sem("x_turned"), s.sem("xT_made")
        q_mult, k_mult, v_mult = s.sem("q_mult"), s.sem("k_mult"), s.sem("v_mult")
        q_made, kd_made, v_made = s.sem("q_made"), s.sem("kd_made"), s.sem("v_made")
        scored, max_made, shifted, exp_made = s.sem("scored"), s.sem("max_made"), s.sem("shifted"), s.sem("exp_made")
        sum_made, probs_made = s.sem("sum_made"), s.sem("probs_made")
        p_turned, pT_made, pv_done, oT_made = s.sem("p_turned"), s.sem("pT_made"), s.sem("pv_done"), s.sem("oT_made")
        projected, rows_made, null_placed = s.sem("projected"), s.sem("rows_made"), s.sem("null_placed")
        block = stack.enter_context(nc.Block())

        @block.sync
        def _(sp):
            sp.dma_start(gam[:], d["gamma"]).then_inc(loaded, 16)
            sp.dma_start(nk[:], d["null_k"]).then_inc(loaded, 16)
            sp.wait_ge(pool_once, 2)
            for h in range(H):
                sp.dma_start(NV[h:h + 1, DH * h:DH * (h + 1)], d["null_v"][h:h + 1, :]).then_inc(null_loaded, 16)

        @block.gpsimd
        def _(pool):
            def rows_of(g):
                return bass.IndirectOffsetOnAxis(ap=IDX[:, g:g + 1].bitcast(U32), axis=0)

            def normalise(b):
                at = slice(3 * b, 3 * b + 3)
                pool.wait_ge(x_turned, 2 * b)
                pool.tensor_tensor(xn[:], X[:, at], mv[:, at, 0:1].to_broadcast([P, 3, C]), ALU.subtract).then_inc(centred, 1)
                pool.wait_ge(centred, b)
                pool.tensor_tensor(xn[:], xn[:], cols(scl[:, at], C), ALU.mult).then_inc(xn_made, 1)
                pool.wait_ge(xn_made, b + 1)

            pool.memset(NK[:], 0.0).then_inc(pool_once, 1)
            pool.memset(NV[:], 0.0).then_inc(pool_once, 1)
            pool.memset(KD[:], 0.0).then_inc(pool_once, 1)
            pool.wait_ge(pool_once, 3)
            normalise(1)
            for b in range(B):
                pool.indirect_dma_start(Z[:, b], None, d["z_rows"], rows_of(3 * b)).then_inc(z_gathered, 16)
            pool.wait_ge(z_gathered, 16 * B)
            for b in range(B):
                if b + 2 < B:
                    normalise(b + 2)
                pool.wait_ge(rows_made, b + 2)
                pool.indirect_dma_start(d["out"], rows_of(3 * b), out_rows[:, b], None).then_inc(scattered, 16)
                pool.wait_ge(scattered, 16 * (b + 1))

        @block.scalar
        def _(act):
            act.wait_ge(pool_once, 3)

            def queries_keys(n):
                act.wait_ge(q_mult, n + 1)
                act.activation(QT[:].rearrange("p k n -> p (k n)"), ps[6][:], ACT.Copy, scale=SCALE).then_inc(q_made, 1)
                for m in range(HP):
                    if m % 2 == 0:
                        act.wait_ge(k_mult, 2 * n + m // 2 + 1)
                    for j in range(2):
                        rows = slice(DH * j, DH * (j + 1))
                        act.activation(KD[rows, m, j], ps[4 + m // 2][rows, NKV * (m % 2):NKV * (m % 2 + 1)],
                                       ACT.Copy).then_inc(kd_made, 1)

            def batch_row(b, last):
                for half in range(2):
                    if half == 0:
                        act.wait_ge(max_made, 5 * b + 5)
                    for h in range(4 * half, 4 * half + 4):
                        ins = act.activation(E[:, h], ps[h // 2][:, NKV * (h % 2):NKV * (h % 2 + 1)], ACT.Exp,
                                             bias=mx[:, h:h + 1], accum_out=sm[:, h:h + 1])
                    ins.then_inc(exp_made, 1)
                    if half == 0:
                        act.wait_ge(shifted, b + 1)
                        act.activation(e0[:], e0[:], ACT.Exp).then_inc(exp_made, 1)
                if not last:
                    queries_keys(b + 1)
                for g in range(4):
                    act.wait_ge(p_turned, 5 * b + 1 + g)
                    act.activation(pT[:, 2 * g:2 * g + 2].rearrange("p h k n -> p (h k n)"), p_bank(g)[:], ACT.Copy).then_inc(pT_made, 1)
                act.wait_ge(p_turned, 5 * b + 5)
                act.activation(p0T[:], p0_ps, ACT.Copy).then_inc(pT_made, 1)

            queries_keys(0)
            with act.Fori(0, B - 1) as b:
                batch_row(b, False)
            batch_row(B - 1, True)

        @block.vector
        def _(dve):
            dve.memset(mx[:], 0.0).then_inc(rows_made, 1)
            for j in range(3):
                ins = dve.tensor_scalar(xn[:, j], X[:, j], mv[:, j, 0:1], scl[:, j:j + 1], ALU.subtract, ALU.mult)
            ins.then_inc(xn_made, 1)
            dve.wait_ge(loaded, 16 * 2)
            dve.wait_ge(pool_once, 1)
            for j in range(2):
                dve.tensor_copy(NK[DH * j:DH * (j + 1), j::H + 2], nk[DH * j:DH * (j + 1), :]).then_inc(null_placed, 1)

            def scale_turned(n):
                for c in range(CC):
                    dve.wait_ge(x_turned, 2 * n + c + 1)
                    dve.tensor_scalar(xT[:, c], ps[4 + c][:, 0:3 * P], gam[:, c:c + 1], None, ALU.mult).then_inc(xT_made, 1)

            def values(n):
                for j in range(2):
                    dve.wait_ge(v_mult, 2 * n + j + 1)
                    dve.tensor_copy(V[:, j], v_bank(n, j)[:]).then_inc(v_made, 1)

            def batch_row(b, last):
                if not last:
                    scale_turned(b + 1)
                for p in range(HP):
                    dve.wait_ge(scored, 4 * b + p + 1)
                    dve.tensor_reduce(mx[:, 2 * p:2 * p + 2], ps[p][:].rearrange("p (h m) -> p h m", m=NKV), AX_X, ALU.max,
                                      negate=True).then_inc(max_made, 1)
                dve.wait_ge(max_made, 5 * b + 4)
                dve.scalar_tensor_tensor(mx[:], null_ps, -1.0, mx[:], ALU.mult, ALU.min).then_inc(max_made, 1)
                dve.wait_ge(max_made, 5 * b + 5)
                dve.tensor_tensor(e0[:], null_ps, mx[:], ALU.add).then_inc(shifted, 1)
                for half in range(2):
                    at = slice(4 * half, 4 * half + 4)
                    dve.wait_ge(exp_made, 3 * b + 2 + half)
                    dve.tensor_tensor(sm[:, at], sm[:, at], e0[:, at], ALU.add).then_inc(sum_made, 1)
                    dve.wait_ge(sum_made, 4 * b + 2 * half + 1)
                    dve.reciprocal(rc[:, at], sm[:, at]).then_inc(sum_made, 1)
                    dve.wait_ge(sum_made, 4 * b + 2 * half + 2)
                    for g in (2 * half, 2 * half + 1):
                        two = slice(2 * g, 2 * g + 2)
                        dve.tensor_tensor(E[:, two], E[:, two], cols(rc[:, two], NKV), ALU.mult).then_inc(probs_made, 1)
                dve.tensor_tensor(e0[:], e0[:], rc[:], ALU.mult).then_inc(probs_made, 1)
                dve.wait_ge(pv_done, b + 1)
                dve.tensor_copy(OT[:], bank_v[:]).then_inc(oT_made, 1)
                if not last:
                    values(b + 1)
                dve.wait_ge(projected, b + 1)
                dve.wait_ge(z_gathered, 16 * B)
                rows = slice(b, b + 1) if last else bass.ds(b, 1)
                dve.scalar_tensor_tensor(flat(out_rows[:, rows]), bank_o[:, 0:C], tg[:, 1:2],
                                         flat(Z[:, rows]), ALU.mult, ALU.add).then_inc(rows_made, 1)

            scale_turned(0)
            values(0)
            with dve.Fori(0, B - 1) as b:
                batch_row(b, False)
            batch_row(B - 1, True)

        @block.tensor
        def _(pe):
            def turn(n):
                pe.wait_ge(xn_made, n + 1)
                for c in range(CC):
                    for j in range(3):
                        ins = pe.transpose(ps[4 + c][:, P * j:P * (j + 1)], xn[:, j, P * c:P * (c + 1)], ident[:])
                    ins.then_inc(x_turned, 1)

            def queries_keys(n):
                pe.wait_ge(xT_made, 2 * n + 2)
                for m in range(HP):
                    for c in range(CC):
                        ins = pe.matmul(ps[6][:, P * m:P * (m + 1)], Wq[:, c, P * m:P * (m + 1)], xT[:, c, 0:P],
                                        start=(c == 0), stop=(c == CC - 1))
                ins.then_inc(q_mult, 1)
                for m in range(HP):
                    for c in range(CC):
                        ins = pe.matmul(ps[4 + m // 2][:, NKV * (m % 2):NKV * (m % 2 + 1)], Wkv[:, c, P * m:P * (m + 1)],
                                        xT[:, c, P:3 * P], start=(c == 0), stop=(c == CC - 1))
                    if m % 2:
                        ins.then_inc(k_mult, 1)

            def values(n):
                for j in range(2):
                    for c in range(CC):
                        ins = pe.matmul(v_bank(n, j)[:], xT[:, c, P * (j + 1):P * (j + 2)], Wkv[:, c, IN:2 * IN],
                                        start=(c == 0), stop=(c == CC - 1))
                    ins.then_inc(v_mult, 1)

            def batch_row(b, last):
                if not last:
                    pe.wait_ge(v_made, 2 * b + 2)
                    turn(b + 1)
                pe.wait_ge(q_made, b + 1)
                pe.wait_ge(kd_made, 8 * b + 8)
                for p in range(HP):
                    pe.matmul(null_ps, QT[:, p], NK[:, H * p:H * (p + 1)], start=(p == 0), stop=(p == HP - 1))
                for p in range(HP):
                    if p == 1:
                        pe.wait_ge(rows_made, b + 1)
                    pe.matmul(ps[p][:], QT[:, p], KD[:, p].rearrange("p h n -> p (h n)"), start=True, stop=True).then_inc(scored, 1)
                if not last:
                    queries_keys(b + 1)
                for g in range(4):
                    pe.wait_ge(probs_made, 5 * b + 1 + g)
                    if g < 3 and not last:
                        if g > 0:
                            pe.wait_ge(kd_made, 8 * b + 8 + 4 * g)
                        else:
                            pe.wait_ge(q_made, b + 2)
                    if g == 0 and last:
                        pe.wait_ge(v_made, 2 * b + 2)
                    if g == 3:
                        pe.wait_ge(pT_made, 5 * b + 1)
                    for q in range(4):
                        hh, kc = 2 * g + q // 2, q % 2
                        ins = pe.transpose(p_bank(g)[:, P * q:P * (q + 1)], E[:, hh, P * kc:P * (kc + 1)], ident[:])
                    ins.then_inc(p_turned, 1)
                pe.wait_ge(probs_made, 5 * b + 5)
                pe.transpose(p0_ps, e0[:], ident[:]).then_inc(p_turned, 1)
                pe.wait_ge(pT_made, 5 * b + 5)
                for p in range(HP):
                    for kc in range(3):
                        for j in range(2):
                            hh = 2 * p + j
                            dst = bank_v[DH * j:DH * (j + 1), P * p:P * (p + 1)]
                            if kc < 2:
                                ins = pe.matmul(dst, V[:, kc, DH * hh:DH * (hh + 1)], pT[:, hh, kc], start=(kc == 0), stop=False)
                            else:
                                ins = pe.matmul(dst, NV[:, DH * hh:DH * (hh + 1)], p0T[:], start=False, stop=True)
                ins.then_inc(pv_done, 1)
                if not last:
                    values(b + 1)
                pe.wait_ge(oT_made, b + 1)
                for p in range(HP):
                    ins = pe.matmul(bank_o[:, 0:C], OT[:, P * p:P * (p + 1)], Wo[:, p], start=(p == 0), stop=(p == HP - 1))
                ins.then_inc(projected, 1)

            turn(0)
            queries_keys(0)
            values(0)
            pe.wait_ge(q_made, 1)
            pe.wait_ge(kd_made, 8)
            pe.wait_ge(null_loaded, 16 * H)
            pe.wait_ge(null_placed, 2)
            with pe.Fori(0, B - 1) as b:
                batch_row(b, False)
            batch_row(B - 1, True)


def build_program(nc, d):
    with ExitStack() as stack:
        s = Space(nc, stack, "all")
        k = {"XR": s.sb("XR", [P, NT, C]), "ident": s.sb("ident", [P, P]), "MV": s.sb("MV", [P, NT, 2]),
             "RS": s.sb("RS", [P, NT]), "tg": s.sb("tg", [P, 2]), "sraw": s.sb("sraw", [P, 2, NT]),
             "IDX": s.sb("IDX", [P, 3 * B], I32)}
        ps = [stack.enter_context(nc.psum_tensor(f"ps{i}", [P, 512], F32)) for i in range(8)]
        for name in ("x1_rows", "z_rows"):
            d[name] = nc.dram_tensor(name, (B * N, C), F32, kind="Internal").ap()
        with ExitStack() as early:
            k["Wst"] = Space(nc, early, "window").sb("Wst", [P, CC, 3 * IN])
        cross_attention(nc, k, ps, d)
        k["X"], k["xmv"], k["scl"] = s.sb("X", [P, G, C]), s.sb("xmv", [P, G, 2]), s.sb("scl", [P, G])
        with ExitStack() as early:
            w = Space(nc, early, "chosen")
            k["hWq"], k["hWkv"], k["hWo"] = w.sb("Wq", [P, CC, IN]), w.sb("Wkv", [P, CC, 2 * IN]), w.sb("Wo", [P, HP, C])
        windowed_attention(nc, k, ps, d)
        chosen_attention(nc, k, ps, d)


def kernel(x, ctx_768, g_xattn, g_ffn, L0_xattn_Wq, L0_xattn_Wk, L0_xattn_Wv, L0_xattn_Wo, L0_xattn_bo,
           L0_ffn_ln_w, L0_ffn_ln_b, L0_ffn_Wqkv, L0_ffn_Wout_l, L0_ffn_rt_q, L0_ffn_rt_kv, L0_ffn_gamma,
           L0_ffn_Wq, L0_ffn_Wkv, L0_ffn_Wout_h, L0_ffn_null_kv, L0_ffn_null_q):
    import numpy as np
    import concourse.bacc as bacc
    from concourse.bass_utils import run_bass_kernel_spmd

    def lay(a):
        return np.ascontiguousarray(a)

    def by_row(a):
        return lay(np.reshape(a, (CC, P)).T)

    ks = [NQ] * B + [NKV] * B

    def lift(q):
        return round(3 * TB // 2 * (2 * log(q * FETCH, 2) - log(N, 2)) / 2)

    same = (np.arange(P)[:, None] // (P // R) == np.arange(P)[None, :] // (P // R)).astype(np.float64)
    arrays = {
        "x": lay(np.reshape(x, (B * N, C))),
        "ctxT": lay(np.reshape(ctx_768, (B * M, XC)).T),
        "g_xattn": lay(g_xattn), "g_ffn": lay(g_ffn),
        "xWqT": lay(np.transpose(L0_xattn_Wq)), "xWk": lay(L0_xattn_Wk), "xWv": lay(L0_xattn_Wv),
        "xWo": lay(L0_xattn_Wo), "xbo": lay(L0_xattn_bo),
        "ln_w": by_row(L0_ffn_ln_w), "ln_b": by_row(L0_ffn_ln_b),
        "WqkvT": lay(np.transpose(L0_ffn_Wqkv)), "WoutlT": lay(np.transpose(L0_ffn_Wout_l)),
        "rt_q": lay(L0_ffn_rt_q), "rt_kv": lay(L0_ffn_rt_kv), "gamma": by_row(L0_ffn_gamma),
        "hWqT": lay(np.transpose(L0_ffn_Wq)),
        "hWkvT": lay(np.reshape(L0_ffn_Wkv, (H, 2, DH, C)).transpose(3, 1, 0, 2).reshape(C, 2 * IN)),
        "hWoutT": lay(np.transpose(L0_ffn_Wout_h)),
        "null_k": lay(np.reshape(L0_ffn_null_kv[0], (HP, P)).T), "null_v": lay(L0_ffn_null_kv[1]), "null_q": lay(L0_ffn_null_q),
        "rows128": np.array([[log(N) - log(q * FETCH), q, 2.0 ** lift(q), lift(q) * log(2.0)] for q in ks for _ in range(P // R)], np.float32),
        "bits128": np.array([[[0, 1 << 30, 1 << 30, 1 << 30]] + [[j << i for j in range(4)] for i in range(28, -1, -2)]] * P, np.int32),
        "blocks": np.stack([same / (np.repeat(ks, P // R)[None, :] * FETCH), same,
                            same * (np.arange(P)[:, None] < np.arange(P)[None, :])], 1).astype(np.float32),
        "fold": np.array([[float(p % SEG == i) for i in range(SEG)] for p in range(P)], np.float32),
        "edge": np.array([[NEG * (p < W), NEG * (p >= W)] for p in range(P)], np.float32),
    }
    nc = bacc.Bacc("TRN2", target_bir_lowering=False, num_devices=1)
    d = {n: nc.dram_tensor(n, a.shape, mybir.dt.from_np(a.dtype), kind="ExternalInput").ap() for n, a in arrays.items()}
    d["out"] = nc.dram_tensor("out", (B * N, C), F32, kind="ExternalOutput").ap()
    build_program(nc, d)
    r = run_bass_kernel_spmd(nc, [arrays], core_ids=[0])
    return r.results[0]["out"].reshape(B, N, C)
```
